# Optimizing a Trainium2 kernel written in Bass

```python
import numpy as np
import jax
import jax.numpy as jnp

def _softmax(x, axis=-1):
    return jax.nn.softmax(x, axis=axis)

def _gelu(x):
    return jax.nn.gelu(x, approximate=True)

def _silu(x):
    return jax.nn.silu(x)

def _sigmoid(x):
    return jax.nn.sigmoid(x)

def _layernorm(x, axis=-1, eps=1e-05):
    m = jnp.mean(x, axis=axis, keepdims=True)
    v = jnp.var(x, axis=axis, keepdims=True)
    return (x - m) / jnp.sqrt(v + eps)

def _scatter_add(tgt, idx, src, axis=0):
    return tgt.at[idx].add(src)

def _segment_sum(src, seg, n):
    return jax.ops.segment_sum(src, seg, n)
kernel_name = 'mk_prb_d2_jaxref_r8_cc28c2'

def setup_inputs(seed: int=0):
    np.random.seed(seed)
    _w = jnp.asarray

    def _L0_attn_setup():
        import jax, jax.numpy as jnp
        import numpy as np
        B_, S, H = (2, 256, 256)
        E = 2 * H
        P = 64
        NH = E // P
        N = 64
        G = 1
        K = 4
        CS = 32
        CONV_DIM = E + 2 * G * N
        PROJ = E + CONV_DIM + NH
        EPS = 1e-06

        def segment_sum(a):
            l = a.shape[-1]
            a_exp = jnp.broadcast_to(a[..., None], (*a.shape, l))
            a_exp = jnp.where(jnp.tril(jnp.ones((l, l), bool), -1), a_exp, 0.0)
            s = jnp.cumsum(a_exp, axis=-2)
            return jnp.where(jnp.tril(jnp.ones((l, l), bool), 0), s, -jnp.inf)
        key = jax.random.key(seed)
        ks = jax.random.split(key, 8)
        s = 0.02
        return {'x': jax.random.normal(ks[0], (B_, S, H), jnp.float32), 'in_proj_w': jax.random.normal(ks[1], (PROJ, H), jnp.float32) * s, 'conv_w': jax.random.normal(ks[2], (CONV_DIM, K), jnp.float32) * s, 'conv_b': jnp.zeros((CONV_DIM,), jnp.float32), 'dt_bias': jax.random.uniform(ks[3], (NH,), jnp.float32, 0.0, 1.0), 'A_log': jnp.log(jax.random.uniform(ks[4], (NH,), jnp.float32, 1.0, 16.0)), 'D': jnp.ones((NH,), jnp.float32), 'norm_w': jnp.ones((E,), jnp.float32), 'out_proj_w': jax.random.normal(ks[5], (H, E), jnp.float32) * s}
    _L0_attn_in = _L0_attn_setup()

    def _L0_ffn_setup():
        import jax, jax.numpy as jnp
        import numpy as np
        B, S, H = (1, 128, 256)
        NH, NKV, D = (32, 8, 64)
        GROUPS = NH // NKV
        E, F, TOPK = (8, 1024, 2)
        EPS = 1e-05

        def rmsnorm(x, w):
            return x * jax.lax.rsqrt(jnp.mean(x * x, axis=-1, keepdims=True) + EPS) * w

        def attention(h, wq, wk, wv, wo):
            b, s, _ = h.shape
            q = (h @ wq).reshape(b, s, NH, D).transpose(0, 2, 1, 3)
            k = (h @ wk).reshape(b, s, NKV, D).transpose(0, 2, 1, 3)
            v = (h @ wv).reshape(b, s, NKV, D).transpose(0, 2, 1, 3)
            k = jnp.repeat(k, GROUPS, axis=1)
            v = jnp.repeat(v, GROUPS, axis=1)
            scores = jnp.einsum('bhqd,bhkd->bhqk', q, k) / jnp.sqrt(jnp.float32(D))
            causal = jnp.tril(jnp.ones((s, s), bool))
            scores = jnp.where(causal, scores, jnp.finfo(scores.dtype).min)
            attn = jax.nn.softmax(scores, axis=-1)
            out = jnp.einsum('bhqk,bhkd->bhqd', attn, v)
            out = out.transpose(0, 2, 1, 3).reshape(b, s, NH * D)
            return out @ wo

        def moe(h, gate_w, w1, w2, w3):
            b, s, hd = h.shape
            t = h.reshape(-1, hd)
            T = t.shape[0]
            probs = jax.nn.softmax(t @ gate_w, axis=-1)
            topw, topi = jax.lax.top_k(probs, TOPK)
            topw = topw / jnp.sum(topw, axis=-1, keepdims=True)
            combine = jnp.zeros((T, E), t.dtype).at[jnp.arange(T)[:, None], topi].add(topw)
            up = jnp.einsum('th,ehf->etf', t, w1)
            gated = jax.nn.relu(up) * jnp.einsum('th,ehf->etf', t, w3)
            down = jnp.einsum('etf,efh->eth', gated, w2)
            out = jnp.einsum('eth,te->th', down, combine)
            return out.reshape(b, s, hd)
        key = jax.random.key(seed)
        ks = jax.random.split(key, 12)
        sc = 0.02
        return {'x': jax.random.normal(ks[0], (B, S, H), dtype=jnp.float32), 'ln1_w': jnp.ones((H,), jnp.float32), 'wq': jax.random.normal(ks[1], (H, NH * D), jnp.float32) * sc, 'wk': jax.random.normal(ks[2], (H, NKV * D), jnp.float32) * sc, 'wv': jax.random.normal(ks[3], (H, NKV * D), jnp.float32) * sc, 'wo': jax.random.normal(ks[4], (NH * D, H), jnp.float32) * sc, 'ln2_w': jnp.ones((H,), jnp.float32), 'gate_w': jax.random.normal(ks[5], (H, E), jnp.float32) * sc, 'w1': jax.random.normal(ks[6], (E, H, F), jnp.float32) * sc, 'w2': jax.random.normal(ks[7], (E, F, H), jnp.float32) * sc, 'w3': jax.random.normal(ks[8], (E, H, F), jnp.float32) * sc}
    _L0_ffn_in = _L0_ffn_setup()

    def _L1_attn_setup():
        import jax, jax.numpy as jnp
        import numpy as np
        from jax import lax
        BATCH = 2
        SEQ = 256
        HID = 256
        EXPAND = 2
        INTER = EXPAND * HID
        HEADS = 64
        PDIM = INTER // HEADS
        NSTATE = 128
        G = 1
        HPG = HEADS // G
        KCONV = 4
        GTS = G * NSTATE
        CONV_DIM = INTER + 2 * GTS
        PROJ_DIM = 2 * INTER + 2 * GTS + HEADS
        EPS = 1e-05
        MUP = (0.25, 0.5, 0.5, 0.5, 1.0)

        def _mup_vector():
            return jnp.concatenate([jnp.full((INTER,), MUP[0], jnp.float32), jnp.full((INTER,), MUP[1], jnp.float32), jnp.full((GTS,), MUP[2], jnp.float32), jnp.full((GTS,), MUP[3], jnp.float32), jnp.full((HEADS,), MUP[4], jnp.float32)])

        def _forward(hidden_states, in_proj_w, conv_w, conv_b, A_log, D, dt_bias, norm_w, out_proj_w):
            b, l, _ = hidden_states.shape
            proj = hidden_states @ in_proj_w * _mup_vector()
            z = proj[..., :INTER]
            xBC = proj[..., INTER:INTER + CONV_DIM]
            dt = proj[..., INTER + CONV_DIM:]
            xBC_cl = jnp.swapaxes(xBC, 1, 2)
            conv = lax.conv_general_dilated(xBC_cl, conv_w[:, None, :], window_strides=(1,), padding=((KCONV - 1, 0),), feature_group_count=CONV_DIM)
            xBC = jax.nn.silu(jnp.swapaxes(conv + conv_b[None, :, None], 1, 2))
            x = xBC[..., :INTER].reshape(b, l, G, HPG, PDIM)
            Bm = xBC[..., INTER:INTER + GTS].reshape(b, l, G, NSTATE)
            Cm = xBC[..., INTER + GTS:].reshape(b, l, G, NSTATE)
            dt = jax.nn.softplus(dt + dt_bias)
            A = -jnp.exp(A_log)
            dA = jnp.exp(dt * A).reshape(b, l, G, HPG)
            dtx = dt.reshape(b, l, G, HPG)[..., None] * x

            def step(state, inp):
                dA_t, dtx_t, B_t, C_t = inp
                state = state * dA_t[..., None, None] + jnp.einsum('bgcp,bgn->bgcpn', dtx_t, B_t)
                y_t = jnp.einsum('bgn,bgcpn->bgcp', C_t, state)
                return (state, y_t)
            inputs = (jnp.moveaxis(dA, 1, 0), jnp.moveaxis(dtx, 1, 0), jnp.moveaxis(Bm, 1, 0), jnp.moveaxis(Cm, 1, 0))
            state0 = jnp.zeros((b, G, HPG, PDIM, NSTATE), hidden_states.dtype)
            _, ys = lax.scan(step, state0, inputs)
            y = jnp.moveaxis(ys, 0, 1) + D.reshape(1, 1, G, HPG, 1) * x
            y = y.reshape(b, l, INTER)
            yg = y.reshape(b, l, G, INTER // G)
            var = jnp.mean(jnp.square(yg), axis=-1, keepdims=True)
            yn = (yg * lax.rsqrt(var + EPS)).reshape(b, l, INTER) * norm_w
            out = yn * jax.nn.silu(z)
            return out @ out_proj_w
        key = jax.random.key(seed)
        ks = jax.random.split(key, 8)
        hidden_states = jax.random.normal(ks[0], (BATCH, SEQ, HID), jnp.float32)
        in_proj_w = jax.random.normal(ks[1], (HID, PROJ_DIM), jnp.float32) * 0.02
        conv_w = jax.random.normal(ks[2], (CONV_DIM, KCONV), jnp.float32) * 0.2
        conv_b = jnp.zeros((CONV_DIM,), jnp.float32)
        A_log = jnp.log(jnp.arange(1, HEADS + 1, dtype=jnp.float32))
        D = jnp.ones((HEADS,), jnp.float32)
        dt_bias = jax.random.uniform(ks[3], (HEADS,), jnp.float32)
        norm_w = jnp.ones((INTER,), jnp.float32)
        out_proj_w = jax.random.normal(ks[4], (INTER, HID), jnp.float32) * 0.02
        return dict(hidden_states=hidden_states, in_proj_w=in_proj_w, conv_w=conv_w, conv_b=conv_b, A_log=A_log, D=D, dt_bias=dt_bias, norm_w=norm_w, out_proj_w=out_proj_w)
    _L1_attn_in = _L1_attn_setup()

    def _L1_ffn_setup():
        import jax, jax.numpy as jnp
        import numpy as np
        B, S, D = (2, 256, 256)
        MOE_D = 176
        E = 16
        K = 6
        ALPHA = 0.001

        def _moe_forward(x, gate_w, w_gate, w_up, w_down):
            b, s, d = x.shape
            T = b * s
            h = x.reshape(T, d)
            logits = h @ gate_w.T
            scores = jax.nn.softmax(logits.astype(jnp.float32), axis=-1)
            topk_w, topk_idx = jax.lax.top_k(scores, K)
            cw = jnp.zeros((T, E), jnp.float32)
            cw = cw.at[jnp.arange(T)[:, None], topk_idx].add(topk_w)
            y = jnp.zeros((T, d), x.dtype)
            for e in range(E):
                g = h @ w_gate[e].T
                u = h @ w_up[e].T
                out = jax.nn.silu(g) * u @ w_down[e].T
                y = y + cw[:, e:e + 1].astype(x.dtype) * out
            counts = jnp.sum(jax.nn.one_hot(topk_idx.reshape(b, s * K), E, dtype=jnp.float32), axis=1)
            ce = counts * (E / (s * K))
            scores_bse = scores.reshape(b, s, E)
            aux = jnp.mean(jnp.sum(ce * scores_bse.mean(axis=1), axis=1)) * ALPHA
            return (y.reshape(b, s, d), aux)
        key = jax.random.key(seed)
        ks = jax.random.split(key, 5)
        sd = 1.0 / np.sqrt(D)
        sm = 1.0 / np.sqrt(MOE_D)
        return {'x': jax.random.normal(ks[0], (B, S, D), jnp.float32), 'gate_w': jax.random.normal(ks[1], (E, D), jnp.float32) * sd, 'w_gate': jax.random.normal(ks[2], (E, MOE_D, D), jnp.float32) * sd, 'w_up': jax.random.normal(ks[3], (E, MOE_D, D), jnp.float32) * sd, 'w_down': jax.random.normal(ks[4], (E, D, MOE_D), jnp.float32) * sm}
    _L1_ffn_in = _L1_ffn_setup()
    _d = {'L0_attn_x': _L0_attn_in['x'], 'L0_attn_in_proj_w': _L0_attn_in['in_proj_w'], 'L0_attn_conv_w': _L0_attn_in['conv_w'], 'L0_attn_conv_b': _L0_attn_in['conv_b'], 'L0_attn_dt_bias': _L0_attn_in['dt_bias'], 'L0_attn_A_log': _L0_attn_in['A_log'], 'L0_attn_D': _L0_attn_in['D'], 'L0_attn_norm_w': _L0_attn_in['norm_w'], 'L0_attn_out_proj_w': _L0_attn_in['out_proj_w'], 'L0_ffn_ln1_w': _L0_ffn_in['ln1_w'], 'L0_ffn_wq': _L0_ffn_in['wq'], 'L0_ffn_wk': _L0_ffn_in['wk'], 'L0_ffn_wv': _L0_ffn_in['wv'], 'L0_ffn_wo': _L0_ffn_in['wo'], 'L0_ffn_ln2_w': _L0_ffn_in['ln2_w'], 'L0_ffn_gate_w': _L0_ffn_in['gate_w'], 'L0_ffn_w1': _L0_ffn_in['w1'], 'L0_ffn_w2': _L0_ffn_in['w2'], 'L0_ffn_w3': _L0_ffn_in['w3'], 'L1_attn_in_proj_w': _L1_attn_in['in_proj_w'], 'L1_attn_conv_w': _L1_attn_in['conv_w'], 'L1_attn_conv_b': _L1_attn_in['conv_b'], 'L1_attn_A_log': _L1_attn_in['A_log'], 'L1_attn_D': _L1_attn_in['D'], 'L1_attn_dt_bias': _L1_attn_in['dt_bias'], 'L1_attn_norm_w': _L1_attn_in['norm_w'], 'L1_attn_out_proj_w': _L1_attn_in['out_proj_w'], 'L1_ffn_gate_w': _L1_ffn_in['gate_w'], 'L1_ffn_w_gate': _L1_ffn_in['w_gate'], 'L1_ffn_w_up': _L1_ffn_in['w_up'], 'L1_ffn_w_down': _L1_ffn_in['w_down']}
    _x0 = _d['L0_attn_x']
    _d['L0_attn_x'] = jax.random.normal(jax.random.fold_in(jax.random.key(seed), 1), (4, 256, 256), dtype=_x0.dtype)
    del _x0
    return _d

def reference(L0_attn_x, L0_attn_in_proj_w, L0_attn_conv_w, L0_attn_conv_b, L0_attn_dt_bias, L0_attn_A_log, L0_attn_D, L0_attn_norm_w, L0_attn_out_proj_w, L0_ffn_ln1_w, L0_ffn_wq, L0_ffn_wk, L0_ffn_wv, L0_ffn_wo, L0_ffn_ln2_w, L0_ffn_gate_w, L0_ffn_w1, L0_ffn_w2, L0_ffn_w3, L1_attn_in_proj_w, L1_attn_conv_w, L1_attn_conv_b, L1_attn_A_log, L1_attn_D, L1_attn_dt_bias, L1_attn_norm_w, L1_attn_out_proj_w, L1_ffn_gate_w, L1_ffn_w_gate, L1_ffn_w_up, L1_ffn_w_down):

    def _L0_attn_ref(x, in_proj_w, conv_w, conv_b, dt_bias, A_log, D, norm_w, out_proj_w):
        import jax, jax.numpy as jnp
        import numpy as np
        B_, S, H = (2, 256, 256)
        E = 2 * H
        P = 64
        NH = E // P
        N = 64
        G = 1
        K = 4
        CS = 32
        CONV_DIM = E + 2 * G * N
        PROJ = E + CONV_DIM + NH
        EPS = 1e-06

        def segment_sum(a):
            l = a.shape[-1]
            a_exp = jnp.broadcast_to(a[..., None], (*a.shape, l))
            a_exp = jnp.where(jnp.tril(jnp.ones((l, l), bool), -1), a_exp, 0.0)
            s = jnp.cumsum(a_exp, axis=-2)
            return jnp.where(jnp.tril(jnp.ones((l, l), bool), 0), s, -jnp.inf)
        b, s, _ = x.shape
        proj = x @ in_proj_w.T
        gate, hBC, dt = jnp.split(proj, [E, E + CONV_DIM], axis=-1)
        xp = jnp.pad(hBC, ((0, 0), (K - 1, 0), (0, 0)))
        conv = sum((xp[:, k:k + s, :] * conv_w[:, k] for k in range(K))) + conv_b
        hBC = jax.nn.silu(conv)
        h, Bm, Cm = jnp.split(hBC, [E, E + G * N], axis=-1)
        dt = jax.nn.softplus(dt + dt_bias)
        A = -jnp.exp(A_log)
        h = h.reshape(b, s, NH, P)
        Bm = jnp.tile(Bm.reshape(b, s, G, N), (1, 1, NH // G, 1))
        Cm = jnp.tile(Cm.reshape(b, s, G, N), (1, 1, NH // G, 1))
        pad = -s % CS
        D_res = D[:, None] * jnp.pad(h, ((0, 0), (0, pad), (0, 0), (0, 0)))
        h = h * dt[..., None]
        A_d = A * dt

        def chunk(t):
            t = jnp.pad(t, ((0, 0), (0, pad)) + ((0, 0),) * (t.ndim - 2))
            return t.reshape(b, -1, CS, *t.shape[2:])
        hc, Ac, Bc, Cc = (chunk(h), chunk(A_d), chunk(Bm), chunk(Cm))
        Ac = jnp.transpose(Ac, (0, 3, 1, 2))
        A_cs = jnp.cumsum(Ac, axis=-1)
        L = jnp.exp(segment_sum(Ac))
        Gm = jnp.einsum('bclhn,bcshn->bclsh', Cc, Bc)
        M = Gm * jnp.transpose(L, (0, 2, 3, 4, 1))
        Y_diag = jnp.einsum('bclsh,bcshp->bclhp', M, hc)
        decay = jnp.exp(A_cs[..., -1:] - A_cs)
        Bdec = Bc * jnp.transpose(decay, (0, 2, 3, 1))[..., None]
        states = jnp.einsum('bclhn,bclhp->bchpn', Bdec, hc)
        states = jnp.concatenate([jnp.zeros_like(states[:, :1]), states], axis=1)
        A_last = jnp.pad(A_cs[..., -1], ((0, 0), (0, 0), (1, 0)))
        dchunk = jnp.transpose(jnp.exp(segment_sum(A_last)), (0, 3, 2, 1))
        new_states = jnp.einsum('bzjh,bzhpn->bjhpn', dchunk, states)
        states = new_states[:, :-1]
        sdo = jnp.exp(A_cs)
        Y_off = jnp.einsum('bclhn,bchpn->bclhp', Cc, states) * jnp.transpose(sdo, (0, 2, 3, 1))[..., None]
        y = (Y_diag + Y_off).reshape(b, -1, NH, P) + D_res
        y = y[:, :s].reshape(b, s, E)
        yf = y * jax.nn.silu(gate)
        var = jnp.mean(yf * yf, axis=-1, keepdims=True)
        yn = norm_w * (yf * jax.lax.rsqrt(var + EPS))
        return yn @ out_proj_w.T

    def _L0_ffn_ref(x, ln1_w, wq, wk, wv, wo, ln2_w, gate_w, w1, w2, w3):
        import jax, jax.numpy as jnp
        import numpy as np
        B, S, H = (1, 128, 256)
        NH, NKV, D = (32, 8, 64)
        GROUPS = NH // NKV
        E, F, TOPK = (8, 1024, 2)
        EPS = 1e-05

        def rmsnorm(x, w):
            return x * jax.lax.rsqrt(jnp.mean(x * x, axis=-1, keepdims=True) + EPS) * w

        def attention(h, wq, wk, wv, wo):
            b, s, _ = h.shape
            q = (h @ wq).reshape(b, s, NH, D).transpose(0, 2, 1, 3)
            k = (h @ wk).reshape(b, s, NKV, D).transpose(0, 2, 1, 3)
            v = (h @ wv).reshape(b, s, NKV, D).transpose(0, 2, 1, 3)
            k = jnp.repeat(k, GROUPS, axis=1)
            v = jnp.repeat(v, GROUPS, axis=1)
            scores = jnp.einsum('bhqd,bhkd->bhqk', q, k) / jnp.sqrt(jnp.float32(D))
            causal = jnp.tril(jnp.ones((s, s), bool))
            scores = jnp.where(causal, scores, jnp.finfo(scores.dtype).min)
            attn = jax.nn.softmax(scores, axis=-1)
            out = jnp.einsum('bhqk,bhkd->bhqd', attn, v)
            out = out.transpose(0, 2, 1, 3).reshape(b, s, NH * D)
            return out @ wo

        def moe(h, gate_w, w1, w2, w3):
            b, s, hd = h.shape
            t = h.reshape(-1, hd)
            T = t.shape[0]
            probs = jax.nn.softmax(t @ gate_w, axis=-1)
            topw, topi = jax.lax.top_k(probs, TOPK)
            topw = topw / jnp.sum(topw, axis=-1, keepdims=True)
            combine = jnp.zeros((T, E), t.dtype).at[jnp.arange(T)[:, None], topi].add(topw)
            up = jnp.einsum('th,ehf->etf', t, w1)
            gated = jax.nn.relu(up) * jnp.einsum('th,ehf->etf', t, w3)
            down = jnp.einsum('etf,efh->eth', gated, w2)
            out = jnp.einsum('eth,te->th', down, combine)
            return out.reshape(b, s, hd)
        h = x + attention(rmsnorm(x, ln1_w), wq, wk, wv, wo)
        return h + moe(rmsnorm(h, ln2_w), gate_w, w1, w2, w3)

    def _L1_attn_ref(hidden_states, in_proj_w, conv_w, conv_b, A_log, D, dt_bias, norm_w, out_proj_w):
        import jax, jax.numpy as jnp
        import numpy as np
        from jax import lax
        BATCH = 2
        SEQ = 256
        HID = 256
        EXPAND = 2
        INTER = EXPAND * HID
        HEADS = 64
        PDIM = INTER // HEADS
        NSTATE = 128
        G = 1
        HPG = HEADS // G
        KCONV = 4
        GTS = G * NSTATE
        CONV_DIM = INTER + 2 * GTS
        PROJ_DIM = 2 * INTER + 2 * GTS + HEADS
        EPS = 1e-05
        MUP = (0.25, 0.5, 0.5, 0.5, 1.0)

        def _mup_vector():
            return jnp.concatenate([jnp.full((INTER,), MUP[0], jnp.float32), jnp.full((INTER,), MUP[1], jnp.float32), jnp.full((GTS,), MUP[2], jnp.float32), jnp.full((GTS,), MUP[3], jnp.float32), jnp.full((HEADS,), MUP[4], jnp.float32)])

        def _forward(hidden_states, in_proj_w, conv_w, conv_b, A_log, D, dt_bias, norm_w, out_proj_w):
            b, l, _ = hidden_states.shape
            proj = hidden_states @ in_proj_w * _mup_vector()
            z = proj[..., :INTER]
            xBC = proj[..., INTER:INTER + CONV_DIM]
            dt = proj[..., INTER + CONV_DIM:]
            xBC_cl = jnp.swapaxes(xBC, 1, 2)
            conv = lax.conv_general_dilated(xBC_cl, conv_w[:, None, :], window_strides=(1,), padding=((KCONV - 1, 0),), feature_group_count=CONV_DIM)
            xBC = jax.nn.silu(jnp.swapaxes(conv + conv_b[None, :, None], 1, 2))
            x = xBC[..., :INTER].reshape(b, l, G, HPG, PDIM)
            Bm = xBC[..., INTER:INTER + GTS].reshape(b, l, G, NSTATE)
            Cm = xBC[..., INTER + GTS:].reshape(b, l, G, NSTATE)
            dt = jax.nn.softplus(dt + dt_bias)
            A = -jnp.exp(A_log)
            dA = jnp.exp(dt * A).reshape(b, l, G, HPG)
            dtx = dt.reshape(b, l, G, HPG)[..., None] * x

            def step(state, inp):
                dA_t, dtx_t, B_t, C_t = inp
                state = state * dA_t[..., None, None] + jnp.einsum('bgcp,bgn->bgcpn', dtx_t, B_t)
                y_t = jnp.einsum('bgn,bgcpn->bgcp', C_t, state)
                return (state, y_t)
            inputs = (jnp.moveaxis(dA, 1, 0), jnp.moveaxis(dtx, 1, 0), jnp.moveaxis(Bm, 1, 0), jnp.moveaxis(Cm, 1, 0))
            state0 = jnp.zeros((b, G, HPG, PDIM, NSTATE), hidden_states.dtype)
            _, ys = lax.scan(step, state0, inputs)
            y = jnp.moveaxis(ys, 0, 1) + D.reshape(1, 1, G, HPG, 1) * x
            y = y.reshape(b, l, INTER)
            yg = y.reshape(b, l, G, INTER // G)
            var = jnp.mean(jnp.square(yg), axis=-1, keepdims=True)
            yn = (yg * lax.rsqrt(var + EPS)).reshape(b, l, INTER) * norm_w
            out = yn * jax.nn.silu(z)
            return out @ out_proj_w
        return _forward(hidden_states, in_proj_w, conv_w, conv_b, A_log, D, dt_bias, norm_w, out_proj_w)

    def _L1_ffn_ref(x, gate_w, w_gate, w_up, w_down):
        import jax, jax.numpy as jnp
        import numpy as np
        B, S, D = (2, 256, 256)
        MOE_D = 176
        E = 16
        K = 6
        ALPHA = 0.001

        def _moe_forward(x, gate_w, w_gate, w_up, w_down):
            b, s, d = x.shape
            T = b * s
            h = x.reshape(T, d)
            logits = h @ gate_w.T
            scores = jax.nn.softmax(logits.astype(jnp.float32), axis=-1)
            topk_w, topk_idx = jax.lax.top_k(scores, K)
            cw = jnp.zeros((T, E), jnp.float32)
            cw = cw.at[jnp.arange(T)[:, None], topk_idx].add(topk_w)
            y = jnp.zeros((T, d), x.dtype)
            for e in range(E):
                g = h @ w_gate[e].T
                u = h @ w_up[e].T
                out = jax.nn.silu(g) * u @ w_down[e].T
                y = y + cw[:, e:e + 1].astype(x.dtype) * out
            counts = jnp.sum(jax.nn.one_hot(topk_idx.reshape(b, s * K), E, dtype=jnp.float32), axis=1)
            ce = counts * (E / (s * K))
            scores_bse = scores.reshape(b, s, E)
            aux = jnp.mean(jnp.sum(ce * scores_bse.mean(axis=1), axis=1)) * ALPHA
            return (y.reshape(b, s, d), aux)
        y, _aux = _moe_forward(x, gate_w, w_gate, w_up, w_down)
        return y
    x = L0_attn_x
    xn = _layernorm(x, axis=-1)
    x = x + _L0_attn_ref(xn, L0_attn_in_proj_w, L0_attn_conv_w, L0_attn_conv_b, L0_attn_dt_bias, L0_attn_A_log, L0_attn_D, L0_attn_norm_w, L0_attn_out_proj_w) + _L0_ffn_ref(xn, L0_ffn_ln1_w, L0_ffn_wq, L0_ffn_wk, L0_ffn_wv, L0_ffn_wo, L0_ffn_ln2_w, L0_ffn_gate_w, L0_ffn_w1, L0_ffn_w2, L0_ffn_w3)
    xn = _layernorm(x, axis=-1)
    x = x + _L1_attn_ref(xn, L1_attn_in_proj_w, L1_attn_conv_w, L1_attn_conv_b, L1_attn_A_log, L1_attn_D, L1_attn_dt_bias, L1_attn_norm_w, L1_attn_out_proj_w) + _L1_ffn_ref(xn, L1_ffn_gate_w, L1_ffn_w_gate, L1_ffn_w_up, L1_ffn_w_down)
    return x

_drawn_inputs = setup_inputs


def setup_inputs(seed=0):
    import zlib

    import numpy as np

    out = dict(_drawn_inputs(seed))
    spreads = {'L0_attn_conv_b': (0.0, 0.1),
     'L0_attn_D': (1.0, 0.6),
     'L0_attn_norm_w': (1.0, 0.559),
     'L0_ffn_ln1_w': (1.0, 0.6),
     'L0_ffn_ln2_w': (1.0, 0.6),
     'L1_attn_conv_b': (0.0, 0.8),
     'L1_attn_D': (1.0, 0.6),
     'L1_attn_norm_w': (1.0, 0.6)}
    factors = {'L0_attn_dt_bias': 64.0,
     'L0_attn_A_log': 8.0,
     'L0_ffn_wq': 8.0,
     'L0_ffn_wk': 8.0,
     'L0_ffn_gate_w': 3.389,
     'L0_ffn_w1': 3.591,
     'L0_ffn_w2': 3.01,
     'L0_ffn_w3': 2.999,
     'L1_attn_in_proj_w': 6.242,
     'L1_attn_conv_w': 8.0,
     'L1_attn_A_log': 51.852,
     'L1_attn_dt_bias': 8.0,
     'L1_attn_out_proj_w': 6.266}
    for name, (base, spread) in spreads.items():
        noise = np.random.default_rng([zlib.crc32(name.encode()), seed]).standard_normal(out[name].shape)
        drawn = base * np.exp(spread * noise) if base else spread * noise
        out[name] = jnp.asarray(drawn.astype(out[name].dtype))
    for name, factor in factors.items():
        out[name] = (out[name] * factor).astype(out[name].dtype)
    return out
```

```python
from contextlib import ExitStack

import numpy as np
import concourse.bass as bass
from concourse import mybir
from concourse.alu_op_type import AluOpType as ALU

F32 = mybir.dt.float32
F32R = mybir.dt.float32r
BF16 = mybir.dt.bfloat16
ACT = mybir.ActivationFunctionType
X = mybir.AxisListType.X

P = 128
B, S, H = 4, 256, 256
T = B * S
KH = H // P
HALF = 512
NHALF = T // HALF
TT = T // P

E0, N0, NH0, P0, Q0 = 512, 64, 8, 64, 128
NE0 = E0 // P
PROJ0 = 2 * E0 + 2 * N0 + NH0
KCONV = 4
NHQ, NKV, D = 32, 8, 64
QT = NHQ * D // P
KT = NKV * D // P
X0, F0, TOP0 = 8, 1024, 2
FT0 = F0 // P
E1, N1, NH1, P1, Q1 = 512, 128, 64, 8, 32
NE1 = E1 // P
NC1 = S // Q1
PROJ1 = 2 * E1 + 2 * N1 + NH1
X1, F1, TOP1 = 16, 176, 6
FT1 = X1 * F1 // P
NEG_MASK = -3.0e38


def half(hf):
    return slice(hf * HALF, (hf + 1) * HALF)


def turns(eng, n):
    yield 0
    with eng.Fori(1, n) as i:
        yield i


def wait_after(eng, sem, n):
    if not (isinstance(n, int) and n <= 0):
        eng.wait_ge(sem, n)


def product3(nc, out, w_hi, w_lo, x_hi, x_lo, start, stop):
    nc.tensor.matmul(out, w_hi, x_hi, start=start, stop=False)
    nc.tensor.matmul(out, w_hi, x_lo, start=False, stop=False)
    return nc.tensor.matmul(out, w_lo, x_hi, start=False, stop=stop)
def norm_phase(nc, new, name, src, dst, ones, eps, centred, weight=None, hi=None, lo=None, ready=None):
    n = src.shape[1]
    width = n * P
    with ExitStack() as ctx:
        sb, sem = new(ctx)
        xc = sb("xc", [P, n, T]) if centred else src
        sq = sb("sq", [P, n, T])
        std = sb("std", [P, T])
        rstd = sb("rstd", [P, T])
        ps_mean = ctx.enter_context(nc.psum_tensor(name + "_ps_mean", [P, NHALF, HALF], F32))
        ps_sq = ctx.enter_context(nc.psum_tensor(name + "_ps_sq", [P, NHALF, HALF], F32))
        sums, centre, squared, sq_sums, stds, rstds, normed, his, los = (
            sem(s) for s in ("sums", "centre", "squared", "sq_sums", "stds", "rstds", "normed", "his", "los"))
        block = ctx.enter_context(nc.Block())

        @block.tensor
        def _(pe):
            if ready is not None:
                pe.wait_ge(*ready)
            if centred:
                for hf in range(NHALF):
                    for k in range(n):
                        mm = nc.tensor.matmul(ps_mean[:, hf], ones, src[:, k, half(hf)], start=k == 0, stop=k == n - 1)
                    mm.then_inc(sums, 1)
            for hf in range(NHALF):
                pe.wait_ge(squared, hf + 1)
                for k in range(n):
                    mm = nc.tensor.matmul(ps_sq[:, hf], ones, sq[:, k, half(hf)], start=k == 0, stop=k == n - 1)
                mm.then_inc(sq_sums, 1)

        @block.scalar
        def _(act):
            if ready is not None:
                act.wait_ge(*ready)
            for hf in range(NHALF):
                if centred:
                    act.wait_ge(centre, hf + 1)
                nc.scalar.activation(sq[:, :, half(hf)], xc[:, :, half(hf)], ACT.Square).then_inc(squared, 1)
            for hf in range(NHALF):
                act.wait_ge(sq_sums, hf + 1)
                nc.scalar.activation(std[:, half(hf)], ps_sq[:, hf], ACT.Sqrt, bias=eps, scale=1.0 / width).then_inc(stds, 1)
            if hi is not None:
                for hf in range(NHALF):
                    act.wait_ge(normed, hf + 1)
                    nc.scalar.activation(hi[:, :, half(hf)], dst[:, :, half(hf)], ACT.Copy).then_inc(his, 1)

        @block.vector
        def _(dve):
            if ready is not None:
                dve.wait_ge(*ready)
            if centred:
                for hf in range(NHALF):
                    dve.wait_ge(sums, hf + 1)
                    for k in range(n):
                        op = nc.vector.scalar_tensor_tensor(out=xc[:, k, half(hf)], in0=ps_mean[:, hf], scalar=-1.0 / width,
                                                            in1=src[:, k, half(hf)], op0=ALU.mult, op1=ALU.add)
                    op.then_inc(centre, 1)
                dve.wait_ge(centre, NHALF)
            for hf in range(NHALF):
                dve.wait_ge(stds, hf + 1)
                nc.vector.reciprocal(rstd[:, half(hf)], std[:, half(hf)]).then_inc(rstds, 1)
                dve.wait_ge(rstds, hf + 1)
                for k in range(n):
                    if weight is None:
                        op = nc.vector.tensor_tensor(dst[:, k, half(hf)], xc[:, k, half(hf)], rstd[:, half(hf)], ALU.mult)
                    else:
                        op = nc.vector.scalar_tensor_tensor(out=dst[:, k, half(hf)], in0=xc[:, k, half(hf)],
                                                            scalar=weight[:, k:k + 1], in1=rstd[:, half(hf)],
                                                            op0=ALU.mult, op1=ALU.mult)
                op.then_inc(normed, 1)
            if hi is not None:
                for hf in range(NHALF):
                    dve.wait_ge(his, hf + 1)
                    nc.vector.tensor_tensor(lo[:, :, half(hf)], dst[:, :, half(hf)], hi[:, :, half(hf)].bitcast(F32),
                                            ALU.subtract).then_inc(los, 1)
def softplus_step(nc, dve, act_side, x, a, e, u, ln, dt, sems):
    chain, magnitude, exped, summed, logged, ready = sems
    if act_side:
        dve.wait_ge(magnitude, 1)
        nc.scalar.activation(e, a, ACT.Exp, scale=-1.0).then_inc(exped, 1)
        dve.wait_ge(summed, 1)
        nc.scalar.activation(ln, u, ACT.Ln).then_inc(logged, 1)
        return
    nc.vector.tensor_scalar(a, x, -1.0, None, ALU.mult).then_inc(chain, 1)
    dve.wait_ge(chain, 1)
    nc.vector.tensor_tensor(a, a, x, ALU.max).then_inc(magnitude, 1)
    dve.wait_ge(exped, 1)
    nc.vector.tensor_scalar(u, e, 1.0, None, ALU.add).then_inc(summed, 1)
    dve.wait_ge(logged, 1)
    nc.vector.scalar_tensor_tensor(out=u, in0=u, scalar=-1.0, in1=e, op0=ALU.add, op1=ALU.subtract).then_inc(chain, 1)
    dve.wait_ge(chain, 2)
    nc.vector.tensor_tensor(ln, ln, u, ALU.subtract).then_inc(chain, 1)
    dve.wait_ge(chain, 3)
    nc.vector.scalar_tensor_tensor(out=dt, in0=x, scalar=0.0, in1=ln, op0=ALU.max, op1=ALU.add).then_inc(ready, 1)


def causal_taps(nc, dve, acc, padded, taps_w, bias, taps, done):
    nc.vector.tensor_scalar(acc, padded[:, :, 0:S], taps_w[:, 0:1], bias, ALU.mult, ALU.add).then_inc(taps, 1)
    for k in range(1, KCONV):
        dve.wait_ge(taps, done + k)
        nc.vector.scalar_tensor_tensor(out=acc, in0=padded[:, :, k:k + S], scalar=taps_w[:, k:k + 1], in1=acc,
                                       op0=ALU.mult, op1=ALU.add).then_inc(taps, 1)


def mixer_project(nc, new, name, w_dram, cw_dram, xn_hi, xn_lo, conv_outs, gate_s, dt, cp, dt_rows, tiles, mup, dcol, bias_col, da_dram,
                  Q, store):
    dt_tile, DT, dt_alone = dt_rows
    nproj = w_dram.shape[1]
    nconv = len(conv_outs)
    with ExitStack() as ctx:
        sb, sem = new(ctx)
        w_raw = sb("w_raw", [P, KH, nproj])
        w_hi = sb("w_hi", [P, KH, nproj], F32R)
        w_lo = sb("w_lo", [P, KH, nproj], F32R)
        padded = sb("padded", [P, nconv, B, KCONV - 1 + S])
        acc = sb("acc", [P, 2, B, S])
        cw = sb("cw", [P, nconv, KCONV])
        dt_x, dt_a, dt_e, dt_u, dt_l = (sb(s, [P, T])[DT, :] for s in ("dt_x", "dt_a", "dt_e", "dt_u", "dt_l"))
        decay, decay0, decay_s = dt_a, dt_e, dt_u
        acol = sb("acol", [P, 3])
        ps = ctx.enter_context(nc.psum_tensor(name + "_ps", [P, 8, HALF], F32))
        (loaded, w_his, w_los, projected, act_took, dve_took, pads, taps, silued, chain, magnitude, exped, summed,
         logged, dt_ready, a_capped, a_exp, a_ready, exponents, decays, copied, zeroed, starts, cps, sent) = (sem(s) for s in (
            "loaded", "w_his", "w_los", "projected", "act_took", "dve_took", "pads", "taps", "silued", "chain", "magnitude",
            "exped", "summed", "logged", "dt_ready", "a_capped", "a_exp", "a_ready", "exponents", "decays", "copied", "zeroed", "starts", "cps", "sent"))
        block = ctx.enter_context(nc.Block())
        blocks = [(kind, c0, m, i, hf) for kind, c0, m, i in tiles for hf in range(NHALF)]
        on_dve = [kind == "conv" for kind, *_ in blocks]
        nth = [sum(1 for j in range(n + 1) if on_dve[j] == on_dve[n]) for n in range(len(blocks))]
        n_dve = sum(on_dve)

        @block.sync
        def _(sp):
            sp.dma_start(w_raw[:], w_dram.rearrange("(k p) n -> p k n", p=P)).then_inc(loaded, 16)
            sp.dma_start(cw[:], cw_dram).then_inc(loaded, 16)
            sp.wait_ge(zeroed, 1)
            sp.dma_start(da_dram.rearrange("c h l -> h c l"), decay0.rearrange("h (c l) -> h c l", l=Q)).then_inc(sent, 16)
            sp.wait_ge(sent, 16)

        @block.gpsimd
        def _(pool):
            nc.gpsimd.memset(padded[:, :, :, 0:KCONV - 1], 0.0).then_inc(pads, 1)
            pool.wait_ge(w_his, 1)
            nc.gpsimd.tensor_tensor(w_lo[:], w_raw[:], w_hi[:].bitcast(F32), ALU.subtract).then_inc(w_los, 1)

        @block.tensor
        def _(pe):
            pe.wait_ge(w_los, 1)
            for n, (kind, c0, m, i, hf) in enumerate(blocks):
                f = slice(c0, c0 + m)
                if n >= 8:
                    pe.wait_ge(dve_took if on_dve[n - 8] else act_took, nth[n - 8])
                for k in range(KH):
                    mm = product3(nc, ps[0:m, n % 8], w_hi[:, k, f], w_lo[:, k, f],
                                  xn_hi[:, k, half(hf)], xn_lo[:, k, half(hf)], k == 0, k == KH - 1)
                mm.then_inc(projected, 1)

        @block.scalar
        def _(act):
            act.wait_ge(loaded, 32)
            nc.scalar.activation(w_hi[:], w_raw[:], ACT.Copy).then_inc(w_his, 1)
            for n, (kind, c0, m, i, hf) in enumerate(blocks):
                if not on_dve[n]:
                    act.wait_ge(projected, n + 1)
                    nc.scalar.activation(gate_s[:, i, half(hf)], ps[:, n % 8], ACT.Silu, scale=mup[0]).then_inc(act_took, 1)
            softplus_step(nc, act, True, dt_x, dt_a, dt_e, dt_u, dt_l, dt, (chain, magnitude, exped, summed, logged, dt_ready))
            act.wait_ge(a_capped, 1)
            nc.scalar.activation(acol[DT, 1:2], acol[DT, 0:1], ACT.Exp).then_inc(a_exp, 1)
            act.wait_ge(exponents, 1)
            nc.scalar.activation(decay, decay, ACT.Exp).then_inc(decays, 1)
            for i, out in enumerate(conv_outs):
                m = out.shape[0]
                act.wait_ge(taps, KCONV * (i + 1))
                nc.scalar.activation(store(out), acc[0:m, i % 2], ACT.Silu).then_inc(silued, 1)

        @block.vector
        def _(dve):
            nc.vector.tensor_scalar(acol[DT, 0:1], dcol[DT, 1:2], 88.0, None, ALU.min).then_inc(a_capped, 1)
            dve.wait_ge(loaded, 32)
            dve.wait_ge(pads, 1)
            for n, (kind, c0, m, i, hf) in enumerate(blocks):
                if on_dve[n]:
                    dve.wait_ge(projected, n + 1)
                    if i >= 0:
                        mc = conv_outs[i].shape[0]
                        op = nc.vector.tensor_scalar(padded[0:mc, i, 2 * hf:2 * hf + 2, KCONV - 1:],
                                                     ps[0:mc, n % 8].rearrange("p (b s) -> p b s", b=2), mup[1], None, ALU.mult)
                    if i == dt_tile:
                        src = ps[DT, n % 8]
                        dst = dt_x[:, half(hf)] if dt_alone is None else dt_alone(dt_x, hf)
                        src = src if dt_alone is None else src.rearrange("p (b c l) -> p b c l", b=2, l=Q)
                        op = nc.vector.tensor_scalar(dst, src, dcol[DT, 0:1], None, ALU.add)
                    op.then_inc(dve_took, 1)
            dve.wait_ge(dve_took, n_dve)
            softplus_step(nc, dve, False, dt_x, dt_a, dt_e, dt_u, dt_l, dt, (chain, magnitude, exped, summed, logged, dt_ready))
            dve.wait_ge(a_exp, 1)
            nc.vector.tensor_scalar(acol[DT, 2:3], acol[DT, 1:2], -1.0, None, ALU.mult).then_inc(a_ready, 1)
            dve.wait_ge(a_ready, 1)
            dve.wait_ge(dt_ready, 1)
            nc.vector.tensor_scalar(decay, dt, acol[DT, 2:3], -200.0, ALU.mult, ALU.max).then_inc(exponents, 1)
            dve.wait_ge(decays, 1)
            nc.vector.tensor_copy(decay0, decay).then_inc(copied, 1)
            dve.wait_ge(copied, 1)
            nc.vector.memset(decay0.rearrange("h (c l) -> h c l", l=Q)[:, :, 0:1], 0.0).then_inc(zeroed, 1)
            dve.wait_ge(zeroed, 1)
            nc.vector.tensor_tensor(decay_s, decay, decay0, ALU.subtract).then_inc(starts, 1)
            dve.wait_ge(starts, 1)
            nc.vector.tensor_tensor_scan(cp, decay0, decay_s, 0.0, ALU.mult, ALU.add).then_inc(cps, 1)
            for i, out in enumerate(conv_outs):
                m = out.shape[0]
                if i >= 2:
                    dve.wait_ge(silued, i - 1)
                causal_taps(nc, dve, acc[0:m, i % 2], padded[0:m, i], cw[0:m, i], bias_col[0:m, i:i + 1], taps, KCONV * i)
def turn_phase(nc, new, name, conv_x, bt, dt, cp, DT, x_tok, b_tok, dt_tok, cp_tok, ident):
    n, nh = bt.shape[0], DT.stop - DT.start
    with ExitStack() as ctx:
        sb, sem = new(ctx)
        ps_x = ctx.enter_context(nc.psum_tensor(name + "_ps_x", [P, 2, HALF], F32))
        ps_b = ctx.enter_context(nc.psum_tensor(name + "_ps_b", [P, 2, HALF], F32))
        x_turned, b_turned, x_copied, b_copied = (sem(s) for s in ("x_turned", "b_turned", "x_copied", "b_copied"))
        block = ctx.enter_context(nc.Block())

        @block.tensor
        def _(pe):
            for t in range(TT):
                tok = slice(t * P, (t + 1) * P)
                if t >= 2:
                    wait_after(pe, x_copied, t - 1)
                for c in range(len(conv_x)):
                    mm = nc.tensor.transpose(ps_x[:, t % 2, c * P:(c + 1) * P], conv_x[c][:, tok], ident)
                mm.then_inc(x_turned, 1)
                if t >= 2:
                    wait_after(pe, b_copied, t - 1)
                o = ps_b[:, t % 2]
                nc.tensor.transpose(o[:, 0:n], bt[:, tok], ident[0:n, 0:n])
                nc.tensor.transpose(o[:, n:n + nh], dt[:, tok], ident[DT, DT])
                nc.tensor.transpose(o[:, n + nh:n + 2 * nh], cp[:, tok], ident[DT, DT]).then_inc(b_turned, 1)

        @block.scalar
        def _(act):
            for t in range(TT):
                act.wait_ge(x_turned, t + 1)
                nc.scalar.activation(x_tok[:, t, :], ps_x[:, t % 2], ACT.Copy).then_inc(x_copied, 1)

        @block.vector
        def _(dve):
            for t in range(TT):
                dve.wait_ge(b_turned, t + 1)
                o = ps_b[:, t % 2]
                nc.vector.tensor_copy(b_tok[:, t, :], o[:, 0:n])
                nc.vector.tensor_copy(dt_tok[:, t, :], o[:, n:n + nh])
                nc.vector.tensor_copy(cp_tok[:, t, :], o[:, n + nh:n + 2 * nh]).then_inc(b_copied, 1)


def scan0_phase(nc, new, conv_x, bt, ct, x_tok, b_tok, dt_tok, cp_tok, da_dram, delta_dram, d_col, gate_s, y_t, ident):
    with ExitStack() as ctx:
        sb, sem = new(ctx)
        NC = S // Q0
        delta = sb("delta", [P, NH0 * Q0])
        da = sb("da", [P, 2, NH0 * Q0])
        bts = sb("bts", [N0, 2, Q0])
        cts = sb("cts", [N0, 2, Q0])
        bs = sb("bs", [P, N0])
        decay = sb("decay", [P, 2, NH0, Q0])
        m = sb("m", [P, 2, NH0, Q0])
        xd = sb("xd", [P, 2, NH0, P0])
        xdec = sb("xdec", [P, NH0, P0])
        state = sb("state", [N0, E0])
        through = sb("through", [P, NH0, P0])
        y_tok = sb("y_tok", [P, 2, E0])
        ps_g = ctx.enter_context(nc.psum_tensor("s0_g", [P, 2, HALF], F32))
        ps_y = ctx.enter_context(nc.psum_tensor("s0_y", [P, 2, HALF], F32))
        ps_s = ctx.enter_context(nc.psum_tensor("s0_s", [P, HALF], F32))
        ps_o = ctx.enter_context(nc.psum_tensor("s0_o", [P, HALF], F32))
        ps_t = ctx.enter_context(nc.psum_tensor("s0_t", [P, 2, HALF], F32))
        (ld_delta, staged, g_made, scanned, m_made, xd_made, xdec_made, y_made, s_made, s_kept, o_made,
         o_scaled, y_kept, turned, y_out) = (sem(s) for s in (
            "ld_delta", "staged", "g_made", "scanned", "m_made", "xd_made", "xdec_made", "y_made", "s_made",
            "s_kept", "o_made", "o_scaled", "y_kept", "turned", "y_out"))
        ld_da = [sem("ld_da0"), sem("ld_da1")]
        block = ctx.enter_context(nc.Block())

        @block.sync
        def _(sp):
            sp.dma_start(delta[:], delta_dram).then_inc(ld_delta, 16)
            for c in range(2):
                sp.dma_start(da[:, c], da_dram[c:c + 1].rearrange("c h l -> c (h l)").partition_broadcast(P)).then_inc(ld_da[c], 16)
            with sp.Fori(1, B) as b:
                for c in range(2):
                    wait_after(sp, scanned, 2 * b + c - 1)
                    sp.dma_start(da[:, c], da_dram[bass.ds(2 * b + c, 1)].rearrange("c h l -> c (h l)").partition_broadcast(P)).then_inc(ld_da[c], 16)

        @block.tensor
        def _(pe):
            for b in turns(pe, B):
                for c in range(2):
                    pe.wait_ge(staged, 2 * b + c + 1)
                    nc.tensor.matmul(ps_g[:, c, 0:Q0], bts[:, c], cts[:, c], start=True, stop=True).then_inc(g_made, 1)
                for c in range(2):
                    if c == 1:
                        pe.wait_ge(s_kept, b + 1)
                        nc.tensor.matmul(ps_o[:], cts[:, 1], state[:], start=True, stop=True).then_inc(o_made, 1)
                    pe.wait_ge(m_made, 2 * b + c + 1)
                    pe.wait_ge(xd_made, 2 * b + c + 1)
                    for h in range(NH0):
                        mm = nc.tensor.matmul(ps_y[:, c, h * P0:(h + 1) * P0], m[:, c, h], xd[:, c, h], start=True, stop=True)
                    mm.then_inc(y_made, 1)
                    if c == 0:
                        pe.wait_ge(xdec_made, b + 1)
                        nc.tensor.matmul(ps_s[0:N0, :], bs[:], xdec[:].rearrange("p h q -> p (h q)"), start=True, stop=True).then_inc(s_made, 1)
                for c in range(2):
                    pe.wait_ge(y_kept, 2 * b + c + 1)
                    for t in range(NE0):
                        mm = nc.tensor.transpose(ps_t[:, c, t * P:(t + 1) * P], y_tok[:, c, t * P:(t + 1) * P], ident)
                    mm.then_inc(turned, 1)

        @block.scalar
        def _(act):
            for b in turns(act, B):
                act.wait_ge(s_made, b + 1)
                nc.scalar.activation(state[:], ps_s[0:N0, :], ACT.Copy).then_inc(s_kept, 1)
                act.wait_ge(y_made, 2 * b + 1)
                nc.scalar.activation(y_tok[:, 0], ps_y[:, 0], ACT.Copy).then_inc(y_kept, 1)

        @block.gpsimd
        def _(pool):
            for b in turns(pool, B):
                for c in range(2):
                    if c == 0:
                        wait_after(pool, o_made, b)
                    tok = bass.ds(b * S + c * Q0, Q0)
                    nc.gpsimd.tensor_copy(bts[:, c], bt[:, tok])
                    if c == 0:
                        wait_after(pool, s_made, b)
                        nc.gpsimd.tensor_copy(bs[:], b_tok[:, bass.ds(2 * b, 1), :].rearrange("p a n -> p (a n)"))
                    nc.gpsimd.tensor_copy(cts[:, c], ct[:, tok]).then_inc(staged, 1)

        @block.vector
        def _(dve):
            dve.wait_ge(ld_delta, 16)
            for b in turns(dve, B):
                for c in range(2):
                    dve.wait_ge(ld_da[c], 16 * (b + 1))
                    nc.vector.tensor_tensor_scan(decay[:, c].rearrange("p h l -> p (h l)"), da[:, c], delta[:], 0.0,
                                                 ALU.mult, ALU.add).then_inc(scanned, 1)
                    nc.vector.tensor_tensor(xd[:, c], x_tok[:, bass.ds(2 * b + c, 1), :].rearrange("p a (h q) -> p (a h) q", q=P0),
                                            dt_tok[:, bass.ds(2 * b + c, 1), :].rearrange("p a h -> p (a h)").unsqueeze(2).to_broadcast([P, NH0, P0]),
                                            ALU.mult).then_inc(xd_made, 1)
                    dve.wait_ge(scanned, 2 * b + c + 1)
                    dve.wait_ge(g_made, 2 * b + c + 1)
                    nc.vector.tensor_tensor(m[:, c], decay[:, c], ps_g[:, c, 0:Q0].unsqueeze(1).to_broadcast([P, NH0, Q0]),
                                            ALU.mult).then_inc(m_made, 1)
                    if c == 0:
                        dve.wait_ge(xd_made, 2 * b + 1)
                        nc.vector.tensor_tensor(xdec[:], xd[:, 0], decay[:, 0, :, Q0 - 1:Q0].to_broadcast([P, NH0, P0]),
                                                ALU.mult).then_inc(xdec_made, 1)
                dve.wait_ge(o_made, b + 1)
                nc.vector.tensor_tensor(through[:], ps_o[:].rearrange("p (h q) -> p h q", q=P0),
                                        cp_tok[:, bass.ds(2 * b + 1, 1), :].rearrange("p a h -> p (a h)").unsqueeze(2).to_broadcast([P, NH0, P0]),
                                        ALU.mult).then_inc(o_scaled, 1)
                dve.wait_ge(o_scaled, b + 1)
                dve.wait_ge(y_made, 2 * b + 2)
                dve.wait_ge(y_kept, 2 * b + 1)
                nc.vector.tensor_tensor(y_tok[:, 1], ps_y[:, 1], through[:].rearrange("p h q -> p (h q)"), ALU.add).then_inc(y_kept, 1)
                for c in range(2):
                    dve.wait_ge(turned, 2 * b + c + 1)
                    tok = bass.ds(b * S + c * Q0, Q0)
                    for t in range(NE0):
                        op = nc.vector.scalar_tensor_tensor(out=y_t[:, t, tok], in0=conv_x[t][:, tok], scalar=d_col[:, t:t + 1],
                                                            in1=ps_t[:, c, t * P:(t + 1) * P], op0=ALU.mult, op1=ALU.add)
                    op.then_inc(y_out, 1)
def router_phase(nc, new, name, h_t, gw, lower, w_dram, ident, X_, TOP, renorm):
    with ExitStack() as ctx:
        sb, sem = new(ctx)
        d = sb("d", [P, TT, X_])
        e = sb("e", [P, TT, X_])
        mx, den, rden = sb("mx", [P, TT]), sb("den", [P, TT]), sb("rden", [P, TT])
        gt = sb("gt", [P, TT, X_, X_])
        eq = sb("eq", [P, TT, X_, X_])
        rank = sb("rank", [P, TT, X_])
        w = sb("w", [P, TT, X_])
        w_t = sb("w_t", [X_, T])
        ps = ctx.enter_context(nc.psum_tensor(name + "_ps", [P, HALF], F32))
        ps_t = ctx.enter_context(nc.psum_tensor(name + "_ps_t", [P, NHALF, HALF], F32))
        logits, shifted, exped, weighed, turned, copied, sent, chain = (
            sem(s) for s in ("logits", "shifted", "exped", "weighed", "turned", "copied", "sent", "chain"))
        block = ctx.enter_context(nc.Block())

        @block.tensor
        def _(pe):
            for t in range(TT):
                for k in range(KH):
                    mm = nc.tensor.matmul(ps[:, t * X_:(t + 1) * X_], h_t[:, k, t * P:(t + 1) * P], gw[:, k, :],
                                          start=k == 0, stop=k == KH - 1)
            mm.then_inc(logits, 1)
            pe.wait_ge(weighed, 1)
            for t in range(TT):
                mm = nc.tensor.transpose(ps_t[0:X_, t // 4, (t % 4) * P:(t % 4 + 1) * P], w[:, t, :], ident)
            mm.then_inc(turned, 1)

        @block.scalar
        def _(act):
            act.wait_ge(shifted, 1)
            nc.scalar.activation(e[:], d[:], ACT.Exp).then_inc(exped, 1)
            act.wait_ge(turned, 1)
            nc.scalar.activation(w_t[:].rearrange("e (a t) -> e a t", a=NHALF), ps_t[0:X_], ACT.Copy).then_inc(copied, 1)

        @block.sync
        def _(sp):
            sp.wait_ge(copied, 1)
            sp.dma_start(w_dram, w_t[:]).then_inc(sent, 16)
            sp.wait_ge(sent, 16)

        @block.vector
        def _(dve):
            n = [0]

            def link(op):
                n[0] += 1
                op.then_inc(chain, 1)
                dve.wait_ge(chain, n[0])

            wide = [P, TT, X_]
            square = [P, TT, X_, X_]
            dve.wait_ge(logits, 1)
            l3 = ps[:, 0:TT * X_].rearrange("p (t e) -> p t e", e=X_)
            link(nc.vector.reduce_max(mx[:], l3, axis=X))
            nc.vector.tensor_tensor(d[:], l3, mx[:].unsqueeze(2).to_broadcast(wide), ALU.subtract).then_inc(shifted, 1)
            dve.wait_ge(exped, 1)
            link(nc.vector.reduce_sum(den[:], e[:], axis=X))
            link(nc.vector.reciprocal(rden[:], den[:]))
            link(nc.vector.tensor_tensor(e[:], e[:], rden[:].unsqueeze(2).to_broadcast(wide), ALU.mult))
            mine, other = e[:].unsqueeze(3).to_broadcast(square), e[:].unsqueeze(2).to_broadcast(square)
            link(nc.vector.tensor_tensor(eq[:], other, mine, ALU.is_equal))
            link(nc.vector.tensor_tensor(eq[:], eq[:], lower.unsqueeze(1).to_broadcast(square), ALU.mult))
            link(nc.vector.tensor_tensor(gt[:], other, mine, ALU.is_gt))
            link(nc.vector.tensor_tensor(gt[:], gt[:], eq[:], ALU.add))
            link(nc.vector.reduce_sum(rank[:], gt[:], axis=X))
            op = nc.vector.scalar_tensor_tensor(out=w[:], in0=rank[:], scalar=TOP - 0.5, in1=e[:], op0=ALU.is_lt, op1=ALU.mult)
            if renorm:
                link(op)
                link(nc.vector.reduce_sum(den[:], w[:], axis=X))
                link(nc.vector.reciprocal(rden[:], den[:]))
                op = nc.vector.tensor_tensor(w[:], w[:], rden[:].unsqueeze(2).to_broadcast(wide), ALU.mult)
            op.then_inc(weighed, 1)


def split_phase(nc, new, src, hi, lo):
    with ExitStack() as ctx:
        sb, sem = new(ctx)
        his = sem("his")
        block = ctx.enter_context(nc.Block())

        @block.scalar
        def _(act):
            for hf in range(NHALF):
                nc.scalar.activation(hi[:, :, half(hf)], src[:, :, half(hf)], ACT.Copy).then_inc(his, 1)

        @block.vector
        def _(dve):
            for hf in range(NHALF):
                dve.wait_ge(his, hf + 1)
                nc.vector.tensor_tensor(lo[:, :, half(hf)], src[:, :, half(hf)], hi[:, :, half(hf)].bitcast(F32), ALU.subtract)


def mixer_out_phase(nc, new, name, y_t, w_dram, addends, dst):
    n = y_t.shape[1]
    with ExitStack() as ctx:
        sb, sem = new(ctx)
        w_raw = sb("w_raw", [P, n, H])
        w_hi = sb("w_hi", [P, n, H], F32R)
        w_lo = sb("w_lo", [P, n, H], F32R)
        y_hi = sb("y_hi", [P, n, T], F32R)
        y_lo = sb("y_lo", [P, n, T], F32R)
        ps = ctx.enter_context(nc.psum_tensor(name + "_ps", [P, KH, NHALF, HALF], F32))
        loaded, w_his, y_his, w_los, y_los, made, chain = (
            sem(s) for s in ("loaded", "w_his", "y_his", "w_los", "y_los", "made", "chain"))
        block = ctx.enter_context(nc.Block())

        @block.sync
        def _(sp):
            sp.dma_start(w_raw[:], w_dram.rearrange("(k p) n -> p k n", p=P)).then_inc(loaded, 16)

        @block.scalar
        def _(act):
            for hf in range(NHALF):
                nc.scalar.activation(y_hi[:, :, half(hf)], y_t[:, :, half(hf)], ACT.Copy).then_inc(y_his, 1)
                if hf == 0:
                    act.wait_ge(loaded, 16)
                    nc.scalar.activation(w_hi[:], w_raw[:], ACT.Copy).then_inc(w_his, 1)

        @block.gpsimd
        def _(pool):
            pool.wait_ge(w_his, 1)
            nc.gpsimd.tensor_tensor(w_lo[:], w_raw[:], w_hi[:].bitcast(F32), ALU.subtract).then_inc(w_los, 1)

        @block.tensor
        def _(pe):
            pe.wait_ge(w_los, 1)
            for hf in range(NHALF):
                pe.wait_ge(y_los, hf + 1)
                for m in range(KH):
                    f = slice(m * P, (m + 1) * P)
                    for k in range(n):
                        mm = product3(nc, ps[:, m, hf], w_hi[:, k, f], w_lo[:, k, f], y_hi[:, k, half(hf)], y_lo[:, k, half(hf)],
                                      k == 0, k == n - 1)
                    mm.then_inc(made, 1)

        @block.vector
        def _(dve):
            for hf in range(NHALF):
                dve.wait_ge(y_his, hf + 1)
                nc.vector.tensor_tensor(y_lo[:, :, half(hf)], y_t[:, :, half(hf)], y_hi[:, :, half(hf)].bitcast(F32),
                                        ALU.subtract).then_inc(y_los, 1)
            done = 0
            for hf in range(NHALF):
                for m in range(KH):
                    dve.wait_ge(made, hf * KH + m + 1)
                    for i, a in enumerate(addends):
                        src = ps[:, m, hf] if i == 0 else dst[:, m, half(hf)]
                        nc.vector.tensor_tensor(dst[:, m, half(hf)], src, a[:, m, half(hf)], ALU.add).then_inc(chain, 1)
                        done += 1
                        dve.wait_ge(chain, done)
def keys_values_phase(nc, new, io, hn_hi, hn_lo, kz, v_tok):
    with ExitStack() as ctx:
        sb, sem = new(ctx)
        w_raw = sb("w_raw", [P, 2, KH, NKV * D])
        w_hi = sb("w_hi", [P, 2, KH, NKV * D], F32R)
        w_lo = sb("w_lo", [P, 2, KH, NKV * D], F32R)
        ps = ctx.enter_context(nc.psum_tensor("kv_ps", [P, 8, HALF], F32))
        loaded, w_his, w_los, made, low_took, high_took, v_took, zeroed = (
            sem(s) for s in ("loaded", "w_his", "w_los", "made", "low_took", "high_took", "v_took", "zeroed"))
        block = ctx.enter_context(nc.Block())
        nk = KT * NHALF

        @block.sync
        def _(sp):
            sp.dma_start(w_raw[:, 0], io["wk"].rearrange("(k p) n -> p k n", p=P)).then_inc(loaded, 16)
            sp.dma_start(w_raw[:, 1], io["wv"].rearrange("(k p) n -> p k n", p=P)).then_inc(loaded, 16)

        @block.gpsimd
        def _(pool):
            nc.gpsimd.memset(kz[D:P, 0], 0.0)
            nc.gpsimd.memset(kz[0:D, 1], 0.0).then_inc(zeroed, 1)

        @block.tensor
        def _(pe):
            pe.wait_ge(w_los, 1)
            for n in range(nk + TT):
                if n >= 8:
                    wait_after(pe, low_took, n - 7)
                    wait_after(pe, high_took, n - 7)
                for k in range(KH):
                    if n < nk:
                        f = slice(n // 2 * P, (n // 2 + 1) * P)
                        mm = product3(nc, ps[:, n % 8], w_hi[:, 0, k, f], w_lo[:, 0, k, f],
                                      hn_hi[:, k, half(n % 2)], hn_lo[:, k, half(n % 2)], k == 0, k == KH - 1)
                    else:
                        tok = slice((n - nk) * P, (n - nk + 1) * P)
                        mm = product3(nc, ps[:, n % 8], hn_hi[:, k, tok], hn_lo[:, k, tok],
                                      w_hi[:, 1, k], w_lo[:, 1, k], k == 0, k == KH - 1)
                mm.then_inc(made, 1)

        @block.scalar
        def _(act):
            act.wait_ge(loaded, 32)
            nc.scalar.activation(w_hi[:], w_raw[:], ACT.Copy).then_inc(w_his, 1)
            for n in range(nk):
                act.wait_ge(made, n + 1)
                nc.scalar.activation(kz[0:D, 0, n // 2, half(n % 2)], ps[0:D, n % 8], ACT.Copy).then_inc(low_took, 1)
            for t in range(0, TT, 2):
                act.wait_ge(made, nk + t + 1)
                nc.scalar.activation(v_tok[:, t, :], ps[:, (nk + t) % 8], ACT.Copy).then_inc(v_took, 1)

        @block.vector
        def _(dve):
            dve.wait_ge(w_his, 1)
            nc.vector.tensor_tensor(w_lo[:], w_raw[:], w_hi[:].bitcast(F32), ALU.subtract).then_inc(w_los, 1)
            for n in range(nk):
                dve.wait_ge(made, n + 1)
                nc.vector.tensor_copy(kz[D:P, 1, n // 2, half(n % 2)], ps[D:P, n % 8]).then_inc(high_took, 1)
            for t in range(1, TT, 2):
                dve.wait_ge(made, nk + t + 1)
                nc.vector.tensor_copy(v_tok[:, t, :], ps[:, (nk + t) % 8])


def attention_phase(nc, new, io, hn_hi, hn_lo, kz, v_tok, attn_t, ident, ident_bf, mask_bf):
    SCALE = float(D) ** -0.5
    NI, NU = 4, 16
    with ExitStack() as ctx:
        sb, sem = new(ctx)
        wq_raw, wo_raw = sb("wq_raw", [P, 2, KH, P]), sb("wo_raw", [P, 2, H])
        wq_hi, wo_hi = sb("wq_hi", [P, 2, KH, P], F32R), sb("wo_hi", [P, 2, H], F32R)
        wq_lo, wo_lo = sb("wq_lo", [P, 2, KH, P], F32R), sb("wo_lo", [P, 2, H], F32R)
        q = sb("q", [P, 2, T])
        vs = sb("vs", [P, TT, P])
        probs = sb("probs", [P, 2, 6 * P])
        pt_a = sb("pt_a", [P, 2, 2, 2 * P])
        pt_b = sb("pt_b", [P, 2, 2, P])
        mx, nb = sb("mx", [P, 2, 4]), sb("nb", [P, 2, 4])
        rs, ri = sb("rs", [P, 2, 4]), sb("ri", [P, 2, 4])
        o_t = sb("o_t", [P, 2, T])
        o_hi, o_lo = sb("o_hi", [P, 2, T], F32R), sb("o_lo", [P, 2, T], F32R)
        ps_a = ctx.enter_context(nc.psum_tensor("at_a", [P, 2, HALF], F32))
        ps_s1 = ctx.enter_context(nc.psum_tensor("at_s1", [P, 2, HALF], F32))
        ps_s0 = ctx.enter_context(nc.psum_tensor("at_s0", [P, 2, HALF], F32))
        ps_t = ctx.enter_context(nc.psum_tensor("at_t", [P, 2, HALF], F32))
        ld_q, ld_o = [sem("ld_q0"), sem("ld_q1")], [sem("ld_o0"), sem("ld_o1")]
        (wq_his, wq_los, wo_his, wo_los, q_made, q_low, q_high, v_staged, s_made, maxed, nb_made, exp_made,
         inverted, p_made, ta_made, tb_made, pta_copied, ptb_copied, o_made, o_copied, o_his, o_los, wo_made, wo_taken,
         cleared) = (
            sem(s) for s in ("wq_his", "wq_los", "wo_his", "wo_los", "q_made", "q_low", "q_high", "v_staged",
                             "s_made", "maxed", "nb_made", "exp_made", "inverted", "p_made", "ta_made", "tb_made",
                             "pta_copied", "ptb_copied", "o_made", "o_copied", "o_his", "o_los", "wo_made", "wo_taken",
                             "cleared"))
        nc.scalar.preload_act_table(ACT.Exp)
        block = ctx.enter_context(nc.Block())

        @block.sync
        def _(sp):
            def load(j, i, wait):
                if wait:
                    wait_after(sp, wq_los, j - 1)
                sp.dma_start(wq_raw[:, i % 2], io["wq_tiles"][bass.ds(j, 1)].rearrange("a p k n -> p (a k) n")).then_inc(ld_q[i % 2], 16)
                if wait:
                    wait_after(sp, wo_los, j - 1)
                sp.dma_start(wo_raw[:, i % 2], io["wo_tiles"][bass.ds(j, 1)].rearrange("a p n -> p (a n)")).then_inc(ld_o[i % 2], 16)

            for i in range(NI):
                load(i, i, i >= 2)
            with sp.Fori(1, KT) as m:
                for i in range(NI):
                    load(NI * m + i, i, True)

        @block.gpsimd
        def _(pool):
            def split_q(m, i):
                pool.wait_ge(wq_his, NI * m + i + 1)
                nc.gpsimd.tensor_tensor(wq_lo[:, i % 2], wq_raw[:, i % 2], wq_hi[:, i % 2].bitcast(F32), ALU.subtract).then_inc(wq_los, 1)

            def split_o(m, i):
                pool.wait_ge(wo_his, NI * m + i + 1)
                nc.gpsimd.tensor_tensor(wo_lo[:, i % 2], wo_raw[:, i % 2], wo_hi[:, i % 2].bitcast(F32), ALU.subtract).then_inc(wo_los, 1)

            def normalize(m, i, b):
                u = NU * m + 4 * i + b
                wait_after(pool, inverted, u + 1)
                p = probs[:, b % 2]
                p1 = p[:, 0:4 * P].rearrange("p (h k) -> p h k", h=2)
                nc.gpsimd.tensor_tensor(p1, p1, ri[:, b % 2, 0:2].unsqueeze(2).to_broadcast([P, 2, 2 * P]), ALU.mult)
                for n in (2, 3):
                    p0 = p[:, (2 + n) * P:(3 + n) * P]
                    op = nc.gpsimd.tensor_scalar(p0, p0, ri[:, b % 2, n:n + 1], None, ALU.mult)
                op.then_inc(p_made, 1)

            for m in turns(pool, KT):
                split_q(m, 0)
                wait_after(pool, o_made, NU * m)
                nc.gpsimd.tensor_copy(vs[:], v_tok[:, :, bass.ds(m * P, P)]).then_inc(v_staged, 1)
                for i in range(NI):
                    for b in range(B):
                        normalize(m, i, b)
                        if b == 0:
                            if i + 1 < NI:
                                split_q(m, i + 1)
                            split_o(m, i)

        @block.tensor
        def _(pe):
            def q_proj(m, i):
                j = NI * m + i
                pe.wait_ge(wq_los, j + 1)
                wait_after(pe, q_low, j)
                wait_after(pe, q_high, j)
                wait_after(pe, wo_taken, 4 * (NI * m + max(i - 1, 0)))
                for hf in range(NHALF):
                    for k in range(KH):
                        mm = product3(nc, ps_a[:, hf], wq_hi[:, i % 2, k], wq_lo[:, i % 2, k],
                                      hn_hi[:, k, half(hf)], hn_lo[:, k, half(hf)], k == 0, k == KH - 1)
                    mm.then_inc(q_made, 1)

            def scores(m, i, b):
                u = NU * m + 4 * i + b
                if b == 0:
                    pe.wait_ge(q_low, NI * m + i + 1)
                    pe.wait_ge(q_high, NI * m + i + 1)
                if i or b > 1:
                    wait_after(pe, exp_made, u - 1)
                else:
                    wait_after(pe, exp_made, NU * m)
                both = [P, 2, P]
                tok = b * S
                s1 = ps_s1[:, b % 2].rearrange("p (h k) -> p h k", h=2)
                s0 = ps_s0[:, b % 2, 0:2 * P].rearrange("p (h k) -> p h k", h=2)
                kzm = kz[:, :, bass.ds(m, 1), :].rearrange("p h a t -> p h (a t)")
                nc.tensor.matmul(s1, q[:, i % 2, tok + P:tok + S], kzm[:, :, tok:tok + S], start=True, stop=False)
                nc.tensor.matmul(s1[:, :, P:], ident_bf, mask_bf.unsqueeze(1).to_broadcast(both), start=False, stop=True)
                nc.tensor.matmul(s0, q[:, i % 2, tok:tok + P], kzm[:, :, tok:tok + P], start=True, stop=False)
                nc.tensor.matmul(s0, ident_bf, mask_bf.unsqueeze(1).to_broadcast(both), start=False, stop=True).then_inc(s_made, 1)

            def turn(m, i, b):
                u = NU * m + 4 * i + b
                p = probs[:, b % 2]
                pe.wait_ge(p_made, u + 1)
                wait_after(pe, pta_copied, u)
                for h in range(2):
                    nc.tensor.transpose(ps_t[:, 0, 2 * h * P:(2 * h + 1) * P], p[:, (4 + h) * P:(5 + h) * P], ident)
                    mm = nc.tensor.transpose(ps_t[:, 0, (2 * h + 1) * P:(2 * h + 2) * P], p[:, 2 * h * P:(2 * h + 1) * P], ident)
                mm.then_inc(ta_made, 1)
                wait_after(pe, o_copied, u)
                for h in range(2):
                    mm = nc.tensor.transpose(ps_t[:, 1, h * P:(h + 1) * P], p[:, (2 * h + 1) * P:(2 * h + 2) * P], ident)
                mm.then_inc(tb_made, 1)

            def heads_out(m, i, b):
                u = NU * m + 4 * i + b
                pe.wait_ge(pta_copied, u + 1)
                pe.wait_ge(ptb_copied, u + 1)
                for h in range(2):
                    rows = slice(h * D, (h + 1) * D)
                    nc.tensor.matmul(ps_t[rows, 1, 2 * P:4 * P], vs[:, 2 * b, rows], pt_a[:, b % 2, h], start=True, stop=False)
                    mm = nc.tensor.matmul(ps_t[rows, 1, 3 * P:4 * P], vs[:, 2 * b + 1, rows], pt_b[:, b % 2, h], start=False, stop=True)
                mm.then_inc(o_made, 1)

            def project(m, i):
                j = NI * m + i
                pe.wait_ge(wo_los, j + 1)
                pe.wait_ge(o_los, j + 1)
                wait_after(pe, q_low, NI * m + min(i + 2, NI))
                wait_after(pe, q_high, NI * m + min(i + 2, NI))
                for n in range(4):
                    d, hf = n // 2, n % 2
                    wait_after(pe, wo_taken, 4 * j + max(n - 1, 0))
                    f = slice(d * P, (d + 1) * P)
                    product3(nc, ps_a[:, hf], wo_hi[:, i % 2, f], wo_lo[:, i % 2, f],
                             o_hi[:, i % 2, half(hf)], o_lo[:, i % 2, half(hf)], True, True).then_inc(wo_made, 1)

            for m in turns(pe, KT):
                q_proj(m, 0)
                pe.wait_ge(v_staged, m + 1)
                scores(m, 0, 0)
                for i in range(NI):
                    for b in range(B):
                        if b == 1 and i + 1 < NI:
                            q_proj(m, i + 1)
                        if b + 1 < B:
                            scores(m, i, b + 1)
                        elif i + 1 < NI:
                            scores(m, i + 1, 0)
                        turn(m, i, b)
                        heads_out(m, i, b)
                        if b == 0 and i > 0:
                            project(m, i - 1)
                project(m, NI - 1)

        @block.scalar
        def _(act):
            def split_q(m, i):
                j = NI * m + i
                act.wait_ge(ld_q[i % 2], 16 * (NI // 2 * m + i // 2 + 1))
                if i >= 2:
                    wait_after(act, q_made, 2 * (j - 1))
                nc.scalar.activation(wq_hi[:, i % 2], wq_raw[:, i % 2], ACT.Copy).then_inc(wq_his, 1)

            def split_o(m, i):
                j = NI * m + i
                act.wait_ge(ld_o[i % 2], 16 * (NI // 2 * m + i // 2 + 1))
                if i >= 2:
                    wait_after(act, wo_made, 4 * (j - 1))
                else:
                    wait_after(act, wo_made, 4 * NI * m)
                nc.scalar.activation(wo_hi[:, i % 2], wo_raw[:, i % 2], ACT.Copy).then_inc(wo_his, 1)

            def take_q(m, i):
                j = NI * m + i
                act.wait_ge(q_made, 2 * j + 2)
                nc.scalar.activation(q[:, i % 2, half(1)], ps_a[:, 1], ACT.Copy).then_inc(q_high, 1)

            def exps(m, i, b):
                u = NU * m + 4 * i + b
                wait_after(act, nb_made, u + 1)
                parts = ((ps_s1[:, b % 2, 0:2 * P], 0, 2 * P), (ps_s1[:, b % 2, 2 * P:4 * P], 2 * P, 2 * P),
                         (ps_s0[:, b % 2, 0:P], 4 * P, P), (ps_s0[:, b % 2, P:2 * P], 5 * P, P))
                for n, (src, c, w) in enumerate(parts):
                    op = nc.scalar.activation(probs[:, b % 2, c:c + w], src, ACT.Exp, bias=nb[:, b % 2, n:n + 1], scale=SCALE,
                                              accum_out=rs[:, b % 2, n:n + 1])
                op.then_inc(exp_made, 1)

            def take_pt(m, i, b):
                u = NU * m + 4 * i + b
                act.wait_ge(ta_made, u + 1)
                nc.scalar.activation(pt_a[:, b % 2].rearrange("p h q -> p (h q)"), ps_t[:, 0], ACT.Copy).then_inc(pta_copied, 1)

            def split_out(m, i):
                act.wait_ge(o_copied, NU * m + 4 * (i + 1))
                nc.scalar.activation(o_hi[:, i % 2], o_t[:, i % 2], ACT.Copy).then_inc(o_his, 1)

            for m in turns(act, KT):
                split_q(m, 0)
                take_q(m, 0)
                exps(m, 0, 0)
                for i in range(NI):
                    for b in range(B):
                        if b == 0:
                            if i + 1 < NI:
                                split_q(m, i + 1)
                            split_o(m, i)
                        if b == 1 and i + 1 < NI:
                            take_q(m, i + 1)
                        if b + 1 < B:
                            exps(m, i, b + 1)
                        elif i + 1 < NI:
                            exps(m, i + 1, 0)
                        if b == 0 and i > 0:
                            split_out(m, i - 1)
                        take_pt(m, i, b)
                split_out(m, NI - 1)

        @block.vector
        def _(dve):
            def take_q(m, i):
                j = NI * m + i
                dve.wait_ge(q_made, 2 * j + 1)
                nc.vector.tensor_copy(q[:, i % 2, half(0)], ps_a[:, 0]).then_inc(q_low, 1)

            def maxima(m, i, b):
                u = NU * m + 4 * i + b
                dve.wait_ge(s_made, u + 1)
                nc.vector.reduce_max(mx[:, b % 2, 0:2], ps_s1[:, b % 2].rearrange("p (h k) -> p h k", h=2), axis=X)
                nc.vector.reduce_max(mx[:, b % 2, 2:4], ps_s0[:, b % 2, 0:2 * P].rearrange("p (h k) -> p h k", h=2), axis=X).then_inc(maxed, 1)
                dve.wait_ge(maxed, u + 1)
                nc.vector.tensor_scalar(nb[:, b % 2], mx[:, b % 2], -SCALE, None, ALU.mult).then_inc(nb_made, 1)

            def invert(m, i, b):
                u = NU * m + 4 * i + b
                dve.wait_ge(exp_made, u + 1)
                nc.vector.reciprocal(ri[:, b % 2], rs[:, b % 2]).then_inc(inverted, 1)

            def take_pt(m, i, b):
                u = NU * m + 4 * i + b
                dve.wait_ge(tb_made, u + 1)
                nc.vector.tensor_copy(pt_b[:, b % 2].rearrange("p h q -> p (h q)"), ps_t[:, 1, 0:2 * P]).then_inc(ptb_copied, 1)

            def take_o(m, i, b):
                u = NU * m + 4 * i + b
                dve.wait_ge(o_made, u + 1)
                nc.vector.tensor_copy(o_t[:, i % 2, b * S:(b + 1) * S], ps_t[:, 1, 2 * P:4 * P]).then_inc(o_copied, 1)

            def split_out(m, i):
                dve.wait_ge(o_his, NI * m + i + 1)
                nc.vector.tensor_tensor(o_lo[:, i % 2], o_t[:, i % 2], o_hi[:, i % 2].bitcast(F32), ALU.subtract).then_inc(o_los, 1)

            def take_projection(m, i):
                j = NI * m + i
                for n in range(4):
                    d, hf = n // 2, n % 2
                    dve.wait_ge(wo_made, 4 * j + n + 1)
                    nc.vector.tensor_tensor(attn_t[:, d, half(hf)], ps_a[:, hf], attn_t[:, d, half(hf)], ALU.add).then_inc(wo_taken, 1)

            nc.vector.memset(attn_t[:], 0.0).then_inc(cleared, 1)
            dve.wait_ge(cleared, 1)
            for m in turns(dve, KT):
                take_q(m, 0)
                maxima(m, 0, 0)
                invert(m, 0, 0)
                for i in range(NI):
                    for b in range(B):
                        last = i + 1 == NI and b + 1 == B
                        ni, nb_ = (i, b + 1) if b + 1 < B else (i + 1, 0)
                        if b == 1 and i + 1 < NI:
                            take_q(m, i + 1)
                        if not last:
                            maxima(m, ni, nb_)
                        take_pt(m, i, b)
                        if not last:
                            invert(m, ni, nb_)
                        take_o(m, i, b)
                        if b == 0 and i > 0:
                            split_out(m, i - 1)
                            take_projection(m, i - 1)
                split_out(m, NI - 1)
                take_projection(m, NI - 1)
def experts0_phase(nc, new, io, t_hi, t_lo, cw_dram, moe_t):
    NU = FT0 * NHALF
    with ExitStack() as ctx:
        sb, sem = new(ctx)
        raw = sb("raw", [P, 2, 3, H])
        w_hi, w_lo = sb("w_hi", [P, 2, 3, H], F32R), sb("w_lo", [P, 2, 3, H], F32R)
        cb = sb("cb", [P, 2, T])
        r, g = sb("r", [P, 2, HALF]), sb("g", [P, 2, HALF])
        g_hi, g_lo = sb("g_hi", [P, 2, HALF], F32R), sb("g_lo", [P, 2, HALF], F32R)
        scaled = sb("scaled", [P, KH, T])
        ps_u = ctx.enter_context(nc.psum_tensor("x0_u", [P, 2, HALF], F32))
        ps_v = ctx.enter_context(nc.psum_tensor("x0_v", [P, 2, HALF], F32))
        ps_y = ctx.enter_context(nc.psum_tensor("x0_y", [P, KH, NHALF, HALF], F32))
        ld_w, ld_c = [sem("ld_w0"), sem("ld_w1")], [sem("ld_c0"), sem("ld_c1")]
        (w_his, w_los, u_made, r_made, g_made, g_his, g_los, y_made, y_scaled, y_added, cleared) = (
            sem(s) for s in ("w_his", "w_los", "u_made", "r_made", "g_made", "g_his", "g_los", "y_made",
                             "y_scaled", "y_added", "cleared"))
        block = ctx.enter_context(nc.Block())

        @block.sync
        def _(sp):
            def load_tile(e, ft, wait):
                if wait:
                    wait_after(sp, w_los, FT0 * e + ft - 1)
                sp.dma_start(raw[:, ft % 2], io["x0_w"][bass.ds(e * FT0 + ft, 1)].rearrange("a p j n -> p (a j) n")).then_inc(ld_w[ft % 2], 16)

            def load_router(e, slot):
                sp.dma_start(cb[:, slot], cw_dram[bass.ds(e, 1)].partition_broadcast(P)).then_inc(ld_c[slot], 16)

            for p in range(2):
                load_router(p, p)
                for ft in range(FT0):
                    load_tile(p, ft, p > 0 or ft >= 2)
            with sp.Fori(1, X0 // 2) as e2:
                for p in range(2):
                    for ft in range(FT0):
                        load_tile(2 * e2 + p, ft, True)
                        if ft == 1:
                            wait_after(sp, y_scaled, 2 * e2 + p - 1)
                            load_router(2 * e2 + p, p)

        @block.gpsimd
        def _(pool):
            for e in turns(pool, X0):
                for ft in range(FT0):
                    pool.wait_ge(w_his, FT0 * e + ft + 1)
                    nc.gpsimd.tensor_tensor(w_lo[:, ft % 2], raw[:, ft % 2], w_hi[:, ft % 2].bitcast(F32),
                                            ALU.subtract).then_inc(w_los, 1)

        @block.tensor
        def _(pe):
            def up(e, ft, hf):
                n = NU * e + 2 * ft + hf
                if hf == 0:
                    pe.wait_ge(w_los, FT0 * e + ft + 1)
                wait_after(pe, g_made, n - 1 if ft else NU * e)
                for ps, j in ((ps_u, 0), (ps_v, 1)):
                    for k in range(KH):
                        f = slice(k * P, (k + 1) * P)
                        mm = product3(nc, ps[:, hf], w_hi[:, ft % 2, j, f], w_lo[:, ft % 2, j, f],
                                      t_hi[:, k, half(hf)], t_lo[:, k, half(hf)], k == 0, k == KH - 1)
                mm.then_inc(u_made, 1)

            def down(e, ft, hf):
                pe.wait_ge(g_los, NU * e + 2 * ft + hf + 1)
                if ft == 0 and hf == 0:
                    wait_after(pe, y_scaled, e)
                for d in range(KH):
                    f = slice(d * P, (d + 1) * P)
                    mm = product3(nc, ps_y[:, d, hf], w_hi[:, ft % 2, 2, f], w_lo[:, ft % 2, 2, f],
                                  g_hi[:, hf], g_lo[:, hf], ft == 0, ft == FT0 - 1)
                mm.then_inc(y_made, 1)

            for e in turns(pe, X0):
                up(e, 0, 0)
                for n in range(1, NU):
                    up(e, n // 2, n % 2)
                    down(e, (n - 1) // 2, (n - 1) % 2)
                down(e, FT0 - 1, 1)

        @block.scalar
        def _(act):
            def split(e, ft, free):
                act.wait_ge(ld_w[ft % 2], 16 * (FT0 // 2 * e + ft // 2 + 1))
                wait_after(act, y_made, free)
                nc.scalar.activation(w_hi[:, ft % 2], raw[:, ft % 2], ACT.Copy).then_inc(w_his, 1)

            for e in turns(act, X0):
                split(e, 0, NU * e)
                for ft in range(FT0):
                    for hf in range(NHALF):
                        n = NU * e + 2 * ft + hf
                        act.wait_ge(u_made, n + 1)
                        nc.scalar.activation(r[:, hf], ps_u[:, hf], ACT.Relu).then_inc(r_made, 1)
                        if hf == 0 and ft + 1 < FT0:
                            split(e, ft + 1, NU * e + 2 * ft)
                        act.wait_ge(g_made, n + 1)
                        nc.scalar.activation(g_hi[:, hf], g[:, hf], ACT.Copy).then_inc(g_his, 1)

        @block.vector
        def _(dve):
            nc.vector.memset(moe_t[:], 0.0).then_inc(cleared, 1)
            dve.wait_ge(cleared, 1)
            for e2 in turns(dve, X0 // 2):
                for p in range(2):
                    e = 2 * e2 + p
                    for ft in range(FT0):
                        for hf in range(NHALF):
                            n = NU * e + 2 * ft + hf
                            dve.wait_ge(r_made, n + 1)
                            nc.vector.tensor_tensor(g[:, hf], r[:, hf], ps_v[:, hf], ALU.mult).then_inc(g_made, 1)
                            dve.wait_ge(g_his, n + 1)
                            nc.vector.tensor_tensor(g_lo[:, hf], g[:, hf], g_hi[:, hf].bitcast(F32), ALU.subtract).then_inc(g_los, 1)
                    dve.wait_ge(ld_c[p], 16 * (e2 + 1))
                    dve.wait_ge(y_made, NU * (e + 1))
                    wait_after(dve, y_added, e)
                    for d in range(KH):
                        op = nc.vector.tensor_tensor(scaled[:, d].rearrange("p (a t) -> p a t", a=NHALF), ps_y[:, d],
                                                     cb[:, p].rearrange("p (a t) -> p a t", a=NHALF), ALU.mult)
                    op.then_inc(y_scaled, 1)
                    dve.wait_ge(y_scaled, e + 1)
                    nc.vector.tensor_tensor(moe_t[:], moe_t[:], scaled[:], ALU.add).then_inc(y_added, 1)


def experts1_phase(nc, new, io, t_hi, t_lo, cw_dram, moe_t):
    NT = 2
    NU = NT * NHALF
    with ExitStack() as ctx:
        sb, sem = new(ctx)
        raw = sb("raw", [P, 2, 3, H])
        w_hi, w_lo = sb("w_hi", [P, 2, 3, H], F32R), sb("w_lo", [P, 2, 3, H], F32R)
        cb = sb("cb", [P, 2, T])
        r, rc, g = sb("r", [P, 2, HALF]), sb("rc", [P, 2, HALF]), sb("g", [P, 2, HALF])
        g_hi, g_lo = sb("g_hi", [P, 2, HALF], F32R), sb("g_lo", [P, 2, HALF], F32R)
        ps_u = ctx.enter_context(nc.psum_tensor("x1_u", [P, 2, HALF], F32))
        ps_v = ctx.enter_context(nc.psum_tensor("x1_v", [P, 2, HALF], F32))
        ps_y = ctx.enter_context(nc.psum_tensor("x1_y", [P, KH, NHALF, HALF], F32))
        ld_w, ld_c = [sem("ld_w0"), sem("ld_w1")], [sem("ld_c0"), sem("ld_c1")]
        (w_his, w_los, u_made, r_made, rc_made, g_made, g_his, g_los, y_made, y_added, cleared) = (
            sem(s) for s in ("w_his", "w_los", "u_made", "r_made", "rc_made", "g_made", "g_his", "g_los",
                             "y_made", "y_added", "cleared"))
        nc.scalar.preload_act_table(ACT.Silu)
        block = ctx.enter_context(nc.Block())

        def segments(q):
            out, p = [], 0
            while p < P:
                e = (q * P + p) // F1
                stop = min(P, (e + 1) * F1 - q * P)
                out.append((e, p, stop))
                p = stop
            return out

        @block.sync
        def _(sp):
            for q in range(FT1):
                if q >= 2:
                    wait_after(sp, w_los, q - 1)
                sp.dma_start(raw[:, q % 2], io["x1_w"][q]).then_inc(ld_w[q % 2], 16)
                if q >= 2:
                    wait_after(sp, rc_made, 2 * (q - 1))
                parts = segments(q)
                if len(parts) == 1:
                    e = parts[0][0]
                    parts = [(e, 0, P // 2), (e, P // 2, P)]
                for e, a, z in parts:
                    sp.dma_start(cb[a:z, q % 2], cw_dram[e:e + 1].partition_broadcast(z - a)).then_inc(ld_c[q % 2], 16)

        @block.gpsimd
        def _(pool):
            for it in turns(pool, FT1 // NT):
                for j in range(NT):
                    q = NT * it + j
                    pool.wait_ge(w_his, q + 1)
                    nc.gpsimd.tensor_tensor(w_lo[:, j], raw[:, j], w_hi[:, j].bitcast(F32), ALU.subtract).then_inc(w_los, 1)
                    pool.wait_ge(ld_c[j], 32 * (it + 1))
                    for hf in range(NHALF):
                        pool.wait_ge(r_made, NU * it + 2 * j + hf + 1)
                        nc.gpsimd.tensor_tensor(rc[:, hf], r[:, hf], cb[:, j, half(hf)], ALU.mult).then_inc(rc_made, 1)

        @block.tensor
        def _(pe):
            def up(it, j, hf):
                n = NU * it + 2 * j + hf
                if hf == 0:
                    pe.wait_ge(w_los, NT * it + j + 1)
                wait_after(pe, g_made, n - 1 if j else NU * it)
                for ps, i in ((ps_u, 0), (ps_v, 1)):
                    for k in range(KH):
                        f = slice(k * P, (k + 1) * P)
                        mm = product3(nc, ps[:, hf], w_hi[:, j, i, f], w_lo[:, j, i, f],
                                      t_hi[:, k, half(hf)], t_lo[:, k, half(hf)], k == 0, k == KH - 1)
                mm.then_inc(u_made, 1)

            def down(it, j, hf):
                pe.wait_ge(g_los, NU * it + 2 * j + hf + 1)
                if j == 0 and hf == 0:
                    wait_after(pe, y_added, it)
                for d in range(KH):
                    f = slice(d * P, (d + 1) * P)
                    mm = product3(nc, ps_y[:, d, hf], w_hi[:, j, 2, f], w_lo[:, j, 2, f], g_hi[:, hf], g_lo[:, hf],
                                  j == 0, j == NT - 1)
                mm.then_inc(y_made, 1)

            for it in turns(pe, FT1 // NT):
                up(it, 0, 0)
                for n in range(1, NU):
                    up(it, n // 2, n % 2)
                    down(it, (n - 1) // 2, (n - 1) % 2)
                down(it, NT - 1, 1)

        @block.scalar
        def _(act):
            def split(it, j, free):
                act.wait_ge(ld_w[j], 16 * (it + 1))
                wait_after(act, y_made, free)
                nc.scalar.activation(w_hi[:, j], raw[:, j], ACT.Copy).then_inc(w_his, 1)

            for it in turns(act, FT1 // NT):
                split(it, 0, NU * it)
                for j in range(NT):
                    for hf in range(NHALF):
                        n = NU * it + 2 * j + hf
                        act.wait_ge(u_made, n + 1)
                        nc.scalar.activation(r[:, hf], ps_u[:, hf], ACT.Silu).then_inc(r_made, 1)
                        if hf == 0 and j + 1 < NT:
                            split(it, j + 1, NU * it)
                        act.wait_ge(g_made, n + 1)
                        nc.scalar.activation(g_hi[:, hf], g[:, hf], ACT.Copy).then_inc(g_his, 1)

        @block.vector
        def _(dve):
            nc.vector.memset(moe_t[:], 0.0).then_inc(cleared, 1)
            dve.wait_ge(cleared, 1)
            for it in turns(dve, FT1 // NT):
                for j in range(NT):
                    for hf in range(NHALF):
                        n = NU * it + 2 * j + hf
                        dve.wait_ge(rc_made, n + 1)
                        nc.vector.tensor_tensor(g[:, hf], rc[:, hf], ps_v[:, hf], ALU.mult).then_inc(g_made, 1)
                        dve.wait_ge(g_his, n + 1)
                        nc.vector.tensor_tensor(g_lo[:, hf], g[:, hf], g_hi[:, hf].bitcast(F32), ALU.subtract).then_inc(g_los, 1)
                dve.wait_ge(y_made, NU * (it + 1))
                for d in range(KH):
                    op = nc.vector.tensor_tensor(moe_t[:, d].rearrange("p (a t) -> p a t", a=NHALF), ps_y[:, d],
                                                 moe_t[:, d].rearrange("p (a t) -> p a t", a=NHALF), ALU.add)
                op.then_inc(y_added, 1)
def scan1_phase(nc, new, conv_x, bt, ct, x_tok, b_tok, dt_tok, cp_tok, da_dram, tot_dram, delta_dram, d_col, y_t, ident):
    with ExitStack() as ctx:
        sb, sem = new(ctx)
        HL = NH1 * Q1
        HQ, HG = 4, NH1 // 4
        delta = sb("delta", [P, HL])
        da = sb("da", [P, HL])
        tot = sb("tot", [P, NC1, B * NH1])
        bts, cts, bs = sb("bts", [N1, P]), sb("cts", [N1, P]), sb("bs", [P, N1])
        decay = sb("decay", [P, NH1, Q1])
        m = sb("m", [P, NH1, Q1])
        xd = sb("xd", [P, NH1, P1])
        xbd = sb("xbd", [P, NH1, B, P1])
        xdec = sb("xdec", [P, NH1, P1])
        state = sb("state", [N1, B, E1])
        through = sb("through", [P, E1])
        y_tok = sb("y_tok", [P, E1])
        ps_g = ctx.enter_context(nc.psum_tensor("s1_g", [P, HALF], F32))
        ps_y = ctx.enter_context(nc.psum_tensor("s1_y", [P, HALF], F32))
        ps_s = ctx.enter_context(nc.psum_tensor("s1_s", [P, B, HALF], F32))
        ps_o = ctx.enter_context(nc.psum_tensor("s1_o", [P, HALF], F32))
        ps_t = ctx.enter_context(nc.psum_tensor("s1_t", [P, HALF], F32))
        (tot_sent, ld_delta, ld_tot, ld_da, staged, g_made, scanned, m_made, xd_made, xbd_made, xdec_made, y_made, s_made, decayed,
         s_kept, o_made, o_scaled, y_kept, turned, y_out, cleared, state_clear) = (sem(s) for s in (
            "tot_sent", "ld_delta", "ld_tot", "ld_da", "staged", "g_made", "scanned", "m_made", "xd_made", "xbd_made", "xdec_made",
            "y_made", "s_made", "decayed", "s_kept", "o_made", "o_scaled", "y_kept", "turned", "y_out", "cleared",
            "state_clear"))
        block = ctx.enter_context(nc.Block())

        @block.sync
        def _(sp):
            def load_decays(c):
                for b in range(B):
                    sp.dma_start(da[b * Q1:(b + 1) * Q1, :],
                                 da_dram[bass.ds(c * B + b, 1)].rearrange("c h l -> c (h l)").partition_broadcast(Q1)).then_inc(ld_da, 16)

            sp.dma_start(delta[:], delta_dram).then_inc(ld_delta, 16)
            load_decays(0)
            sp.dma_start(tot_dram.rearrange("(c b) h -> b c h", b=B), cp_tok[Q1 - 1:P:Q1]).then_inc(tot_sent, 16)
            sp.wait_ge(tot_sent, 16)
            sp.dma_start(tot[:].rearrange("p c n -> p (c n)"),
                         tot_dram.rearrange("(o c) h -> o (c h)", o=1).partition_broadcast(P)).then_inc(ld_tot, 16)
            with sp.Fori(1, NC1) as c:
                wait_after(sp, scanned, c)
                load_decays(c)

        @block.gpsimd
        def _(pool):
            nc.gpsimd.memset(xbd[:], 0.0).then_inc(cleared, 1)
            nc.gpsimd.memset(state[:], 0.0).then_inc(state_clear, 1)
            for c in turns(pool, NC1):
                wait_after(pool, s_made, c)
                wait_after(pool, o_made, c)
                tok = bass.ds(c * P, P)
                nc.gpsimd.tensor_copy(bts[:], bt[:, tok])
                nc.gpsimd.tensor_copy(cts[:], ct[:, tok])
                nc.gpsimd.tensor_copy(bs[:], b_tok[:, bass.ds(c, 1), :].rearrange("p a n -> p (a n)")).then_inc(staged, 1)
                pool.wait_ge(o_made, c + 1)
                pool.wait_ge(ld_tot, 16)
                st = state[:].rearrange("n b (h q) -> n (b h) q", q=P1)
                nc.gpsimd.tensor_tensor(st, st, tot[:, bass.ds(c, 1), :].rearrange("p a n -> p (a n)").unsqueeze(2).to_broadcast([P, B * NH1, P1]),
                                        ALU.mult).then_inc(decayed, 1)

        @block.tensor
        def _(pe):
            for c in turns(pe, NC1):
                pe.wait_ge(staged, c + 1)
                for b in range(B):
                    rows = slice(b * Q1, (b + 1) * Q1)
                    mm = nc.tensor.matmul(ps_g[rows, 0:Q1], bts[:, rows], cts[:, rows], start=True, stop=True, tile_position=(0, b * Q1))
                mm.then_inc(g_made, 1)
                wait_after(pe, s_kept, c)
                pe.wait_ge(state_clear, 1)
                for b in range(B):
                    rows = slice(b * Q1, (b + 1) * Q1)
                    mm = nc.tensor.matmul(ps_o[rows, :], cts[:, rows], state[:, b], start=True, stop=True, tile_position=(0, b * Q1))
                mm.then_inc(o_made, 1)
                pe.wait_ge(xdec_made, c + 1)
                for b in range(B):
                    rows = slice(b * Q1, (b + 1) * Q1)
                    mm = nc.tensor.matmul(ps_s[:, b], bs[rows, :], xdec[rows].rearrange("p h q -> p (h q)"), start=True, stop=True,
                                          tile_position=(b * Q1, 0))
                mm.then_inc(s_made, 1)
                pe.wait_ge(m_made, c + 1)
                pe.wait_ge(xbd_made, c + 1)
                for h in range(NH1):
                    hq, hg = h // HG, h % HG
                    mm = nc.tensor.matmul(ps_y[hq * Q1:(hq + 1) * Q1, hg * Q1:(hg + 1) * Q1], m[:, h],
                                          xbd[:, h].rearrange("p b q -> p (b q)"), start=True, stop=True, tile_position=(0, hq * Q1))
                mm.then_inc(y_made, 1)
                pe.wait_ge(y_kept, c + 1)
                for t in range(NE1):
                    mm = nc.tensor.transpose(ps_t[:, t * P:(t + 1) * P], y_tok[:, t * P:(t + 1) * P], ident)
                mm.then_inc(turned, 1)

        @block.scalar
        def _(act):
            act.wait_ge(cleared, 1)
            for c in turns(act, NC1):
                act.wait_ge(xd_made, c + 1)
                for b in range(B):
                    rows = slice(b * Q1, (b + 1) * Q1)
                    op = nc.scalar.activation(xbd[rows, :, b], xd[rows], ACT.Copy)
                op.then_inc(xbd_made, 1)

        @block.vector
        def _(dve):
            dve.wait_ge(ld_delta, 16)
            for c in turns(dve, NC1):
                dve.wait_ge(ld_da, 64 * (c + 1))
                nc.vector.tensor_tensor_scan(decay[:].rearrange("p h l -> p (h l)"), da[:], delta[:], 0.0,
                                             ALU.mult, ALU.add).then_inc(scanned, 1)
                nc.vector.tensor_tensor(xd[:], x_tok[:, bass.ds(c, 1), :].rearrange("p a (h q) -> p (a h) q", q=P1),
                                        dt_tok[:, bass.ds(c, 1), :].rearrange("p a h -> p (a h)").unsqueeze(2).to_broadcast([P, NH1, P1]),
                                        ALU.mult).then_inc(xd_made, 1)
                dve.wait_ge(xd_made, c + 1)
                dve.wait_ge(scanned, c + 1)
                nc.vector.tensor_tensor(xdec[:], xd[:], decay[:, :, Q1 - 1:Q1].to_broadcast([P, NH1, P1]),
                                        ALU.mult).then_inc(xdec_made, 1)
                dve.wait_ge(g_made, c + 1)
                nc.vector.tensor_tensor(m[:], decay[:], ps_g[:, 0:Q1].unsqueeze(1).to_broadcast([P, NH1, Q1]),
                                        ALU.mult).then_inc(m_made, 1)
                dve.wait_ge(o_made, c + 1)
                nc.vector.tensor_tensor(through[:].rearrange("p (h q) -> p h q", q=P1), ps_o[:].rearrange("p (h q) -> p h q", q=P1),
                                        cp_tok[:, bass.ds(c, 1), :].rearrange("p a h -> p (a h)").unsqueeze(2).to_broadcast([P, NH1, P1]),
                                        ALU.mult).then_inc(o_scaled, 1)
                dve.wait_ge(s_made, c + 1)
                dve.wait_ge(decayed, c + 1)
                for b in range(B):
                    op = nc.vector.tensor_tensor(state[:, b], ps_s[:, b], state[:, b], ALU.add)
                op.then_inc(s_kept, 1)
                dve.wait_ge(o_scaled, c + 1)
                dve.wait_ge(y_made, c + 1)
                for hq in range(HQ):
                    for b in range(B):
                        rows, cols = slice(b * Q1, (b + 1) * Q1), slice(hq * P, (hq + 1) * P)
                        src = ps_y[hq * Q1:(hq + 1) * Q1, :].rearrange("l (g b q) -> l g b q", b=B, q=P1)[:, :, b]
                        op = nc.vector.tensor_tensor(y_tok[rows, cols].rearrange("l (g q) -> l g q", q=P1), src,
                                                     through[rows, cols].rearrange("l (g q) -> l g q", q=P1), ALU.add)
                op.then_inc(y_kept, 1)
                dve.wait_ge(turned, c + 1)
                tok = bass.ds(c * P, P)
                for t in range(NE1):
                    nat = y_t[:, t, :].rearrange("p (b c l) -> p b c l", b=B, l=Q1)[:, :, bass.ds(c, 1), :].rearrange("p b a l -> p b (a l)")
                    op = nc.vector.scalar_tensor_tensor(out=nat, in0=conv_x[t][:, tok].rearrange("p (b l) -> p b l", b=B),
                                                        scalar=d_col[:, t:t + 1],
                                                        in1=ps_t[:, t * P:(t + 1) * P].rearrange("p (b l) -> p b l", b=B),
                                                        op0=ALU.mult, op1=ALU.add)
                op.then_inc(y_out, 1)
def gate_phase(nc, y_t, gate_s, n):
    with nc.Block() as block:
        @block.vector
        def _(dve):
            for t in range(n // 2):
                nc.vector.tensor_tensor(y_t[:, t], y_t[:, t], gate_s[:, t], ALU.mult)

        @block.gpsimd
        def _(pool):
            for t in range(n // 2, n):
                nc.gpsimd.tensor_tensor(y_t[:, t], y_t[:, t], gate_s[:, t], ALU.mult)


def program(nc, io, out):
    count = [0]

    def new(ctx):
        count[0] += 1
        n = count[0]

        def sb(name, shape, dt=F32):
            return ctx.enter_context(nc.sbuf_tensor(f"t{n}_{name}", shape, dt))

        mine = []

        def sem(name):
            mine.append(nc.alloc_semaphore(f"s{n}_{name}"))
            return mine[-1]

        def clear():
            if mine:
                nc.clear_and_free_semaphores(mine)
                nc.all_engine_barrier()

        ctx.callback(clear)

        return sb, sem

    with ExitStack() as whole:
        sb, sem = new(whole)
        da0_dram = nc.dram_tensor("da0_scratch", [B * S // Q0, NH0, Q0], F32).ap()
        da1_dram = nc.dram_tensor("da1_scratch", [NC1 * B, NH1, Q1], F32).ap()
        tot1_dram = nc.dram_tensor("tot1_scratch", [NC1 * B, NH1], F32).ap()
        cw0_dram = nc.dram_tensor("cw0_scratch", [X0, T], F32).ap()
        cw1_dram = nc.dram_tensor("cw1_scratch", [X1, T], F32).ap()
        x_t = sb("x", [P, KH, T])
        xn = sb("xn", [P, KH, T])
        xn_hi, xn_lo = sb("xn_hi", [P, KH, T], F32R), sb("xn_lo", [P, KH, T], F32R)
        ones, ident = sb("ones", [P, P]), sb("ident", [P, P])
        ident_bf, mask_bf = sb("ident_bf", [P, P], BF16), sb("mask_bf", [P, P], BF16)
        mask_f = sb("mask_f", [P, P])
        eps = sb("eps", [P, 2])
        ln1_w, ln2_w = sb("ln1_w", [P, KH]), sb("ln2_w", [P, KH])
        gw0, gw1 = sb("gw0", [P, KH, X0]), sb("gw1", [P, KH, X1])
        lower0, lower1 = sb("lower0", [P, X0, X0]), sb("lower1", [P, X1, X1])
        conv0_b, dt0, d0 = sb("conv0_b", [P, 6]), sb("dt0", [P, 2]), sb("d0", [P, NE0])
        conv1_b, dt1, d1 = sb("conv1_b", [P, 6]), sb("dt1", [P, 2]), sb("d1", [P, NE1])
        norm0_w, norm1_w = sb("norm0_w", [P, NE0]), sb("norm1_w", [P, NE1])
        ld, ready, made_bf = sem("ld"), sem("ready"), sem("made_bf")

        with nc.Block() as block:
            small = [(ident, "ident"), (mask_f, "mask"), (eps, "eps"), (ln1_w, "ln1_w"), (ln2_w, "ln2_w"), (gw0, "gw0"),
                     (gw1, "gw1"), (lower0, "lower0"), (lower1, "lower1"), (conv0_b, "conv0_b"), (dt0, "dt0"), (d0, "d0"),
                     (conv1_b, "conv1_b"), (dt1, "dt1"), (d1, "d1"), (norm0_w, "norm0_w"), (norm1_w, "norm1_w")]

            @block.sync
            def _(sp):
                sp.dma_start(x_t[:], io["x"]).then_inc(ld, 16)
                for tile, name in small[0::2]:
                    sp.dma_start(tile[:], io[name]).then_inc(ready, 16)

            @block.scalar
            def _(act):
                for tile, name in small[1::2]:
                    act.dma_start(tile[:], io[name]).then_inc(ready, 16)

            @block.vector
            def _(dve):
                nc.vector.memset(ones[:], 1.0)
                dve.wait_ge(ready, 16 * len(small))
                nc.vector.tensor_copy(ident_bf[:], ident[:])
                nc.vector.tensor_copy(mask_bf[:], mask_f[:])

            @block.gpsimd
            def _(pool):
                pool.wait_ge(ld, 16)

        ones_, ident_ = ones[:], ident[:]
        norm_phase(nc, new, "n0", x_t, xn, ones_, eps[:, 0:1], True, hi=xn_hi, lo=xn_lo)
        with ExitStack() as layer:
            sbl, _ = new(layer)
            gate_s = sbl("gate_s", [P, NE0, T])
            y_t = sbl("y_t", [P, NE0, T])
            with ExitStack() as mix:
                sbm, _ = new(mix)
                cx = sbm("conv_x", [P, NE0, T])
                conv_x = [cx[:, i] for i in range(NE0)]
                bt, ct = sbm("bt", [N0, T])[:], sbm("ct", [N0, T])[:]
                DT = slice(N0, N0 + NH0)
                dt, cp = sbm("dt", [P, T])[DT, :], sbm("cp", [P, T])[DT, :]
                x_tok, b_tok = sbm("x_tok", [P, TT, E0]), sbm("b_tok", [P, TT, N0])
                dt_tok, cp_tok = sbm("dt_tok", [P, TT, NH0]), sbm("cp_tok", [P, TT, NH0])
                tiles = ([("conv", 8 * P, N0, 4), ("conv", 8 * P + N0, N0 + NH0, 5)] + [("conv", (4 + i) * P, P, i) for i in range(4)]
                         + [("gate", i * P, P, i) for i in range(4)])
                mixer_project(nc, new, "m0", io["in0_w"], io["conv0_w"], xn_hi, xn_lo, conv_x + [bt, ct], gate_s, dt, cp,
                              (5, DT, None), tiles, (1.0, 1.0), dt0, conv0_b, da0_dram, Q0, lambda ap: ap.rearrange("p (b s) -> p b s", b=B))
                turn_phase(nc, new, "t0", conv_x, bt, dt, cp, DT, x_tok, b_tok, dt_tok, cp_tok, ident_)
                scan0_phase(nc, new, conv_x, bt, ct, x_tok, b_tok, dt_tok, cp_tok, da0_dram, io["delta0"], d0, gate_s, y_t, ident_)
            gate_phase(nc, y_t, gate_s, NE0)
            norm_phase(nc, new, "g0", y_t, y_t, ones_, eps[:, 1:2], False, weight=norm0_w)
            mixer_out_phase(nc, new, "o0", y_t, io["out0_w"], [x_t], x_t)
        with ExitStack() as layer:
            sbl, _ = new(layer)
            attn_t = sbl("attn_t", [P, KH, T])
            with ExitStack() as att:
                sba, _ = new(att)
                hn = sba("hn", [P, KH, T])
                hn_hi, hn_lo = sba("hn_hi", [P, KH, T], F32R), sba("hn_lo", [P, KH, T], F32R)
                kz, v_tok = sba("kz", [P, 2, KT, T]), sba("v_tok", [P, TT, NKV * D])
                norm_phase(nc, new, "n1", xn, hn, ones_, eps[:, 0:1], False, weight=ln1_w, hi=hn_hi, lo=hn_lo)
                keys_values_phase(nc, new, io, hn_hi, hn_lo, kz, v_tok)
                attention_phase(nc, new, io, hn_hi, hn_lo, kz, v_tok, attn_t, ident_, ident_bf[:], mask_bf[:])
            add_phase(nc, new, attn_t, attn_t, xn)
            norm_phase(nc, new, "n2", attn_t, xn, ones_, eps[:, 0:1], False, weight=ln2_w, hi=xn_hi, lo=xn_lo)
            router_phase(nc, new, "r0", xn, gw0, lower0[:], cw0_dram, ident_, X0, TOP0, True)
            moe_t = sbl("moe_t", [P, KH, T])
            experts0_phase(nc, new, io, xn_hi, xn_lo, cw0_dram, moe_t)
            add_phase(nc, new, x_t, x_t, attn_t)
            add_phase(nc, new, x_t, x_t, moe_t)
        norm_phase(nc, new, "n3", x_t, xn, ones_, eps[:, 0:1], True, hi=xn_hi, lo=xn_lo)
        with ExitStack() as layer:
            sbl, _ = new(layer)
            gate_s = sbl("gate_s", [P, NE1, T])
            y_t = sbl("y_t", [P, NE1, T])
            with ExitStack() as mix:
                sbm, _ = new(mix)
                cx = sbm("conv_x", [P, NE1, T])
                conv_x = [cx[:, i] for i in range(NE1)]
                bt, ct = sbm("bt", [N1, T])[:], sbm("ct", [N1, T])[:]
                DT = slice(0, NH1)
                dt, cp = sbm("dt", [P, T])[DT, :], sbm("cp", [P, T])[DT, :]
                x_tok, b_tok = sbm("x_tok", [P, TT, E1]), sbm("b_tok", [P, TT, N1])
                dt_tok, cp_tok = sbm("dt_tok", [P, TT, NH1]), sbm("cp_tok", [P, TT, NH1])
                tiles = ([("conv", 10 * P, NH1, -1)] + [("conv", (4 + i) * P, P, i) for i in range(6)]
                         + [("gate", i * P, P, i) for i in range(4)])
                by_chunk = lambda ap: ap.rearrange("p (c b l) -> p b c l", b=B, l=Q1)
                mixer_project(nc, new, "m1", io["in1_w"], io["conv1_w"], xn_hi, xn_lo, conv_x + [bt, ct], gate_s, dt, cp,
                              (-1, DT, lambda ap, hf: by_chunk(ap)[:, 2 * hf:2 * hf + 2]), tiles, (0.25, 0.5), dt1, conv1_b,
                              da1_dram, Q1, by_chunk)
                turn_phase(nc, new, "t1", conv_x, bt, dt, cp, DT, x_tok, b_tok, dt_tok, cp_tok, ident_)
                scan1_phase(nc, new, conv_x, bt, ct, x_tok, b_tok, dt_tok, cp_tok, da1_dram, tot1_dram, io["delta1"], d1, y_t, ident_)
            norm_phase(nc, new, "g1", y_t, y_t, ones_, eps[:, 0:1], False, weight=norm1_w)
            gate_phase(nc, y_t, gate_s, NE1)
            mixer_out_phase(nc, new, "o1", y_t, io["out1_w"], [x_t], x_t)
        with ExitStack() as layer:
            sbl, _ = new(layer)
            router_phase(nc, new, "r1", xn, gw1, lower1[:], cw1_dram, ident_, X1, TOP1, False)
            moe_t = sbl("moe_t", [P, KH, T])
            experts1_phase(nc, new, io, xn_hi, xn_lo, cw1_dram, moe_t)
            add_phase(nc, new, x_t, x_t, moe_t)
        stored = sem("stored")
        with nc.Block() as block:
            @block.sync
            def _(sp):
                sp.dma_start(out, x_t[:]).then_inc(stored, 16)
                sp.wait_ge(stored, 16)


def add_phase(nc, new, dst, a, b):
    with nc.Block() as block:
        @block.vector
        def _(dve):
            nc.vector.tensor_tensor(dst[:], a[:], b[:], ALU.add)


def layout(inputs):
    f32 = np.float32
    g = {k: np.asarray(v) for k, v in inputs.items()}

    def col(v, n):
        return np.ascontiguousarray(v.reshape(n, P).T)

    def kpn(w):
        return np.ascontiguousarray(w.reshape(KH, P, -1).transpose(1, 0, 2))

    a = {}
    a["x"] = np.ascontiguousarray(g["L0_attn_x"].reshape(T, KH, P).transpose(2, 1, 0))
    a["in0_w"] = np.ascontiguousarray(g["L0_attn_in_proj_w"].T)
    a["in1_w"] = np.ascontiguousarray(g["L1_attn_in_proj_w"])
    a["out0_w"] = np.ascontiguousarray(g["L0_attn_out_proj_w"].T)
    a["out1_w"] = np.ascontiguousarray(g["L1_attn_out_proj_w"])
    a["wk"], a["wv"] = np.ascontiguousarray(g["L0_ffn_wk"]), np.ascontiguousarray(g["L0_ffn_wv"])
    for n, (w, b, N) in enumerate(((g["L0_attn_conv_w"], g["L0_attn_conv_b"], N0), (g["L1_attn_conv_w"], g["L1_attn_conv_b"], N1))):
        cw, cb = np.zeros((P, 6, KCONV), f32), np.zeros((P, 6), f32)
        for i in range(4):
            cw[:, i], cb[:, i] = w[i * P:(i + 1) * P], b[i * P:(i + 1) * P]
        for i in range(2):
            cw[0:N, 4 + i], cb[0:N, 4 + i] = w[512 + i * N:512 + (i + 1) * N], b[512 + i * N:512 + (i + 1) * N]
        a[f"conv{n}_w"], a[f"conv{n}_b"] = cw, cb
    dt0, dt1 = np.zeros((P, 2), f32), np.zeros((P, 2), f32)
    dt0[N0:N0 + NH0, 0], dt0[N0:N0 + NH0, 1] = g["L0_attn_dt_bias"], g["L0_attn_A_log"]
    dt1[0:NH1, 0], dt1[0:NH1, 1] = g["L1_attn_dt_bias"], g["L1_attn_A_log"]
    a["dt0"], a["dt1"] = dt0, dt1
    a["d0"] = col(np.repeat(g["L0_attn_D"], P0), NE0)
    a["d1"] = col(np.repeat(g["L1_attn_D"], P1), NE1)
    a["norm0_w"], a["norm1_w"] = col(g["L0_attn_norm_w"], NE0), col(g["L1_attn_norm_w"], NE1)
    a["ln1_w"], a["ln2_w"] = col(g["L0_ffn_ln1_w"], KH), col(g["L0_ffn_ln2_w"], KH)
    a["gw0"], a["gw1"] = kpn(g["L0_ffn_gate_w"]), kpn(np.ascontiguousarray(g["L1_ffn_gate_w"].T))
    order = [(2 * m + r) * (NHQ // NKV) + i for m in range(KT) for i in range(4) for r in range(2)]
    wq = g["L0_ffn_wq"].reshape(KH, P, NHQ, D)[:, :, order].reshape(KH, P, QT, P)
    a["wq_tiles"] = np.ascontiguousarray(wq.transpose(2, 1, 0, 3))
    a["wo_tiles"] = np.ascontiguousarray(g["L0_ffn_wo"].reshape(NHQ, D, H)[order].reshape(QT, P, H))
    w1 = g["L0_ffn_w1"].reshape(X0, KH, P, FT0, P).transpose(0, 3, 2, 1, 4).reshape(X0 * FT0, P, H)
    w3 = g["L0_ffn_w3"].reshape(X0, KH, P, FT0, P).transpose(0, 3, 2, 1, 4).reshape(X0 * FT0, P, H)
    w2 = g["L0_ffn_w2"].reshape(X0 * FT0, P, H)
    a["x0_w"] = np.ascontiguousarray(np.stack([w1, w3, w2], axis=2))
    wg = g["L1_ffn_w_gate"].reshape(FT1, P, KH, P).transpose(0, 3, 2, 1).reshape(FT1, P, H)
    wu = g["L1_ffn_w_up"].reshape(FT1, P, KH, P).transpose(0, 3, 2, 1).reshape(FT1, P, H)
    wd = g["L1_ffn_w_down"].transpose(0, 2, 1).reshape(FT1, P, H)
    a["x1_w"] = np.ascontiguousarray(np.stack([wg, wu, wd], axis=2))
    a["ident"] = np.eye(P, dtype=f32)
    a["mask"] = np.where(np.arange(P)[None, :] > np.arange(P)[:, None], f32(NEG_MASK), f32(0)).astype(f32)
    a["eps"] = np.tile(np.array([[1e-5, 1e-6]], f32), (P, 1))
    a["lower0"] = np.tile(np.tril(np.ones((X0, X0), f32), -1)[None], (P, 1, 1))
    a["lower1"] = np.tile(np.tril(np.ones((X1, X1), f32), -1)[None], (P, 1, 1))
    a["delta0"] = np.tile(np.eye(Q0, dtype=f32), (1, NH0))
    a["delta1"] = np.tile(np.eye(Q1, dtype=f32), (B, NH1))
    return a


def build(nc, arrays):
    io = {k: nc.dram_tensor(f"in_{k}", v.shape, mybir.dt.from_np(v.dtype), kind="ExternalInput").ap() for k, v in arrays.items()}
    out = nc.dram_tensor("out_x", (P, KH, T), F32, kind="ExternalOutput").ap()
    program(nc, io, out)


def kernel(**inputs):
    import concourse.bacc as bacc
    from concourse.bass_utils import run_bass_kernel_spmd

    arrays = layout(inputs)
    nc = bacc.Bacc("TRN2", target_bir_lowering=False, num_devices=1)
    build(nc, arrays)
    r = run_bass_kernel_spmd(nc, [{f"in_{k}": v for k, v in arrays.items()}], core_ids=[0])
    y = r.results[0]["out_x"]
    return np.ascontiguousarray(y.transpose(2, 1, 0)).reshape(B, S, H)
```

```python
from contextlib import ExitStack

import numpy as np
import concourse.bass as bass
from concourse import mybir
from concourse.alu_op_type import AluOpType as ALU

F32 = mybir.dt.float32
F32R = mybir.dt.float32r
BF16 = mybir.dt.bfloat16
ACT = mybir.ActivationFunctionType
X = mybir.AxisListType.X

P = 128
B, S, H = 4, 256, 256
T = B * S
KH = H // P
HALF = 512
NHALF = T // HALF
TT = T // P

E0, N0, NH0, P0, Q0 = 512, 64, 8, 64, 128
NE0 = E0 // P
PROJ0 = 2 * E0 + 2 * N0 + NH0
KCONV = 4
NHQ, NKV, D = 32, 8, 64
QT = NHQ * D // P
KT = NKV * D // P
X0, F0, TOP0 = 8, 1024, 2
FT0 = F0 // P
E1, N1, NH1, P1, Q1 = 512, 128, 64, 8, 32
NE1 = E1 // P
NC1 = S // Q1
PROJ1 = 2 * E1 + 2 * N1 + NH1
X1, F1, TOP1 = 16, 176, 6
FT1 = X1 * F1 // P
NEG_MASK = -3.0e38


def half(hf):
    return slice(hf * HALF, (hf + 1) * HALF)


def turns(eng, n):
    yield 0, True, False
    with eng.Fori(1, n - 1) as i:
        yield i, False, False
    yield n - 1, False, True


def wait_after(eng, sem, n):
    if not (isinstance(n, int) and n <= 0):
        eng.wait_ge(sem, n)


def product3(nc, out, w_hi, w_lo, x_hi, x_lo, start, stop):
    nc.tensor.matmul(out, w_hi, x_hi, start=start, stop=False)
    nc.tensor.matmul(out, w_hi, x_lo, start=False, stop=False)
    return nc.tensor.matmul(out, w_lo, x_hi, start=False, stop=stop)
def norm_phase(nc, new, name, src, dst, ones, eps, centred, weight=None, hi=None, lo=None, ready=None):
    n = src.shape[1]
    width = n * P
    with ExitStack() as ctx:
        sb, sem = new(ctx)
        xc = sb("xc", [P, n, T]) if centred else src
        sq = sb("sq", [P, n, T])
        std = sb("std", [P, T])
        rstd = sb("rstd", [P, T])
        ps_mean = ctx.enter_context(nc.psum_tensor(name + "_ps_mean", [P, NHALF, HALF], F32))
        ps_sq = ctx.enter_context(nc.psum_tensor(name + "_ps_sq", [P, NHALF, HALF], F32))
        sums, centre, squared, sq_sums, stds, rstds, normed, his, los = (
            sem(s) for s in ("sums", "centre", "squared", "sq_sums", "stds", "rstds", "normed", "his", "los"))
        block = ctx.enter_context(nc.Block())

        @block.tensor
        def _(pe):
            if ready is not None:
                pe.wait_ge(*ready)
            if centred:
                for hf in range(NHALF):
                    for k in range(n):
                        mm = nc.tensor.matmul(ps_mean[:, hf], ones, src[:, k, half(hf)], start=k == 0, stop=k == n - 1)
                    mm.then_inc(sums, 1)
            for hf in range(NHALF):
                pe.wait_ge(squared, hf + 1)
                for k in range(n):
                    mm = nc.tensor.matmul(ps_sq[:, hf], ones, sq[:, k, half(hf)], start=k == 0, stop=k == n - 1)
                mm.then_inc(sq_sums, 1)

        @block.scalar
        def _(act):
            if ready is not None:
                act.wait_ge(*ready)
            for hf in range(NHALF):
                if centred:
                    act.wait_ge(centre, hf + 1)
                nc.scalar.activation(sq[:, :, half(hf)], xc[:, :, half(hf)], ACT.Square).then_inc(squared, 1)
            for hf in range(NHALF):
                act.wait_ge(sq_sums, hf + 1)
                nc.scalar.activation(std[:, half(hf)], ps_sq[:, hf], ACT.Sqrt, bias=eps, scale=1.0 / width).then_inc(stds, 1)
            if hi is not None:
                for hf in range(NHALF):
                    act.wait_ge(normed, hf + 1)
                    nc.scalar.activation(hi[:, :, half(hf)], dst[:, :, half(hf)], ACT.Copy).then_inc(his, 1)

        @block.vector
        def _(dve):
            if ready is not None:
                dve.wait_ge(*ready)
            if centred:
                for hf in range(NHALF):
                    dve.wait_ge(sums, hf + 1)
                    for k in range(n):
                        op = nc.vector.scalar_tensor_tensor(out=xc[:, k, half(hf)], in0=ps_mean[:, hf], scalar=-1.0 / width,
                                                            in1=src[:, k, half(hf)], op0=ALU.mult, op1=ALU.add)
                    op.then_inc(centre, 1)
                dve.wait_ge(centre, NHALF)
            for hf in range(NHALF):
                dve.wait_ge(stds, hf + 1)
                nc.vector.reciprocal(rstd[:, half(hf)], std[:, half(hf)]).then_inc(rstds, 1)
                dve.wait_ge(rstds, hf + 1)
                for k in range(n):
                    if weight is None:
                        op = nc.vector.tensor_tensor(dst[:, k, half(hf)], xc[:, k, half(hf)], rstd[:, half(hf)], ALU.mult)
                    else:
                        op = nc.vector.scalar_tensor_tensor(out=dst[:, k, half(hf)], in0=xc[:, k, half(hf)],
                                                            scalar=weight[:, k:k + 1], in1=rstd[:, half(hf)],
                                                            op0=ALU.mult, op1=ALU.mult)
                op.then_inc(normed, 1)
            if hi is not None:
                for hf in range(NHALF):
                    dve.wait_ge(his, hf + 1)
                    nc.vector.tensor_tensor(lo[:, :, half(hf)], dst[:, :, half(hf)], hi[:, :, half(hf)].bitcast(F32),
                                            ALU.subtract).then_inc(los, 1)
def softplus_step(nc, dve, act_side, x, a, e, u, ln, dt, sems):
    chain, magnitude, exped, summed, logged, ready = sems
    if act_side:
        dve.wait_ge(magnitude, 1)
        nc.scalar.activation(e, a, ACT.Exp, scale=-1.0).then_inc(exped, 1)
        dve.wait_ge(summed, 1)
        nc.scalar.activation(ln, u, ACT.Ln).then_inc(logged, 1)
        return
    nc.vector.tensor_scalar(a, x, -1.0, None, ALU.mult).then_inc(chain, 1)
    dve.wait_ge(chain, 1)
    nc.vector.tensor_tensor(a, a, x, ALU.max).then_inc(magnitude, 1)
    dve.wait_ge(exped, 1)
    nc.vector.tensor_scalar(u, e, 1.0, None, ALU.add).then_inc(summed, 1)
    dve.wait_ge(logged, 1)
    nc.vector.scalar_tensor_tensor(out=u, in0=u, scalar=-1.0, in1=e, op0=ALU.add, op1=ALU.subtract).then_inc(chain, 1)
    dve.wait_ge(chain, 2)
    nc.vector.tensor_tensor(ln, ln, u, ALU.subtract).then_inc(chain, 1)
    dve.wait_ge(chain, 3)
    nc.vector.scalar_tensor_tensor(out=dt, in0=x, scalar=0.0, in1=ln, op0=ALU.max, op1=ALU.add).then_inc(ready, 1)


def causal_taps(nc, dve, acc, padded, taps_w, bias, taps, done):
    nc.vector.tensor_scalar(acc, padded[:, :, 0:S], taps_w[:, 0:1], bias, ALU.mult, ALU.add).then_inc(taps, 1)
    for k in range(1, KCONV):
        dve.wait_ge(taps, done + k)
        nc.vector.scalar_tensor_tensor(out=acc, in0=padded[:, :, k:k + S], scalar=taps_w[:, k:k + 1], in1=acc,
                                       op0=ALU.mult, op1=ALU.add).then_inc(taps, 1)


def mixer_project(nc, new, name, w_dram, cw_dram, xn_hi, xn_lo, conv_outs, gate_s, dt, cp, dt_rows, tiles, mup, dcol, bias_col, da_dram,
                  Q, store):
    dt_tile, DT, dt_alone = dt_rows
    nproj = w_dram.shape[1]
    nconv = len(conv_outs)
    with ExitStack() as ctx:
        sb, sem = new(ctx)
        w_raw = sb("w_raw", [P, KH, nproj])
        w_hi = sb("w_hi", [P, KH, nproj], F32R)
        w_lo = sb("w_lo", [P, KH, nproj], F32R)
        padded = sb("padded", [P, nconv, B, KCONV - 1 + S])
        acc = sb("acc", [P, 2, B, S])
        cw = sb("cw", [P, nconv, KCONV])
        dt_x, dt_a, dt_e, dt_u, dt_l = (sb(s, [P, T])[DT, :] for s in ("dt_x", "dt_a", "dt_e", "dt_u", "dt_l"))
        decay, decay0, decay_s = dt_a, dt_e, dt_u
        acol = sb("acol", [P, 3])
        ps = ctx.enter_context(nc.psum_tensor(name + "_ps", [P, 8, HALF], F32))
        (loaded, w_his, w_los, projected, act_took, dve_took, pads, taps, silued, chain, magnitude, exped, summed,
         logged, dt_ready, a_capped, a_exp, a_ready, exponents, decays, copied, zeroed, starts, cps, sent) = (sem(s) for s in (
            "loaded", "w_his", "w_los", "projected", "act_took", "dve_took", "pads", "taps", "silued", "chain", "magnitude",
            "exped", "summed", "logged", "dt_ready", "a_capped", "a_exp", "a_ready", "exponents", "decays", "copied", "zeroed", "starts", "cps", "sent"))
        block = ctx.enter_context(nc.Block())
        blocks = [(kind, c0, m, i, hf) for kind, c0, m, i in tiles for hf in range(NHALF)]
        on_dve = [kind == "conv" for kind, *_ in blocks]
        nth = [sum(1 for j in range(n + 1) if on_dve[j] == on_dve[n]) for n in range(len(blocks))]
        n_dve = sum(on_dve)

        @block.sync
        def _(sp):
            sp.dma_start(w_raw[:], w_dram.rearrange("(k p) n -> p k n", p=P)).then_inc(loaded, 16)
            sp.dma_start(cw[:], cw_dram).then_inc(loaded, 16)
            sp.wait_ge(zeroed, 1)
            sp.dma_start(da_dram.rearrange("c h l -> h c l"), decay0.rearrange("h (c l) -> h c l", l=Q)).then_inc(sent, 16)
            sp.wait_ge(sent, 16)

        @block.gpsimd
        def _(pool):
            nc.gpsimd.memset(padded[:, :, :, 0:KCONV - 1], 0.0).then_inc(pads, 1)
            pool.wait_ge(w_his, 1)
            nc.gpsimd.tensor_tensor(w_lo[:], w_raw[:], w_hi[:].bitcast(F32), ALU.subtract).then_inc(w_los, 1)

        @block.tensor
        def _(pe):
            pe.wait_ge(w_los, 1)
            for n, (kind, c0, m, i, hf) in enumerate(blocks):
                f = slice(c0, c0 + m)
                if n >= 8:
                    pe.wait_ge(dve_took if on_dve[n - 8] else act_took, nth[n - 8])
                for k in range(KH):
                    mm = product3(nc, ps[0:m, n % 8], w_hi[:, k, f], w_lo[:, k, f],
                                  xn_hi[:, k, half(hf)], xn_lo[:, k, half(hf)], k == 0, k == KH - 1)
                mm.then_inc(projected, 1)

        @block.scalar
        def _(act):
            act.wait_ge(loaded, 32)
            nc.scalar.activation(w_hi[:], w_raw[:], ACT.Copy).then_inc(w_his, 1)
            for n, (kind, c0, m, i, hf) in enumerate(blocks):
                if not on_dve[n]:
                    act.wait_ge(projected, n + 1)
                    nc.scalar.activation(gate_s[:, i, half(hf)], ps[:, n % 8], ACT.Silu, scale=mup[0]).then_inc(act_took, 1)
            softplus_step(nc, act, True, dt_x, dt_a, dt_e, dt_u, dt_l, dt, (chain, magnitude, exped, summed, logged, dt_ready))
            act.wait_ge(a_capped, 1)
            nc.scalar.activation(acol[DT, 1:2], acol[DT, 0:1], ACT.Exp).then_inc(a_exp, 1)
            act.wait_ge(exponents, 1)
            nc.scalar.activation(decay, decay, ACT.Exp).then_inc(decays, 1)
            for i, out in enumerate(conv_outs):
                m = out.shape[0]
                act.wait_ge(taps, KCONV * (i + 1))
                nc.scalar.activation(store(out), acc[0:m, i % 2], ACT.Silu).then_inc(silued, 1)

        @block.vector
        def _(dve):
            nc.vector.tensor_scalar(acol[DT, 0:1], dcol[DT, 1:2], 88.0, None, ALU.min).then_inc(a_capped, 1)
            dve.wait_ge(loaded, 32)
            dve.wait_ge(pads, 1)
            for n, (kind, c0, m, i, hf) in enumerate(blocks):
                if on_dve[n]:
                    dve.wait_ge(projected, n + 1)
                    if i >= 0:
                        mc = conv_outs[i].shape[0]
                        op = nc.vector.tensor_scalar(padded[0:mc, i, 2 * hf:2 * hf + 2, KCONV - 1:],
                                                     ps[0:mc, n % 8].rearrange("p (b s) -> p b s", b=2), mup[1], None, ALU.mult)
                    if i == dt_tile:
                        src = ps[DT, n % 8]
                        dst = dt_x[:, half(hf)] if dt_alone is None else dt_alone(dt_x, hf)
                        src = src if dt_alone is None else src.rearrange("p (b c l) -> p b c l", b=2, l=Q)
                        op = nc.vector.tensor_scalar(dst, src, dcol[DT, 0:1], None, ALU.add)
                    op.then_inc(dve_took, 1)
            dve.wait_ge(dve_took, n_dve)
            softplus_step(nc, dve, False, dt_x, dt_a, dt_e, dt_u, dt_l, dt, (chain, magnitude, exped, summed, logged, dt_ready))
            dve.wait_ge(a_exp, 1)
            nc.vector.tensor_scalar(acol[DT, 2:3], acol[DT, 1:2], -1.0, None, ALU.mult).then_inc(a_ready, 1)
            dve.wait_ge(a_ready, 1)
            dve.wait_ge(dt_ready, 1)
            nc.vector.tensor_scalar(decay, dt, acol[DT, 2:3], -200.0, ALU.mult, ALU.max).then_inc(exponents, 1)
            dve.wait_ge(decays, 1)
            nc.vector.tensor_copy(decay0, decay).then_inc(copied, 1)
            dve.wait_ge(copied, 1)
            nc.vector.memset(decay0.rearrange("h (c l) -> h c l", l=Q)[:, :, 0:1], 0.0).then_inc(zeroed, 1)
            dve.wait_ge(zeroed, 1)
            nc.vector.tensor_tensor(decay_s, decay, decay0, ALU.subtract).then_inc(starts, 1)
            dve.wait_ge(starts, 1)
            nc.vector.tensor_tensor_scan(cp, decay0, decay_s, 0.0, ALU.mult, ALU.add).then_inc(cps, 1)
            for i, out in enumerate(conv_outs):
                m = out.shape[0]
                if i >= 2:
                    dve.wait_ge(silued, i - 1)
                causal_taps(nc, dve, acc[0:m, i % 2], padded[0:m, i], cw[0:m, i], bias_col[0:m, i:i + 1], taps, KCONV * i)
def turn_phase(nc, new, name, conv_x, bt, dt, cp, DT, x_tok, b_tok, dt_tok, cp_tok, ident):
    n, nh = bt.shape[0], DT.stop - DT.start
    with ExitStack() as ctx:
        sb, sem = new(ctx)
        ps_x = ctx.enter_context(nc.psum_tensor(name + "_ps_x", [P, 2, HALF], F32))
        ps_b = ctx.enter_context(nc.psum_tensor(name + "_ps_b", [P, 2, HALF], F32))
        x_turned, b_turned, x_copied, b_copied = (sem(s) for s in ("x_turned", "b_turned", "x_copied", "b_copied"))
        block = ctx.enter_context(nc.Block())

        @block.tensor
        def _(pe):
            for t in range(TT):
                tok = slice(t * P, (t + 1) * P)
                if t >= 2:
                    wait_after(pe, x_copied, t - 1)
                for c in range(len(conv_x)):
                    mm = nc.tensor.transpose(ps_x[:, t % 2, c * P:(c + 1) * P], conv_x[c][:, tok], ident)
                mm.then_inc(x_turned, 1)
                if t >= 2:
                    wait_after(pe, b_copied, t - 1)
                o = ps_b[:, t % 2]
                nc.tensor.transpose(o[:, 0:n], bt[:, tok], ident[0:n, 0:n])
                nc.tensor.transpose(o[:, n:n + nh], dt[:, tok], ident[DT, DT])
                nc.tensor.transpose(o[:, n + nh:n + 2 * nh], cp[:, tok], ident[DT, DT]).then_inc(b_turned, 1)

        @block.scalar
        def _(act):
            for t in range(TT):
                act.wait_ge(x_turned, t + 1)
                nc.scalar.activation(x_tok[:, t, :], ps_x[:, t % 2], ACT.Copy).then_inc(x_copied, 1)

        @block.vector
        def _(dve):
            for t in range(TT):
                dve.wait_ge(b_turned, t + 1)
                o = ps_b[:, t % 2]
                nc.vector.tensor_copy(b_tok[:, t, :], o[:, 0:n])
                nc.vector.tensor_copy(dt_tok[:, t, :], o[:, n:n + nh])
                nc.vector.tensor_copy(cp_tok[:, t, :], o[:, n + nh:n + 2 * nh]).then_inc(b_copied, 1)


def scan0_phase(nc, new, conv_x, bt, ct, x_tok, b_tok, dt_tok, cp_tok, da_dram, delta_dram, d_col, gate_s, y_t, ident):
    with ExitStack() as ctx:
        sb, sem = new(ctx)
        NC = S // Q0
        delta = sb("delta", [P, NH0 * Q0])
        da = sb("da", [P, 2, NH0 * Q0])
        bts = sb("bts", [N0, 2, Q0])
        cts = sb("cts", [N0, 2, Q0])
        bs = sb("bs", [P, N0])
        decay = sb("decay", [P, 2, NH0, Q0])
        m = sb("m", [P, 2, NH0, Q0])
        xd = sb("xd", [P, 2, NH0, P0])
        xdec = sb("xdec", [P, NH0, P0])
        state = sb("state", [N0, E0])
        through = sb("through", [P, NH0, P0])
        y_tok = sb("y_tok", [P, 2, E0])
        ps_g = ctx.enter_context(nc.psum_tensor("s0_g", [P, 2, HALF], F32))
        ps_y = ctx.enter_context(nc.psum_tensor("s0_y", [P, 2, HALF], F32))
        ps_s = ctx.enter_context(nc.psum_tensor("s0_s", [P, HALF], F32))
        ps_o = ctx.enter_context(nc.psum_tensor("s0_o", [P, HALF], F32))
        ps_t = ctx.enter_context(nc.psum_tensor("s0_t", [P, 2, HALF], F32))
        (ld_delta, staged, g_made, scanned, m_made, xd_made, xdec_made, y_made, s_made, s_kept, o_made,
         o_scaled, y_kept, turned, y_out) = (sem(s) for s in (
            "ld_delta", "staged", "g_made", "scanned", "m_made", "xd_made", "xdec_made", "y_made", "s_made",
            "s_kept", "o_made", "o_scaled", "y_kept", "turned", "y_out"))
        ld_da = [sem("ld_da0"), sem("ld_da1")]
        block = ctx.enter_context(nc.Block())

        @block.sync
        def _(sp):
            sp.dma_start(delta[:], delta_dram).then_inc(ld_delta, 16)
            for c in range(2):
                sp.dma_start(da[:, c], da_dram[c:c + 1].rearrange("c h l -> c (h l)").partition_broadcast(P)).then_inc(ld_da[c], 16)
            with sp.Fori(1, B) as b:
                for c in range(2):
                    wait_after(sp, scanned, 2 * b + c - 1)
                    sp.dma_start(da[:, c], da_dram[bass.ds(2 * b + c, 1)].rearrange("c h l -> c (h l)").partition_broadcast(P)).then_inc(ld_da[c], 16)

        @block.tensor
        def _(pe):
            for b, first, last in turns(pe, B):
                for c in range(2):
                    pe.wait_ge(staged, 2 * b + c + 1)
                    nc.tensor.matmul(ps_g[:, c, 0:Q0], bts[:, c], cts[:, c], start=True, stop=True).then_inc(g_made, 1)
                for c in range(2):
                    if c == 1:
                        pe.wait_ge(s_kept, b + 1)
                        nc.tensor.matmul(ps_o[:], cts[:, 1], state[:], start=True, stop=True).then_inc(o_made, 1)
                    pe.wait_ge(m_made, 2 * b + c + 1)
                    pe.wait_ge(xd_made, 2 * b + c + 1)
                    for h in range(NH0):
                        mm = nc.tensor.matmul(ps_y[:, c, h * P0:(h + 1) * P0], m[:, c, h], xd[:, c, h], start=True, stop=True)
                    mm.then_inc(y_made, 1)
                    if c == 0:
                        pe.wait_ge(xdec_made, b + 1)
                        nc.tensor.matmul(ps_s[0:N0, :], bs[:], xdec[:].rearrange("p h q -> p (h q)"), start=True, stop=True).then_inc(s_made, 1)
                for c in range(2):
                    pe.wait_ge(y_kept, 2 * b + c + 1)
                    for t in range(NE0):
                        mm = nc.tensor.transpose(ps_t[:, c, t * P:(t + 1) * P], y_tok[:, c, t * P:(t + 1) * P], ident)
                    mm.then_inc(turned, 1)

        @block.scalar
        def _(act):
            for b, first, last in turns(act, B):
                act.wait_ge(s_made, b + 1)
                nc.scalar.activation(state[:], ps_s[0:N0, :], ACT.Copy).then_inc(s_kept, 1)
                act.wait_ge(y_made, 2 * b + 1)
                nc.scalar.activation(y_tok[:, 0], ps_y[:, 0], ACT.Copy).then_inc(y_kept, 1)

        @block.gpsimd
        def _(pool):
            for b, first, last in turns(pool, B):
                for c in range(2):
                    if c == 0:
                        wait_after(pool, o_made, b)
                    tok = bass.ds(b * S + c * Q0, Q0)
                    nc.gpsimd.tensor_copy(bts[:, c], bt[:, tok])
                    if c == 0:
                        wait_after(pool, s_made, b)
                        nc.gpsimd.tensor_copy(bs[:], b_tok[:, bass.ds(2 * b, 1), :].rearrange("p a n -> p (a n)"))
                    nc.gpsimd.tensor_copy(cts[:, c], ct[:, tok]).then_inc(staged, 1)

        @block.vector
        def _(dve):
            dve.wait_ge(ld_delta, 16)
            for b, first, last in turns(dve, B):
                for c in range(2):
                    dve.wait_ge(ld_da[c], 16 * (b + 1))
                    nc.vector.tensor_tensor_scan(decay[:, c].rearrange("p h l -> p (h l)"), da[:, c], delta[:], 0.0,
                                                 ALU.mult, ALU.add).then_inc(scanned, 1)
                    nc.vector.tensor_tensor(xd[:, c], x_tok[:, bass.ds(2 * b + c, 1), :].rearrange("p a (h q) -> p (a h) q", q=P0),
                                            dt_tok[:, bass.ds(2 * b + c, 1), :].rearrange("p a h -> p (a h)").unsqueeze(2).to_broadcast([P, NH0, P0]),
                                            ALU.mult).then_inc(xd_made, 1)
                    dve.wait_ge(scanned, 2 * b + c + 1)
                    dve.wait_ge(g_made, 2 * b + c + 1)
                    nc.vector.tensor_tensor(m[:, c], decay[:, c], ps_g[:, c, 0:Q0].unsqueeze(1).to_broadcast([P, NH0, Q0]),
                                            ALU.mult).then_inc(m_made, 1)
                    if c == 0:
                        dve.wait_ge(xd_made, 2 * b + 1)
                        nc.vector.tensor_tensor(xdec[:], xd[:, 0], decay[:, 0, :, Q0 - 1:Q0].to_broadcast([P, NH0, P0]),
                                                ALU.mult).then_inc(xdec_made, 1)
                dve.wait_ge(o_made, b + 1)
                nc.vector.tensor_tensor(through[:], ps_o[:].rearrange("p (h q) -> p h q", q=P0),
                                        cp_tok[:, bass.ds(2 * b + 1, 1), :].rearrange("p a h -> p (a h)").unsqueeze(2).to_broadcast([P, NH0, P0]),
                                        ALU.mult).then_inc(o_scaled, 1)
                dve.wait_ge(o_scaled, b + 1)
                dve.wait_ge(y_made, 2 * b + 2)
                dve.wait_ge(y_kept, 2 * b + 1)
                nc.vector.tensor_tensor(y_tok[:, 1], ps_y[:, 1], through[:].rearrange("p h q -> p (h q)"), ALU.add).then_inc(y_kept, 1)
                for c in range(2):
                    dve.wait_ge(turned, 2 * b + c + 1)
                    tok = bass.ds(b * S + c * Q0, Q0)
                    for t in range(NE0):
                        op = nc.vector.scalar_tensor_tensor(out=y_t[:, t, tok], in0=conv_x[t][:, tok], scalar=d_col[:, t:t + 1],
                                                            in1=ps_t[:, c, t * P:(t + 1) * P], op0=ALU.mult, op1=ALU.add)
                    op.then_inc(y_out, 1)
def router_phase(nc, new, name, h_t, gw, lower, w_dram, ident, X_, TOP, renorm):
    with ExitStack() as ctx:
        sb, sem = new(ctx)
        d = sb("d", [P, TT, X_])
        e = sb("e", [P, TT, X_])
        mx, den, rden = sb("mx", [P, TT]), sb("den", [P, TT]), sb("rden", [P, TT])
        gt = sb("gt", [P, TT, X_, X_])
        eq = sb("eq", [P, TT, X_, X_])
        rank = sb("rank", [P, TT, X_])
        w = sb("w", [P, TT, X_])
        w_t = sb("w_t", [X_, T])
        ps = ctx.enter_context(nc.psum_tensor(name + "_ps", [P, HALF], F32))
        ps_t = ctx.enter_context(nc.psum_tensor(name + "_ps_t", [P, NHALF, HALF], F32))
        logits, shifted, exped, weighed, turned, copied, sent, chain = (
            sem(s) for s in ("logits", "shifted", "exped", "weighed", "turned", "copied", "sent", "chain"))
        block = ctx.enter_context(nc.Block())

        @block.tensor
        def _(pe):
            for t in range(TT):
                for k in range(KH):
                    mm = nc.tensor.matmul(ps[:, t * X_:(t + 1) * X_], h_t[:, k, t * P:(t + 1) * P], gw[:, k, :],
                                          start=k == 0, stop=k == KH - 1)
            mm.then_inc(logits, 1)
            pe.wait_ge(weighed, 1)
            for t in range(TT):
                mm = nc.tensor.transpose(ps_t[0:X_, t // 4, (t % 4) * P:(t % 4 + 1) * P], w[:, t, :], ident)
            mm.then_inc(turned, 1)

        @block.scalar
        def _(act):
            act.wait_ge(shifted, 1)
            nc.scalar.activation(e[:], d[:], ACT.Exp).then_inc(exped, 1)
            act.wait_ge(turned, 1)
            nc.scalar.activation(w_t[:].rearrange("e (a t) -> e a t", a=NHALF), ps_t[0:X_], ACT.Copy).then_inc(copied, 1)

        @block.sync
        def _(sp):
            sp.wait_ge(copied, 1)
            sp.dma_start(w_dram, w_t[:]).then_inc(sent, 16)
            sp.wait_ge(sent, 16)

        @block.vector
        def _(dve):
            n = [0]

            def link(op):
                n[0] += 1
                op.then_inc(chain, 1)
                dve.wait_ge(chain, n[0])

            wide = [P, TT, X_]
            square = [P, TT, X_, X_]
            dve.wait_ge(logits, 1)
            l3 = ps[:, 0:TT * X_].rearrange("p (t e) -> p t e", e=X_)
            link(nc.vector.reduce_max(mx[:], l3, axis=X))
            nc.vector.tensor_tensor(d[:], l3, mx[:].unsqueeze(2).to_broadcast(wide), ALU.subtract).then_inc(shifted, 1)
            dve.wait_ge(exped, 1)
            link(nc.vector.reduce_sum(den[:], e[:], axis=X))
            link(nc.vector.reciprocal(rden[:], den[:]))
            link(nc.vector.tensor_tensor(e[:], e[:], rden[:].unsqueeze(2).to_broadcast(wide), ALU.mult))
            mine, other = e[:].unsqueeze(3).to_broadcast(square), e[:].unsqueeze(2).to_broadcast(square)
            link(nc.vector.tensor_tensor(eq[:], other, mine, ALU.is_equal))
            link(nc.vector.tensor_tensor(eq[:], eq[:], lower.unsqueeze(1).to_broadcast(square), ALU.mult))
            link(nc.vector.tensor_tensor(gt[:], other, mine, ALU.is_gt))
            link(nc.vector.tensor_tensor(gt[:], gt[:], eq[:], ALU.add))
            link(nc.vector.reduce_sum(rank[:], gt[:], axis=X))
            op = nc.vector.scalar_tensor_tensor(out=w[:], in0=rank[:], scalar=TOP - 0.5, in1=e[:], op0=ALU.is_lt, op1=ALU.mult)
            if renorm:
                link(op)
                link(nc.vector.reduce_sum(den[:], w[:], axis=X))
                link(nc.vector.reciprocal(rden[:], den[:]))
                op = nc.vector.tensor_tensor(w[:], w[:], rden[:].unsqueeze(2).to_broadcast(wide), ALU.mult)
            op.then_inc(weighed, 1)


def split_phase(nc, new, src, hi, lo):
    with ExitStack() as ctx:
        sb, sem = new(ctx)
        his = sem("his")
        block = ctx.enter_context(nc.Block())

        @block.scalar
        def _(act):
            for hf in range(NHALF):
                nc.scalar.activation(hi[:, :, half(hf)], src[:, :, half(hf)], ACT.Copy).then_inc(his, 1)

        @block.vector
        def _(dve):
            for hf in range(NHALF):
                dve.wait_ge(his, hf + 1)
                nc.vector.tensor_tensor(lo[:, :, half(hf)], src[:, :, half(hf)], hi[:, :, half(hf)].bitcast(F32), ALU.subtract)


def mixer_out_phase(nc, new, name, y_t, w_dram, addends, dst):
    n = y_t.shape[1]
    with ExitStack() as ctx:
        sb, sem = new(ctx)
        w_raw = sb("w_raw", [P, n, H])
        w_hi = sb("w_hi", [P, n, H], F32R)
        w_lo = sb("w_lo", [P, n, H], F32R)
        y_hi = sb("y_hi", [P, n, T], F32R)
        y_lo = sb("y_lo", [P, n, T], F32R)
        ps = ctx.enter_context(nc.psum_tensor(name + "_ps", [P, KH, NHALF, HALF], F32))
        loaded, w_his, y_his, w_los, y_los, made, chain = (
            sem(s) for s in ("loaded", "w_his", "y_his", "w_los", "y_los", "made", "chain"))
        block = ctx.enter_context(nc.Block())

        @block.sync
        def _(sp):
            sp.dma_start(w_raw[:], w_dram.rearrange("(k p) n -> p k n", p=P)).then_inc(loaded, 16)

        @block.scalar
        def _(act):
            for hf in range(NHALF):
                nc.scalar.activation(y_hi[:, :, half(hf)], y_t[:, :, half(hf)], ACT.Copy).then_inc(y_his, 1)
                if hf == 0:
                    act.wait_ge(loaded, 16)
                    nc.scalar.activation(w_hi[:], w_raw[:], ACT.Copy).then_inc(w_his, 1)

        @block.gpsimd
        def _(pool):
            pool.wait_ge(w_his, 1)
            nc.gpsimd.tensor_tensor(w_lo[:], w_raw[:], w_hi[:].bitcast(F32), ALU.subtract).then_inc(w_los, 1)

        @block.tensor
        def _(pe):
            pe.wait_ge(w_los, 1)
            for hf in range(NHALF):
                pe.wait_ge(y_los, hf + 1)
                for m in range(KH):
                    f = slice(m * P, (m + 1) * P)
                    for k in range(n):
                        mm = product3(nc, ps[:, m, hf], w_hi[:, k, f], w_lo[:, k, f], y_hi[:, k, half(hf)], y_lo[:, k, half(hf)],
                                      k == 0, k == n - 1)
                    mm.then_inc(made, 1)

        @block.vector
        def _(dve):
            for hf in range(NHALF):
                dve.wait_ge(y_his, hf + 1)
                nc.vector.tensor_tensor(y_lo[:, :, half(hf)], y_t[:, :, half(hf)], y_hi[:, :, half(hf)].bitcast(F32),
                                        ALU.subtract).then_inc(y_los, 1)
            done = 0
            for hf in range(NHALF):
                for m in range(KH):
                    dve.wait_ge(made, hf * KH + m + 1)
                    for i, a in enumerate(addends):
                        src = ps[:, m, hf] if i == 0 else dst[:, m, half(hf)]
                        nc.vector.tensor_tensor(dst[:, m, half(hf)], src, a[:, m, half(hf)], ALU.add).then_inc(chain, 1)
                        done += 1
                        dve.wait_ge(chain, done)
def keys_values_phase(nc, new, io, hn_hi, hn_lo, kz, v_tok):
    with ExitStack() as ctx:
        sb, sem = new(ctx)
        w_raw = sb("w_raw", [P, 2, KH, NKV * D])
        w_hi = sb("w_hi", [P, 2, KH, NKV * D], F32R)
        w_lo = sb("w_lo", [P, 2, KH, NKV * D], F32R)
        ps = ctx.enter_context(nc.psum_tensor("kv_ps", [P, 8, HALF], F32))
        loaded, w_his, w_los, made, low_took, high_took, v_took, zeroed = (
            sem(s) for s in ("loaded", "w_his", "w_los", "made", "low_took", "high_took", "v_took", "zeroed"))
        block = ctx.enter_context(nc.Block())
        nk = KT * NHALF

        @block.sync
        def _(sp):
            sp.dma_start(w_raw[:, 0], io["wk"].rearrange("(k p) n -> p k n", p=P)).then_inc(loaded, 16)
            sp.dma_start(w_raw[:, 1], io["wv"].rearrange("(k p) n -> p k n", p=P)).then_inc(loaded, 16)

        @block.gpsimd
        def _(pool):
            nc.gpsimd.memset(kz[D:P, 0], 0.0)
            nc.gpsimd.memset(kz[0:D, 1], 0.0).then_inc(zeroed, 1)

        @block.tensor
        def _(pe):
            pe.wait_ge(w_los, 1)
            for n in range(nk + TT):
                if n >= 8:
                    wait_after(pe, low_took, n - 7)
                    wait_after(pe, high_took, n - 7)
                for k in range(KH):
                    if n < nk:
                        f = slice(n // 2 * P, (n // 2 + 1) * P)
                        mm = product3(nc, ps[:, n % 8], w_hi[:, 0, k, f], w_lo[:, 0, k, f],
                                      hn_hi[:, k, half(n % 2)], hn_lo[:, k, half(n % 2)], k == 0, k == KH - 1)
                    else:
                        tok = slice((n - nk) * P, (n - nk + 1) * P)
                        mm = product3(nc, ps[:, n % 8], hn_hi[:, k, tok], hn_lo[:, k, tok],
                                      w_hi[:, 1, k], w_lo[:, 1, k], k == 0, k == KH - 1)
                mm.then_inc(made, 1)

        @block.scalar
        def _(act):
            act.wait_ge(loaded, 32)
            nc.scalar.activation(w_hi[:], w_raw[:], ACT.Copy).then_inc(w_his, 1)
            for n in range(nk):
                act.wait_ge(made, n + 1)
                nc.scalar.activation(kz[0:D, 0, n // 2, half(n % 2)], ps[0:D, n % 8], ACT.Copy).then_inc(low_took, 1)
            for t in range(0, TT, 2):
                act.wait_ge(made, nk + t + 1)
                nc.scalar.activation(v_tok[:, t, :], ps[:, (nk + t) % 8], ACT.Copy).then_inc(v_took, 1)

        @block.vector
        def _(dve):
            dve.wait_ge(w_his, 1)
            nc.vector.tensor_tensor(w_lo[:], w_raw[:], w_hi[:].bitcast(F32), ALU.subtract).then_inc(w_los, 1)
            for n in range(nk):
                dve.wait_ge(made, n + 1)
                nc.vector.tensor_copy(kz[D:P, 1, n // 2, half(n % 2)], ps[D:P, n % 8]).then_inc(high_took, 1)
            for t in range(1, TT, 2):
                dve.wait_ge(made, nk + t + 1)
                nc.vector.tensor_copy(v_tok[:, t, :], ps[:, (nk + t) % 8])


def attention_phase(nc, new, io, hn_hi, hn_lo, kz, v_tok, attn_t, ident, ident_bf, mask_bf):
    SCALE = float(D) ** -0.5
    NI = NHQ // NKV
    NU = NI * B
    AHEAD = 2
    with ExitStack() as ctx:
        sb, sem = new(ctx)
        wq_raw, wo_raw = sb("wq_raw", [P, 2, KH, P]), sb("wo_raw", [P, 2, H])
        wq_hi, wo_hi = sb("wq_hi", [P, 2, KH, P], F32R), sb("wo_hi", [P, 2, H], F32R)
        wq_lo, wo_lo = sb("wq_lo", [P, 2, KH, P], F32R), sb("wo_lo", [P, 2, H], F32R)
        q = sb("q", [P, 2, T])
        vs = sb("vs", [P, TT, P])
        probs = sb("probs", [P, 2, 6 * P])
        pt_a = sb("pt_a", [P, 2, 2, 2 * P])
        pt_b = sb("pt_b", [P, 2, 2, P])
        mx, nb = sb("mx", [P, 2, 4]), sb("nb", [P, 2, 4])
        rs, ri = sb("rs", [P, 2, 4]), sb("ri", [P, 2, 4])
        o_hi, o_lo = sb("o_hi", [P, 2, T], F32R), sb("o_lo", [P, 2, T], F32R)
        ps_a = ctx.enter_context(nc.psum_tensor("at_a", [P, HALF], F32))
        ps_s1 = ctx.enter_context(nc.psum_tensor("at_s1", [P, 2, HALF], F32))
        ps_s0 = ctx.enter_context(nc.psum_tensor("at_s0", [P, 2, HALF], F32))
        ps_t = ctx.enter_context(nc.psum_tensor("at_t", [P, 2, HALF], F32))
        ps_o = ctx.enter_context(nc.psum_tensor("at_o", [P, HALF], F32))
        ld_q, ld_o = [sem("ld_q0"), sem("ld_q1")], [sem("ld_o0"), sem("ld_o1")]
        (wq_his, wq_los, wo_his, wo_los, q_made, q_taken, v_staged, s_made, maxed, nb_made, exp_made, inverted, p_made,
         ta_made, tb_made, pta_copied, ptb_copied, o_made, o_his, o_los, wo_made, wo_taken, cleared) = (
            sem(s) for s in ("wq_his", "wq_los", "wo_his", "wo_los", "q_made", "q_taken", "v_staged", "s_made", "maxed",
                             "nb_made", "exp_made", "inverted", "p_made", "ta_made", "tb_made", "pta_copied",
                             "ptb_copied", "o_made", "o_his", "o_los", "wo_made", "wo_taken", "cleared"))
        nc.scalar.preload_act_table(ACT.Exp)
        block = ctx.enter_context(nc.Block())

        def later(m, i, b, n):
            k = 4 * i + b + n
            if k >= NU:
                m, k = m + 1, k - NU
            return None if isinstance(m, int) and m >= KT else (m, k // B, k % B)

        def before(m, i, b):
            return (m, i, b - 1) if b else (m, i - 1, B - 1) if i else (m - 1, NI - 1, B - 1)

        def next_tile(m, i, n):
            u = later(m, i, 0, n * B)
            return u and u[:2]

        @block.sync
        def _(sp):
            def load(m, i):
                j, slot = NI * m + i, i % 2
                wait_after(sp, wq_los, j - 1)
                sp.dma_start(wq_raw[:, slot], io["wq_tiles"][bass.ds(j, 1)].rearrange("a p k n -> p (a k) n")).then_inc(ld_q[slot], 16)
                wait_after(sp, wo_los, j - 1)
                sp.dma_start(wo_raw[:, slot], io["wo_tiles"][bass.ds(j, 1)].rearrange("a p n -> p (a n)")).then_inc(ld_o[slot], 16)

            for i in range(NI):
                load(0, i)
            with sp.Fori(1, KT) as m:
                for i in range(NI):
                    load(m, i)

        @block.gpsimd
        def _(pool):
            def split_q(m, i):
                pool.wait_ge(wq_his, NI * m + i + 1)
                nc.gpsimd.tensor_tensor(wq_lo[:, i % 2], wq_raw[:, i % 2], wq_hi[:, i % 2].bitcast(F32), ALU.subtract).then_inc(wq_los, 1)

            def split_o(m, i):
                pool.wait_ge(wo_his, NI * m + i + 1)
                nc.gpsimd.tensor_tensor(wo_lo[:, i % 2], wo_raw[:, i % 2], wo_hi[:, i % 2].bitcast(F32), ALU.subtract).then_inc(wo_los, 1)

            def stage_v(m, b):
                wait_after(pool, o_made, NU * m - B + b + 1)
                nc.gpsimd.tensor_copy(vs[:, 2 * b:2 * b + 2], v_tok[:, 2 * b:2 * b + 2, bass.ds(m * P, P)]).then_inc(v_staged, 1)

            split_q(0, 0)
            split_q(0, 1)
            for b in range(B):
                stage_v(0, b)
            for m, first, last in turns(pool, KT):
                for i in range(NI):
                    split_o(m, i)
                    ahead = next_tile(m, i, 2)
                    if ahead:
                        split_q(*ahead)
                    if i == NI - 1 and not last:
                        for b in range(B):
                            stage_v(m + 1, b)

        @block.tensor
        def _(pe):
            def project_q(m, i, hf):
                j = NI * m + i
                if hf == 0:
                    pe.wait_ge(wq_los, j + 1)
                wait_after(pe, q_taken, 2 * j + hf)
                wait_after(pe, wo_taken, 4 * (j - 2) + 2 * (hf + 1))
                for k in range(KH):
                    mm = product3(nc, ps_a[:], wq_hi[:, i % 2, k], wq_lo[:, i % 2, k],
                                  hn_hi[:, k, half(hf)], hn_lo[:, k, half(hf)], k == 0, k == KH - 1)
                mm.then_inc(q_made, 1)

            def project_o(m, i, hf, d, queries):
                j = NI * m + i
                if hf == 0 and d == 0:
                    pe.wait_ge(wo_los, j + 1)
                if d == 0:
                    pe.wait_ge(o_los, 4 * j + 2 * hf + 2)
                wait_after(pe, wo_taken, 4 * j + 2 * hf + d)
                if d == 0 and queries:
                    pe.wait_ge(q_taken, 2 * (j + 2) + (1 if hf else 0))
                f = slice(d * P, (d + 1) * P)
                product3(nc, ps_a[:], wo_hi[:, i % 2, f], wo_lo[:, i % 2, f],
                         o_hi[:, i % 2, half(hf)], o_lo[:, i % 2, half(hf)], True, True).then_inc(wo_made, 1)

            def scores(m, i, b):
                u = NU * m + 4 * i + b
                if b % 2 == 0:
                    pe.wait_ge(q_taken, 2 * (NI * m + i) + b // 2 + 1)
                wait_after(pe, exp_made, u - 1)
                both = [P, 2, P]
                tok = b * S
                s1 = ps_s1[:, b % 2].rearrange("p (h k) -> p h k", h=2)
                s0 = ps_s0[:, b % 2, 0:2 * P].rearrange("p (h k) -> p h k", h=2)
                kzm = kz[:, :, bass.ds(m, 1), :].rearrange("p h a t -> p h (a t)")
                nc.tensor.matmul(s1, q[:, i % 2, tok + P:tok + S], kzm[:, :, tok:tok + S], start=True, stop=False)
                nc.tensor.matmul(s1[:, :, P:], ident_bf, mask_bf.unsqueeze(1).to_broadcast(both), start=False, stop=True)
                nc.tensor.matmul(s0, q[:, i % 2, tok:tok + P], kzm[:, :, tok:tok + P], start=True, stop=False)
                nc.tensor.matmul(s0, ident_bf, mask_bf.unsqueeze(1).to_broadcast(both), start=False, stop=True).then_inc(s_made, 1)

            def turn(m, i, b):
                u = NU * m + 4 * i + b
                p = probs[:, b % 2]
                pe.wait_ge(p_made, u + 1)
                wait_after(pe, pta_copied, u)
                for h in range(2):
                    nc.tensor.transpose(ps_t[:, 0, 2 * h * P:(2 * h + 1) * P], p[:, (4 + h) * P:(5 + h) * P], ident)
                    mm = nc.tensor.transpose(ps_t[:, 0, (2 * h + 1) * P:(2 * h + 2) * P], p[:, 2 * h * P:(2 * h + 1) * P], ident)
                mm.then_inc(ta_made, 1)
                wait_after(pe, ptb_copied, u)
                for h in range(2):
                    mm = nc.tensor.transpose(ps_t[:, 1, h * P:(h + 1) * P], p[:, (2 * h + 1) * P:(2 * h + 2) * P], ident)
                mm.then_inc(tb_made, 1)

            def heads_out(m, i, b):
                u = NU * m + 4 * i + b
                if i == 0:
                    pe.wait_ge(v_staged, B * m + b + 1)
                pe.wait_ge(pta_copied, u + 1)
                pe.wait_ge(ptb_copied, u + 1)
                wait_after(pe, o_los, u)
                for h in range(2):
                    rows = slice(h * D, (h + 1) * D)
                    nc.tensor.matmul(ps_o[rows, 0:2 * P], vs[:, 2 * b, rows], pt_a[:, b % 2, h], start=True, stop=False)
                    mm = nc.tensor.matmul(ps_o[rows, P:2 * P], vs[:, 2 * b + 1, rows], pt_b[:, b % 2, h], start=False, stop=True)
                mm.then_inc(o_made, 1)

            for hf in range(NHALF):
                project_q(0, 0, hf)
            for b in range(AHEAD):
                scores(0, 0, b)
            for m, first, last in turns(pe, KT):
                for i in range(NI):
                    for b in range(B):
                        turn(m, i, b)
                        following = next_tile(m, i, 1)
                        if b % 2 == 0 and following:
                            project_q(*following, b // 2)
                        done = None
                        if b == 1 and not (first and i == 0):
                            done = ((m, i - 1) if i else (m - 1, NI - 1)) + (1,)
                        if b == 3:
                            done = (m, i, 0)
                        if done:
                            project_o(*done, 0, following)
                        unit = later(m, i, b, AHEAD)
                        if unit:
                            scores(*unit)
                        if done:
                            project_o(*done, 1, following)
                        heads_out(m, i, b)
            for d in range(KH):
                project_o(KT - 1, NI - 1, 1, d, None)

        @block.scalar
        def _(act):
            def split_q(m, i):
                j = NI * m + i
                act.wait_ge(ld_q[i % 2], 16 * (NI // 2 * m + i // 2 + 1))
                wait_after(act, q_made, 2 * (j - 1))
                nc.scalar.activation(wq_hi[:, i % 2], wq_raw[:, i % 2], ACT.Copy).then_inc(wq_his, 1)

            def split_o(m, i):
                j = NI * m + i
                act.wait_ge(ld_o[i % 2], 16 * (NI // 2 * m + i // 2 + 1))
                wait_after(act, wo_made, 4 * (j - 1))
                nc.scalar.activation(wo_hi[:, i % 2], wo_raw[:, i % 2], ACT.Copy).then_inc(wo_his, 1)

            def take_q(m, i, hf):
                j = NI * m + i
                act.wait_ge(q_made, 2 * j + hf + 1)
                nc.scalar.activation(q[:, i % 2, half(hf)], ps_a[:], ACT.Copy).then_inc(q_taken, 1)

            def exps(m, i, b):
                u = NU * m + 4 * i + b
                wait_after(act, nb_made, u + 1)
                parts = ((ps_s1[:, b % 2, 0:2 * P], 0, 2 * P), (ps_s1[:, b % 2, 2 * P:4 * P], 2 * P, 2 * P),
                         (ps_s0[:, b % 2, 0:P], 4 * P, P), (ps_s0[:, b % 2, P:2 * P], 5 * P, P))
                for n, (src, c, w) in enumerate(parts):
                    op = nc.scalar.activation(probs[:, b % 2, c:c + w], src, ACT.Exp, bias=nb[:, b % 2, n:n + 1], scale=SCALE,
                                              accum_out=rs[:, b % 2, n:n + 1])
                op.then_inc(exp_made, 1)

            def take_pt(m, i, b):
                u = NU * m + 4 * i + b
                act.wait_ge(ta_made, u + 1)
                nc.scalar.activation(pt_a[:, b % 2].rearrange("p h q -> p (h q)"), ps_t[:, 0], ACT.Copy).then_inc(pta_copied, 1)

            def take_o(m, i, b):
                u = NU * m + 4 * i + b
                act.wait_ge(o_made, u + 1)
                nc.scalar.activation(o_hi[:, i % 2, b * S:(b + 1) * S], ps_o[:, 0:2 * P], ACT.Copy).then_inc(o_his, 1)

            split_q(0, 0)
            split_q(0, 1)
            for hf in range(NHALF):
                take_q(0, 0, hf)
            exps(0, 0, 0)
            for m, first, last in turns(act, KT):
                for i in range(NI):
                    for b in range(B):
                        if not (first and i == 0 and b == 0):
                            take_o(*before(m, i, b))
                        take_pt(m, i, b)
                        following, ahead = next_tile(m, i, 1), next_tile(m, i, 2)
                        unit = later(m, i, b, 1)
                        if unit:
                            exps(*unit)
                        if b % 2 == 0 and following:
                            take_q(*following, b // 2)
                        if b == 1 and ahead:
                            split_q(*ahead)
                        if b == 1:
                            split_o(m, i)
            take_o(KT - 1, NI - 1, B - 1)

        @block.vector
        def _(dve):
            def maxima(m, i, b):
                u = NU * m + 4 * i + b
                dve.wait_ge(s_made, u + 1)
                nc.vector.reduce_max(mx[:, b % 2, 0:2], ps_s1[:, b % 2].rearrange("p (h k) -> p h k", h=2), axis=X)
                nc.vector.reduce_max(mx[:, b % 2, 2:4], ps_s0[:, b % 2, 0:2 * P].rearrange("p (h k) -> p h k", h=2), axis=X).then_inc(maxed, 1)
                dve.wait_ge(maxed, u + 1)
                nc.vector.tensor_scalar(nb[:, b % 2], mx[:, b % 2], -SCALE, None, ALU.mult).then_inc(nb_made, 1)

            def normalize(m, i, b):
                u = NU * m + 4 * i + b
                dve.wait_ge(exp_made, u + 1)
                nc.vector.reciprocal(ri[:, b % 2], rs[:, b % 2]).then_inc(inverted, 1)
                dve.wait_ge(inverted, u + 1)
                for n, (c, w) in enumerate(((0, 2 * P), (2 * P, 2 * P), (4 * P, P), (5 * P, P))):
                    p = probs[:, b % 2, c:c + w]
                    op = nc.vector.tensor_scalar(p, p, ri[:, b % 2, n:n + 1], None, ALU.mult)
                op.then_inc(p_made, 1)

            def take_pt(m, i, b):
                u = NU * m + 4 * i + b
                dve.wait_ge(tb_made, u + 1)
                nc.vector.tensor_copy(pt_b[:, b % 2].rearrange("p h q -> p (h q)"), ps_t[:, 1, 0:2 * P]).then_inc(ptb_copied, 1)

            def split_o(m, i, b):
                u = NU * m + 4 * i + b
                dve.wait_ge(o_his, u + 1)
                o = (slice(None), i % 2, slice(b * S, (b + 1) * S))
                nc.vector.tensor_tensor(o_lo[o], ps_o[:, 0:2 * P], o_hi[o].bitcast(F32), ALU.subtract).then_inc(o_los, 1)

            def take_projection(m, i, hf, d):
                dve.wait_ge(wo_made, 4 * (NI * m + i) + 2 * hf + d + 1)
                nc.vector.tensor_tensor(attn_t[:, d, half(hf)], ps_a[:], attn_t[:, d, half(hf)], ALU.add).then_inc(wo_taken, 1)

            nc.vector.memset(attn_t[:], 0.0).then_inc(cleared, 1)
            dve.wait_ge(cleared, 1)
            for b in range(AHEAD):
                maxima(0, 0, b)
            normalize(0, 0, 0)
            for m, first, last in turns(dve, KT):
                for i in range(NI):
                    for b in range(B):
                        if not (first and i == 0 and b == 0):
                            split_o(*before(m, i, b))
                        take_pt(m, i, b)
                        done = None
                        if b == 1 and not (first and i == 0):
                            done = ((m, i - 1) if i else (m - 1, NI - 1)) + (1,)
                        if b == 3:
                            done = (m, i, 0)
                        if done:
                            take_projection(*done, 0)
                        unit = later(m, i, b, 1)
                        if unit:
                            normalize(*unit)
                        if done:
                            take_projection(*done, 1)
                        unit = later(m, i, b, AHEAD)
                        if unit:
                            maxima(*unit)
            split_o(KT - 1, NI - 1, B - 1)
            for d in range(KH):
                take_projection(KT - 1, NI - 1, 1, d)
class Experts:

    def __init__(self, nc, ctx, new, name, w_dram, func, t_hi, t_lo, acc):
        sb, sem = new(ctx)
        self.nc, self.w_dram, self.func, self.t_hi, self.t_lo, self.acc = nc, w_dram, func, t_hi, t_lo, acc
        self.raw_ab, self.raw_c = sb("raw_ab", [P, 2, 2, H]), sb("raw_c", [P, 2, H])
        self.ab_hi, self.ab_lo = sb("ab_hi", [P, 2, 2, H], F32R), sb("ab_lo", [P, 2, 2, H], F32R)
        self.c_hi, self.c_lo = sb("c_hi", [P, 2, H], F32R), sb("c_lo", [P, 2, H], F32R)
        self.r, self.rc, self.g = sb("r", [P, 2, HALF]), sb("rc", [P, 2, HALF]), sb("g", [P, 2, HALF])
        self.g_hi, self.g_lo = sb("g_hi", [P, 2, HALF], F32R), sb("g_lo", [P, 2, HALF], F32R)
        self.ps_u = ctx.enter_context(nc.psum_tensor(name + "_u", [P, 2, HALF], F32))
        self.ps_v = ctx.enter_context(nc.psum_tensor(name + "_v", [P, 2, HALF], F32))
        self.ps_y = ctx.enter_context(nc.psum_tensor(name + "_y", [P, KH, HALF], F32))
        self.ld_ab, self.ld_c = [sem("ld_ab0"), sem("ld_ab1")], [sem("ld_c0"), sem("ld_c1")]
        (self.ab_his, self.ab_los, self.c_his, self.c_los, self.u_made, self.r_made, self.rc_made, self.g_made, self.g_his,
         self.g_los, self.y_made, self.y_added, self.cleared) = (
            sem(s) for s in ("ab_his", "ab_los", "c_his", "c_los", "u_made", "r_made", "rc_made", "g_made", "g_his", "g_los",
                             "y_made", "y_added", "cleared"))

    def load(self, sp, t, j):
        src = self.w_dram[bass.ds(2 * t + j, 1)].rearrange("a p j n -> p (a j) n")
        wait_after(sp, self.ab_los, 2 * t + j - 1)
        sp.dma_start(self.raw_ab[:, j], src[:, 0:2]).then_inc(self.ld_ab[j], 16)
        wait_after(sp, self.c_los, 2 * t + j - 1)
        sp.dma_start(self.raw_c[:, j], src[:, 2]).then_inc(self.ld_c[j], 16)

    def up(self, pe, t, s):
        nc, (hf, j), n = self.nc, divmod(s, 2), 4 * t + s
        if hf == 0:
            pe.wait_ge(self.ab_los, 2 * t + j + 1)
        wait_after(pe, self.g_made, n - 1)
        for ps, i in ((self.ps_u, 0), (self.ps_v, 1)):
            for k in range(KH):
                f = slice(k * P, (k + 1) * P)
                mm = product3(nc, ps[:, j], self.ab_hi[:, j, i, f], self.ab_lo[:, j, i, f],
                              self.t_hi[:, k, half(hf)], self.t_lo[:, k, half(hf)], k == 0, k == KH - 1)
        mm.then_inc(self.u_made, 1)

    def down(self, pe, t, s):
        nc, (hf, j), n = self.nc, divmod(s, 2), 4 * t + s
        if hf == 0:
            pe.wait_ge(self.c_los, 2 * t + j + 1)
        pe.wait_ge(self.g_los, n + 1)
        if j == 0:
            wait_after(pe, self.y_added, 2 * t + hf)
        for d in range(KH):
            f = slice(d * P, (d + 1) * P)
            mm = product3(nc, self.ps_y[:, d], self.c_hi[:, j, f], self.c_lo[:, j, f], self.g_hi[:, j], self.g_lo[:, j],
                          j == 0, j == 1)
        mm.then_inc(self.y_made, 1)

    def pe_step(self, pe, t, s, first):
        self.up(pe, t, s)
        if s >= 2:
            self.down(pe, t, s - 2)
        elif not first:
            self.down(pe, t - 1, s + 2)

    def pe_end(self, pe, t):
        self.down(pe, t, 2)
        self.down(pe, t, 3)

    def split_ab_hi(self, act, t, j):
        act.wait_ge(self.ld_ab[j], 16 * (t + 1))
        wait_after(act, self.u_made, 4 * t - 1 + j)
        self.nc.scalar.activation(self.ab_hi[:, j], self.raw_ab[:, j], ACT.Copy).then_inc(self.ab_his, 1)

    def split_c_hi(self, act, t, j):
        act.wait_ge(self.ld_c[j], 16 * (t + 1))
        wait_after(act, self.y_made, 4 * t - 1 + j)
        self.nc.scalar.activation(self.c_hi[:, j], self.raw_c[:, j], ACT.Copy).then_inc(self.c_his, 1)

    def act_step(self, act, t, s, first, last):
        j, n = s % 2, 4 * t + s
        if s == 0 and first:
            self.split_ab_hi(act, t, 0)
            self.split_ab_hi(act, t, 1)
        if s >= 2 and not last:
            self.split_ab_hi(act, t + 1, s - 2)
        act.wait_ge(self.u_made, n + 1)
        wait_after(act, self.rc_made, n - 1)
        self.nc.scalar.activation(self.r[:, j], self.ps_u[:, j], self.func).then_inc(self.r_made, 1)
        if s < 2:
            self.split_c_hi(act, t, s)
        act.wait_ge(self.g_made, n + 1)
        wait_after(act, self.y_made, n - 1)
        self.nc.scalar.activation(self.g_hi[:, j], self.g[:, j], ACT.Copy).then_inc(self.g_his, 1)

    def split_c_lo(self, pool, t, j):
        pool.wait_ge(self.c_his, 2 * t + j + 1)
        self.nc.gpsimd.tensor_tensor(self.c_lo[:, j], self.raw_c[:, j], self.c_hi[:, j].bitcast(F32),
                                     ALU.subtract).then_inc(self.c_los, 1)

    def pool_step(self, pool, t, s, router):
        (hf, j), n = divmod(s, 2), 4 * t + s
        pool.wait_ge(self.r_made, n + 1)
        self.nc.gpsimd.tensor_tensor(self.rc[:, j], self.r[:, j], router, ALU.mult).then_inc(self.rc_made, 1)
        if s < 2:
            self.split_c_lo(pool, t, s)

    def dve_start(self, dve):
        self.nc.vector.memset(self.acc[:], 0.0).then_inc(self.cleared, 1)
        dve.wait_ge(self.cleared, 1)

    def split_ab_lo(self, dve, t, j):
        dve.wait_ge(self.ab_his, 2 * t + j + 1)
        self.nc.vector.tensor_tensor(self.ab_lo[:, j], self.raw_ab[:, j], self.ab_hi[:, j].bitcast(F32),
                                     ALU.subtract).then_inc(self.ab_los, 1)

    def add_y(self, dve, t, hf):
        dve.wait_ge(self.y_made, 4 * t + 2 * hf + 2)
        op = self.nc.vector.tensor_tensor(self.acc[:, :, half(hf)], self.ps_y[:], self.acc[:, :, half(hf)], ALU.add)
        op.then_inc(self.y_added, 1)

    def dve_step(self, dve, t, s, first, last):
        nc, j, n = self.nc, s % 2, 4 * t + s
        if s == 0 and first:
            self.split_ab_lo(dve, t, 0)
            self.split_ab_lo(dve, t, 1)
        if s >= 2 and not last:
            self.split_ab_lo(dve, t + 1, s - 2)
        if s == 3:
            self.add_y(dve, t, 0)
        if s == 1 and not first:
            self.add_y(dve, t - 1, 1)
        dve.wait_ge(self.rc_made, n + 1)
        nc.vector.tensor_tensor(self.g[:, j], self.rc[:, j], self.ps_v[:, j], ALU.mult).then_inc(self.g_made, 1)
        dve.wait_ge(self.g_his, n + 1)
        nc.vector.tensor_tensor(self.g_lo[:, j], self.g[:, j], self.g_hi[:, j].bitcast(F32), ALU.subtract).then_inc(self.g_los, 1)

    def dve_end(self, dve, t):
        self.add_y(dve, t, 1)


def experts0_phase(nc, new, io, t_hi, t_lo, cw_dram, moe_t):
    NT = FT0 // 2
    with ExitStack() as ctx:
        sb, sem = new(ctx)
        x = Experts(nc, ctx, new, "x0", io["x0_w"], ACT.Relu, t_hi, t_lo, moe_t)
        router = sb("router", [P, T])
        ld_router = [sem("ld_router0"), sem("ld_router1")]
        block = ctx.enter_context(nc.Block())

        @block.sync
        def _(sp):
            for j in range(2):
                x.load(sp, 0, j)
            for t in range(1, NT):
                for j in range(2):
                    x.load(sp, t, j)
            with sp.Fori(1, X0) as e:
                for t in range(NT):
                    for j in range(2):
                        x.load(sp, NT * e + t, j)

        @block.tensor
        def _(pe):
            for e, first, last in turns(pe, X0):
                for t in range(NT):
                    for s in range(4):
                        x.pe_step(pe, NT * e + t, s, first and t == 0)
            x.pe_end(pe, NT * X0 - 1)

        @block.scalar
        def _(act):
            def load_router(e, hf):
                act.dma_start(router[:, half(hf)], cw_dram[bass.ds(e, 1), half(hf)].partition_broadcast(P)).then_inc(ld_router[hf], 16)

            for hf in range(NHALF):
                load_router(0, hf)
            for e, first, last in turns(act, X0):
                for t in range(NT):
                    for s in range(4):
                        x.act_step(act, NT * e + t, s, first and t == 0, last and t == NT - 1)
                        if t == NT - 1 and s % 2 and not last:
                            act.wait_ge(x.rc_made, 4 * NT * e + 4 * t + s + 1)
                            load_router(e + 1, s // 2)

        @block.gpsimd
        def _(pool):
            for e, first, last in turns(pool, X0):
                for t in range(NT):
                    for s in range(4):
                        if t == 0 and s % 2 == 0:
                            pool.wait_ge(ld_router[s // 2], 16 * (e + 1))
                        x.pool_step(pool, NT * e + t, s, router[:, half(s // 2)])

        @block.vector
        def _(dve):
            x.dve_start(dve)
            for e, first, last in turns(dve, X0):
                for t in range(NT):
                    for s in range(4):
                        x.dve_step(dve, NT * e + t, s, first and t == 0, last and t == NT - 1)
            x.dve_end(dve, NT * X0 - 1)


def router_segments(q):
    out, p = [], 0
    while p < P:
        e = (q * P + p) // F1
        stop = min(P, (e + 1) * F1 - q * P)
        out.append((e, p, stop))
        p = stop
    return out if len(out) > 1 else [(out[0][0], 0, P // 2), (out[0][0], P // 2, P)]


def experts1_phase(nc, new, io, t_hi, t_lo, cw_dram, moe_t):
    NT = FT1 // 2
    with ExitStack() as ctx:
        sb, sem = new(ctx)
        x = Experts(nc, ctx, new, "x1", io["x1_w"], ACT.Silu, t_hi, t_lo, moe_t)
        router = sb("router", [P, 2, T])
        ld_router = [sem("ld_router0"), sem("ld_router1")]
        nc.scalar.preload_act_table(ACT.Silu)
        block = ctx.enter_context(nc.Block())

        @block.sync
        def _(sp):
            for t in range(NT):
                for j in range(2):
                    x.load(sp, t, j)
                    if t > 0:
                        sp.wait_ge(x.rc_made, 4 * (t - 1) + 3 + j)
                    for e, a, z in router_segments(2 * t + j):
                        sp.dma_start(router[a:z, j], cw_dram[e:e + 1].partition_broadcast(z - a)).then_inc(ld_router[j], 16)

        @block.tensor
        def _(pe):
            for t, first, last in turns(pe, NT):
                for s in range(4):
                    x.pe_step(pe, t, s, first)
            x.pe_end(pe, NT - 1)

        @block.scalar
        def _(act):
            for t, first, last in turns(act, NT):
                for s in range(4):
                    x.act_step(act, t, s, first, last)

        @block.gpsimd
        def _(pool):
            for t, first, last in turns(pool, NT):
                for s in range(4):
                    if s < 2:
                        pool.wait_ge(ld_router[s], 32 * (t + 1))
                    x.pool_step(pool, t, s, router[:, s % 2, half(s // 2)])

        @block.vector
        def _(dve):
            x.dve_start(dve)
            for t, first, last in turns(dve, NT):
                for s in range(4):
                    x.dve_step(dve, t, s, first, last)
            x.dve_end(dve, NT - 1)
def scan1_phase(nc, new, conv_x, bt, ct, x_tok, b_tok, dt_tok, cp_tok, da_dram, tot_dram, delta_dram, d_col, y_t, ident):
    with ExitStack() as ctx:
        sb, sem = new(ctx)
        HL = NH1 * Q1
        HQ, HG = 4, NH1 // 4
        delta = sb("delta", [P, HL])
        da = sb("da", [P, HL])
        tot = sb("tot", [P, NC1, B * NH1])
        bts, cts, bs = sb("bts", [N1, P]), sb("cts", [N1, P]), sb("bs", [P, N1])
        decay = sb("decay", [P, NH1, Q1])
        m = sb("m", [P, NH1, Q1])
        xd = sb("xd", [P, NH1, P1])
        xbd = sb("xbd", [P, NH1, B, P1])
        xdec = sb("xdec", [P, NH1, P1])
        state = sb("state", [N1, B, E1])
        through = sb("through", [P, E1])
        y_tok = sb("y_tok", [P, E1])
        ps_g = ctx.enter_context(nc.psum_tensor("s1_g", [P, HALF], F32))
        ps_y = ctx.enter_context(nc.psum_tensor("s1_y", [P, HALF], F32))
        ps_s = ctx.enter_context(nc.psum_tensor("s1_s", [P, B, HALF], F32))
        ps_o = ctx.enter_context(nc.psum_tensor("s1_o", [P, HALF], F32))
        ps_t = ctx.enter_context(nc.psum_tensor("s1_t", [P, HALF], F32))
        (tot_sent, ld_delta, ld_tot, ld_da, staged, g_made, scanned, m_made, xd_made, xbd_made, xdec_made, y_made, s_made, decayed,
         s_kept, o_made, o_scaled, y_kept, turned, y_out, cleared, state_clear) = (sem(s) for s in (
            "tot_sent", "ld_delta", "ld_tot", "ld_da", "staged", "g_made", "scanned", "m_made", "xd_made", "xbd_made", "xdec_made",
            "y_made", "s_made", "decayed", "s_kept", "o_made", "o_scaled", "y_kept", "turned", "y_out", "cleared",
            "state_clear"))
        block = ctx.enter_context(nc.Block())

        @block.sync
        def _(sp):
            def load_decays(c):
                for b in range(B):
                    sp.dma_start(da[b * Q1:(b + 1) * Q1, :],
                                 da_dram[bass.ds(c * B + b, 1)].rearrange("c h l -> c (h l)").partition_broadcast(Q1)).then_inc(ld_da, 16)

            sp.dma_start(delta[:], delta_dram).then_inc(ld_delta, 16)
            load_decays(0)
            sp.dma_start(tot_dram.rearrange("(c b) h -> b c h", b=B), cp_tok[Q1 - 1:P:Q1]).then_inc(tot_sent, 16)
            sp.wait_ge(tot_sent, 16)
            sp.dma_start(tot[:].rearrange("p c n -> p (c n)"),
                         tot_dram.rearrange("(o c) h -> o (c h)", o=1).partition_broadcast(P)).then_inc(ld_tot, 16)
            with sp.Fori(1, NC1) as c:
                wait_after(sp, scanned, c)
                load_decays(c)

        @block.gpsimd
        def _(pool):
            nc.gpsimd.memset(xbd[:], 0.0).then_inc(cleared, 1)
            nc.gpsimd.memset(state[:], 0.0).then_inc(state_clear, 1)
            for c, first, last in turns(pool, NC1):
                wait_after(pool, s_made, c)
                wait_after(pool, o_made, c)
                tok = bass.ds(c * P, P)
                nc.gpsimd.tensor_copy(bts[:], bt[:, tok])
                nc.gpsimd.tensor_copy(cts[:], ct[:, tok])
                nc.gpsimd.tensor_copy(bs[:], b_tok[:, bass.ds(c, 1), :].rearrange("p a n -> p (a n)")).then_inc(staged, 1)
                pool.wait_ge(o_made, c + 1)
                pool.wait_ge(ld_tot, 16)
                st = state[:].rearrange("n b (h q) -> n (b h) q", q=P1)
                nc.gpsimd.tensor_tensor(st, st, tot[:, bass.ds(c, 1), :].rearrange("p a n -> p (a n)").unsqueeze(2).to_broadcast([P, B * NH1, P1]),
                                        ALU.mult).then_inc(decayed, 1)

        @block.tensor
        def _(pe):
            for c, first, last in turns(pe, NC1):
                pe.wait_ge(staged, c + 1)
                for b in range(B):
                    rows = slice(b * Q1, (b + 1) * Q1)
                    mm = nc.tensor.matmul(ps_g[rows, 0:Q1], bts[:, rows], cts[:, rows], start=True, stop=True, tile_position=(0, b * Q1))
                mm.then_inc(g_made, 1)
                wait_after(pe, s_kept, c)
                pe.wait_ge(state_clear, 1)
                for b in range(B):
                    rows = slice(b * Q1, (b + 1) * Q1)
                    mm = nc.tensor.matmul(ps_o[rows, :], cts[:, rows], state[:, b], start=True, stop=True, tile_position=(0, b * Q1))
                mm.then_inc(o_made, 1)
                pe.wait_ge(xdec_made, c + 1)
                for b in range(B):
                    rows = slice(b * Q1, (b + 1) * Q1)
                    mm = nc.tensor.matmul(ps_s[:, b], bs[rows, :], xdec[rows].rearrange("p h q -> p (h q)"), start=True, stop=True,
                                          tile_position=(b * Q1, 0))
                mm.then_inc(s_made, 1)
                pe.wait_ge(m_made, c + 1)
                pe.wait_ge(xbd_made, c + 1)
                for h in range(NH1):
                    hq, hg = h // HG, h % HG
                    mm = nc.tensor.matmul(ps_y[hq * Q1:(hq + 1) * Q1, hg * Q1:(hg + 1) * Q1], m[:, h],
                                          xbd[:, h].rearrange("p b q -> p (b q)"), start=True, stop=True, tile_position=(0, hq * Q1))
                mm.then_inc(y_made, 1)
                pe.wait_ge(y_kept, c + 1)
                for t in range(NE1):
                    mm = nc.tensor.transpose(ps_t[:, t * P:(t + 1) * P], y_tok[:, t * P:(t + 1) * P], ident)
                mm.then_inc(turned, 1)

        @block.scalar
        def _(act):
            act.wait_ge(cleared, 1)
            for c, first, last in turns(act, NC1):
                act.wait_ge(xd_made, c + 1)
                for b in range(B):
                    rows = slice(b * Q1, (b + 1) * Q1)
                    op = nc.scalar.activation(xbd[rows, :, b], xd[rows], ACT.Copy)
                op.then_inc(xbd_made, 1)

        @block.vector
        def _(dve):
            dve.wait_ge(ld_delta, 16)
            for c, first, last in turns(dve, NC1):
                dve.wait_ge(ld_da, 64 * (c + 1))
                nc.vector.tensor_tensor_scan(decay[:].rearrange("p h l -> p (h l)"), da[:], delta[:], 0.0,
                                             ALU.mult, ALU.add).then_inc(scanned, 1)
                nc.vector.tensor_tensor(xd[:], x_tok[:, bass.ds(c, 1), :].rearrange("p a (h q) -> p (a h) q", q=P1),
                                        dt_tok[:, bass.ds(c, 1), :].rearrange("p a h -> p (a h)").unsqueeze(2).to_broadcast([P, NH1, P1]),
                                        ALU.mult).then_inc(xd_made, 1)
                dve.wait_ge(xd_made, c + 1)
                dve.wait_ge(scanned, c + 1)
                nc.vector.tensor_tensor(xdec[:], xd[:], decay[:, :, Q1 - 1:Q1].to_broadcast([P, NH1, P1]),
                                        ALU.mult).then_inc(xdec_made, 1)
                dve.wait_ge(g_made, c + 1)
                nc.vector.tensor_tensor(m[:], decay[:], ps_g[:, 0:Q1].unsqueeze(1).to_broadcast([P, NH1, Q1]),
                                        ALU.mult).then_inc(m_made, 1)
                dve.wait_ge(o_made, c + 1)
                nc.vector.tensor_tensor(through[:].rearrange("p (h q) -> p h q", q=P1), ps_o[:].rearrange("p (h q) -> p h q", q=P1),
                                        cp_tok[:, bass.ds(c, 1), :].rearrange("p a h -> p (a h)").unsqueeze(2).to_broadcast([P, NH1, P1]),
                                        ALU.mult).then_inc(o_scaled, 1)
                dve.wait_ge(s_made, c + 1)
                dve.wait_ge(decayed, c + 1)
                for b in range(B):
                    op = nc.vector.tensor_tensor(state[:, b], ps_s[:, b], state[:, b], ALU.add)
                op.then_inc(s_kept, 1)
                dve.wait_ge(o_scaled, c + 1)
                dve.wait_ge(y_made, c + 1)
                for hq in range(HQ):
                    for b in range(B):
                        rows, cols = slice(b * Q1, (b + 1) * Q1), slice(hq * P, (hq + 1) * P)
                        src = ps_y[hq * Q1:(hq + 1) * Q1, :].rearrange("l (g b q) -> l g b q", b=B, q=P1)[:, :, b]
                        op = nc.vector.tensor_tensor(y_tok[rows, cols].rearrange("l (g q) -> l g q", q=P1), src,
                                                     through[rows, cols].rearrange("l (g q) -> l g q", q=P1), ALU.add)
                op.then_inc(y_kept, 1)
                dve.wait_ge(turned, c + 1)
                tok = bass.ds(c * P, P)
                for t in range(NE1):
                    nat = y_t[:, t, :].rearrange("p (b c l) -> p b c l", b=B, l=Q1)[:, :, bass.ds(c, 1), :].rearrange("p b a l -> p b (a l)")
                    op = nc.vector.scalar_tensor_tensor(out=nat, in0=conv_x[t][:, tok].rearrange("p (b l) -> p b l", b=B),
                                                        scalar=d_col[:, t:t + 1],
                                                        in1=ps_t[:, t * P:(t + 1) * P].rearrange("p (b l) -> p b l", b=B),
                                                        op0=ALU.mult, op1=ALU.add)
                op.then_inc(y_out, 1)
def gate_phase(nc, y_t, gate_s, n):
    with nc.Block() as block:
        @block.vector
        def _(dve):
            for t in range(n // 2):
                nc.vector.tensor_tensor(y_t[:, t], y_t[:, t], gate_s[:, t], ALU.mult)

        @block.gpsimd
        def _(pool):
            for t in range(n // 2, n):
                nc.gpsimd.tensor_tensor(y_t[:, t], y_t[:, t], gate_s[:, t], ALU.mult)


def program(nc, io, out):
    count = [0]

    def new(ctx):
        count[0] += 1
        n = count[0]

        def sb(name, shape, dt=F32):
            return ctx.enter_context(nc.sbuf_tensor(f"t{n}_{name}", shape, dt))

        mine = []

        def sem(name):
            mine.append(nc.alloc_semaphore(f"s{n}_{name}"))
            return mine[-1]

        def clear():
            if mine:
                nc.clear_and_free_semaphores(mine)
                nc.all_engine_barrier()

        ctx.callback(clear)

        return sb, sem

    with ExitStack() as whole:
        sb, sem = new(whole)
        da0_dram = nc.dram_tensor("da0_scratch", [B * S // Q0, NH0, Q0], F32).ap()
        da1_dram = nc.dram_tensor("da1_scratch", [NC1 * B, NH1, Q1], F32).ap()
        tot1_dram = nc.dram_tensor("tot1_scratch", [NC1 * B, NH1], F32).ap()
        cw0_dram = nc.dram_tensor("cw0_scratch", [X0, T], F32).ap()
        cw1_dram = nc.dram_tensor("cw1_scratch", [X1, T], F32).ap()
        x_t = sb("x", [P, KH, T])
        xn = sb("xn", [P, KH, T])
        xn_hi, xn_lo = sb("xn_hi", [P, KH, T], F32R), sb("xn_lo", [P, KH, T], F32R)
        ones, ident = sb("ones", [P, P]), sb("ident", [P, P])
        ident_bf, mask_bf = sb("ident_bf", [P, P], BF16), sb("mask_bf", [P, P], BF16)
        mask_f = sb("mask_f", [P, P])
        eps = sb("eps", [P, 2])
        ln1_w, ln2_w = sb("ln1_w", [P, KH]), sb("ln2_w", [P, KH])
        gw0, gw1 = sb("gw0", [P, KH, X0]), sb("gw1", [P, KH, X1])
        lower0, lower1 = sb("lower0", [P, X0, X0]), sb("lower1", [P, X1, X1])
        conv0_b, dt0, d0 = sb("conv0_b", [P, 6]), sb("dt0", [P, 2]), sb("d0", [P, NE0])
        conv1_b, dt1, d1 = sb("conv1_b", [P, 6]), sb("dt1", [P, 2]), sb("d1", [P, NE1])
        norm0_w, norm1_w = sb("norm0_w", [P, NE0]), sb("norm1_w", [P, NE1])
        ld, ready, made_bf = sem("ld"), sem("ready"), sem("made_bf")

        with nc.Block() as block:
            small = [(ident, "ident"), (mask_f, "mask"), (eps, "eps"), (ln1_w, "ln1_w"), (ln2_w, "ln2_w"), (gw0, "gw0"),
                     (gw1, "gw1"), (lower0, "lower0"), (lower1, "lower1"), (conv0_b, "conv0_b"), (dt0, "dt0"), (d0, "d0"),
                     (conv1_b, "conv1_b"), (dt1, "dt1"), (d1, "d1"), (norm0_w, "norm0_w"), (norm1_w, "norm1_w")]

            @block.sync
            def _(sp):
                sp.dma_start(x_t[:], io["x"]).then_inc(ld, 16)
                for tile, name in small[0::2]:
                    sp.dma_start(tile[:], io[name]).then_inc(ready, 16)

            @block.scalar
            def _(act):
                for tile, name in small[1::2]:
                    act.dma_start(tile[:], io[name]).then_inc(ready, 16)

            @block.vector
            def _(dve):
                nc.vector.memset(ones[:], 1.0)
                dve.wait_ge(ready, 16 * len(small))
                nc.vector.tensor_copy(ident_bf[:], ident[:])
                nc.vector.tensor_copy(mask_bf[:], mask_f[:])

            @block.gpsimd
            def _(pool):
                pool.wait_ge(ld, 16)

        ones_, ident_ = ones[:], ident[:]
        norm_phase(nc, new, "n0", x_t, xn, ones_, eps[:, 0:1], True, hi=xn_hi, lo=xn_lo)
        with ExitStack() as layer:
            sbl, _ = new(layer)
            gate_s = sbl("gate_s", [P, NE0, T])
            y_t = sbl("y_t", [P, NE0, T])
            with ExitStack() as mix:
                sbm, _ = new(mix)
                cx = sbm("conv_x", [P, NE0, T])
                conv_x = [cx[:, i] for i in range(NE0)]
                bt, ct = sbm("bt", [N0, T])[:], sbm("ct", [N0, T])[:]
                DT = slice(N0, N0 + NH0)
                dt, cp = sbm("dt", [P, T])[DT, :], sbm("cp", [P, T])[DT, :]
                x_tok, b_tok = sbm("x_tok", [P, TT, E0]), sbm("b_tok", [P, TT, N0])
                dt_tok, cp_tok = sbm("dt_tok", [P, TT, NH0]), sbm("cp_tok", [P, TT, NH0])
                tiles = ([("conv", 8 * P, N0, 4), ("conv", 8 * P + N0, N0 + NH0, 5)] + [("conv", (4 + i) * P, P, i) for i in range(4)]
                         + [("gate", i * P, P, i) for i in range(4)])
                mixer_project(nc, new, "m0", io["in0_w"], io["conv0_w"], xn_hi, xn_lo, conv_x + [bt, ct], gate_s, dt, cp,
                              (5, DT, None), tiles, (1.0, 1.0), dt0, conv0_b, da0_dram, Q0, lambda ap: ap.rearrange("p (b s) -> p b s", b=B))
                turn_phase(nc, new, "t0", conv_x, bt, dt, cp, DT, x_tok, b_tok, dt_tok, cp_tok, ident_)
                scan0_phase(nc, new, conv_x, bt, ct, x_tok, b_tok, dt_tok, cp_tok, da0_dram, io["delta0"], d0, gate_s, y_t, ident_)
            gate_phase(nc, y_t, gate_s, NE0)
            norm_phase(nc, new, "g0", y_t, y_t, ones_, eps[:, 1:2], False, weight=norm0_w)
            mixer_out_phase(nc, new, "o0", y_t, io["out0_w"], [x_t], x_t)
        with ExitStack() as layer:
            sbl, _ = new(layer)
            attn_t = sbl("attn_t", [P, KH, T])
            with ExitStack() as att:
                sba, _ = new(att)
                hn = sba("hn", [P, KH, T])
                hn_hi, hn_lo = sba("hn_hi", [P, KH, T], F32R), sba("hn_lo", [P, KH, T], F32R)
                kz, v_tok = sba("kz", [P, 2, KT, T]), sba("v_tok", [P, TT, NKV * D])
                norm_phase(nc, new, "n1", xn, hn, ones_, eps[:, 0:1], False, weight=ln1_w, hi=hn_hi, lo=hn_lo)
                keys_values_phase(nc, new, io, hn_hi, hn_lo, kz, v_tok)
                attention_phase(nc, new, io, hn_hi, hn_lo, kz, v_tok, attn_t, ident_, ident_bf[:], mask_bf[:])
            add_phase(nc, new, attn_t, attn_t, xn)
            norm_phase(nc, new, "n2", attn_t, xn, ones_, eps[:, 0:1], False, weight=ln2_w, hi=xn_hi, lo=xn_lo)
            router_phase(nc, new, "r0", xn, gw0, lower0[:], cw0_dram, ident_, X0, TOP0, True)
            moe_t = sbl("moe_t", [P, KH, T])
            experts0_phase(nc, new, io, xn_hi, xn_lo, cw0_dram, moe_t)
            add_phase(nc, new, x_t, x_t, attn_t)
            add_phase(nc, new, x_t, x_t, moe_t)
        norm_phase(nc, new, "n3", x_t, xn, ones_, eps[:, 0:1], True, hi=xn_hi, lo=xn_lo)
        with ExitStack() as layer:
            sbl, _ = new(layer)
            gate_s = sbl("gate_s", [P, NE1, T])
            y_t = sbl("y_t", [P, NE1, T])
            with ExitStack() as mix:
                sbm, _ = new(mix)
                cx = sbm("conv_x", [P, NE1, T])
                conv_x = [cx[:, i] for i in range(NE1)]
                bt, ct = sbm("bt", [N1, T])[:], sbm("ct", [N1, T])[:]
                DT = slice(0, NH1)
                dt, cp = sbm("dt", [P, T])[DT, :], sbm("cp", [P, T])[DT, :]
                x_tok, b_tok = sbm("x_tok", [P, TT, E1]), sbm("b_tok", [P, TT, N1])
                dt_tok, cp_tok = sbm("dt_tok", [P, TT, NH1]), sbm("cp_tok", [P, TT, NH1])
                tiles = ([("conv", 10 * P, NH1, -1)] + [("conv", (4 + i) * P, P, i) for i in range(6)]
                         + [("gate", i * P, P, i) for i in range(4)])
                by_chunk = lambda ap: ap.rearrange("p (c b l) -> p b c l", b=B, l=Q1)
                mixer_project(nc, new, "m1", io["in1_w"], io["conv1_w"], xn_hi, xn_lo, conv_x + [bt, ct], gate_s, dt, cp,
                              (-1, DT, lambda ap, hf: by_chunk(ap)[:, 2 * hf:2 * hf + 2]), tiles, (0.25, 0.5), dt1, conv1_b,
                              da1_dram, Q1, by_chunk)
                turn_phase(nc, new, "t1", conv_x, bt, dt, cp, DT, x_tok, b_tok, dt_tok, cp_tok, ident_)
                scan1_phase(nc, new, conv_x, bt, ct, x_tok, b_tok, dt_tok, cp_tok, da1_dram, tot1_dram, io["delta1"], d1, y_t, ident_)
            norm_phase(nc, new, "g1", y_t, y_t, ones_, eps[:, 0:1], False, weight=norm1_w)
            gate_phase(nc, y_t, gate_s, NE1)
            mixer_out_phase(nc, new, "o1", y_t, io["out1_w"], [x_t], x_t)
        with ExitStack() as layer:
            sbl, _ = new(layer)
            router_phase(nc, new, "r1", xn, gw1, lower1[:], cw1_dram, ident_, X1, TOP1, False)
            moe_t = sbl("moe_t", [P, KH, T])
            experts1_phase(nc, new, io, xn_hi, xn_lo, cw1_dram, moe_t)
            add_phase(nc, new, x_t, x_t, moe_t)
        stored = sem("stored")
        with nc.Block() as block:
            @block.sync
            def _(sp):
                sp.dma_start(out, x_t[:]).then_inc(stored, 16)
                sp.wait_ge(stored, 16)


def add_phase(nc, new, dst, a, b):
    with nc.Block() as block:
        @block.vector
        def _(dve):
            nc.vector.tensor_tensor(dst[:], a[:], b[:], ALU.add)


def layout(inputs):
    f32 = np.float32
    g = {k: np.asarray(v) for k, v in inputs.items()}

    def col(v, n):
        return np.ascontiguousarray(v.reshape(n, P).T)

    def kpn(w):
        return np.ascontiguousarray(w.reshape(KH, P, -1).transpose(1, 0, 2))

    a = {}
    a["x"] = np.ascontiguousarray(g["L0_attn_x"].reshape(T, KH, P).transpose(2, 1, 0))
    a["in0_w"] = np.ascontiguousarray(g["L0_attn_in_proj_w"].T)
    a["in1_w"] = np.ascontiguousarray(g["L1_attn_in_proj_w"])
    a["out0_w"] = np.ascontiguousarray(g["L0_attn_out_proj_w"].T)
    a["out1_w"] = np.ascontiguousarray(g["L1_attn_out_proj_w"])
    a["wk"], a["wv"] = np.ascontiguousarray(g["L0_ffn_wk"]), np.ascontiguousarray(g["L0_ffn_wv"])
    for n, (w, b, N) in enumerate(((g["L0_attn_conv_w"], g["L0_attn_conv_b"], N0), (g["L1_attn_conv_w"], g["L1_attn_conv_b"], N1))):
        cw, cb = np.zeros((P, 6, KCONV), f32), np.zeros((P, 6), f32)
        for i in range(4):
            cw[:, i], cb[:, i] = w[i * P:(i + 1) * P], b[i * P:(i + 1) * P]
        for i in range(2):
            cw[0:N, 4 + i], cb[0:N, 4 + i] = w[512 + i * N:512 + (i + 1) * N], b[512 + i * N:512 + (i + 1) * N]
        a[f"conv{n}_w"], a[f"conv{n}_b"] = cw, cb
    dt0, dt1 = np.zeros((P, 2), f32), np.zeros((P, 2), f32)
    dt0[N0:N0 + NH0, 0], dt0[N0:N0 + NH0, 1] = g["L0_attn_dt_bias"], g["L0_attn_A_log"]
    dt1[0:NH1, 0], dt1[0:NH1, 1] = g["L1_attn_dt_bias"], g["L1_attn_A_log"]
    a["dt0"], a["dt1"] = dt0, dt1
    a["d0"] = col(np.repeat(g["L0_attn_D"], P0), NE0)
    a["d1"] = col(np.repeat(g["L1_attn_D"], P1), NE1)
    a["norm0_w"], a["norm1_w"] = col(g["L0_attn_norm_w"], NE0), col(g["L1_attn_norm_w"], NE1)
    a["ln1_w"], a["ln2_w"] = col(g["L0_ffn_ln1_w"], KH), col(g["L0_ffn_ln2_w"], KH)
    a["gw0"], a["gw1"] = kpn(g["L0_ffn_gate_w"]), kpn(np.ascontiguousarray(g["L1_ffn_gate_w"].T))
    order = [(2 * m + r) * (NHQ // NKV) + i for m in range(KT) for i in range(4) for r in range(2)]
    wq = g["L0_ffn_wq"].reshape(KH, P, NHQ, D)[:, :, order].reshape(KH, P, QT, P)
    a["wq_tiles"] = np.ascontiguousarray(wq.transpose(2, 1, 0, 3))
    a["wo_tiles"] = np.ascontiguousarray(g["L0_ffn_wo"].reshape(NHQ, D, H)[order].reshape(QT, P, H))
    w1 = g["L0_ffn_w1"].reshape(X0, KH, P, FT0, P).transpose(0, 3, 2, 1, 4).reshape(X0 * FT0, P, H)
    w3 = g["L0_ffn_w3"].reshape(X0, KH, P, FT0, P).transpose(0, 3, 2, 1, 4).reshape(X0 * FT0, P, H)
    w2 = g["L0_ffn_w2"].reshape(X0 * FT0, P, H)
    a["x0_w"] = np.ascontiguousarray(np.stack([w1, w3, w2], axis=2))
    wg = g["L1_ffn_w_gate"].reshape(FT1, P, KH, P).transpose(0, 3, 2, 1).reshape(FT1, P, H)
    wu = g["L1_ffn_w_up"].reshape(FT1, P, KH, P).transpose(0, 3, 2, 1).reshape(FT1, P, H)
    wd = g["L1_ffn_w_down"].transpose(0, 2, 1).reshape(FT1, P, H)
    a["x1_w"] = np.ascontiguousarray(np.stack([wg, wu, wd], axis=2))
    a["ident"] = np.eye(P, dtype=f32)
    a["mask"] = np.where(np.arange(P)[None, :] > np.arange(P)[:, None], f32(NEG_MASK), f32(0)).astype(f32)
    a["eps"] = np.tile(np.array([[1e-5, 1e-6]], f32), (P, 1))
    a["lower0"] = np.tile(np.tril(np.ones((X0, X0), f32), -1)[None], (P, 1, 1))
    a["lower1"] = np.tile(np.tril(np.ones((X1, X1), f32), -1)[None], (P, 1, 1))
    a["delta0"] = np.tile(np.eye(Q0, dtype=f32), (1, NH0))
    a["delta1"] = np.tile(np.eye(Q1, dtype=f32), (B, NH1))
    return a


def build(nc, arrays):
    io = {k: nc.dram_tensor(f"in_{k}", v.shape, mybir.dt.from_np(v.dtype), kind="ExternalInput").ap() for k, v in arrays.items()}
    out = nc.dram_tensor("out_x", (P, KH, T), F32, kind="ExternalOutput").ap()
    program(nc, io, out)


def kernel(**inputs):
    import concourse.bacc as bacc
    from concourse.bass_utils import run_bass_kernel_spmd

    arrays = layout(inputs)
    nc = bacc.Bacc("TRN2", target_bir_lowering=False, num_devices=1)
    build(nc, arrays)
    r = run_bass_kernel_spmd(nc, [{f"in_{k}": v for k, v in arrays.items()}], core_ids=[0])
    y = r.results[0]["out_x"]
    return np.ascontiguousarray(y.transpose(2, 1, 0)).reshape(B, S, H)
```

```python
from contextlib import ExitStack

import numpy as np
import concourse.bass as bass
from concourse import mybir
from concourse.alu_op_type import AluOpType as ALU

F32 = mybir.dt.float32
F32R = mybir.dt.float32r
BF16 = mybir.dt.bfloat16
ACT = mybir.ActivationFunctionType
X = mybir.AxisListType.X

P = 128
B, S, H = 4, 256, 256
T = B * S
KH = H // P
HALF = 512
NHALF = T // HALF
TT = T // P

E0, N0, NH0, P0, Q0 = 512, 64, 8, 64, 128
NE0 = E0 // P
KCONV = 4
NHQ, NKV, D = 32, 8, 64
QT = NHQ * D // P
KT = NKV * D // P
X0, F0, TOP0 = 8, 1024, 2
FT0 = F0 // P
E1, N1, NH1, P1, Q1 = 512, 128, 64, 8, 32
NE1 = E1 // P
NC1 = S // Q1
X1, F1, TOP1 = 16, 176, 6
FT1 = X1 * F1 // P
NEG_MASK = -3.0e38

SMALL = [("ident", P), ("mask", P), ("eps", 2), ("ln1_w", KH), ("ln2_w", KH), ("gw0", KH * X0), ("gw1", KH * X1),
         ("lower0", X0 * X0), ("lower1", X1 * X1), ("conv0_b", 6), ("dt0", 2), ("d0", NE0), ("conv1_b", 6), ("dt1", 2),
         ("d1", NE1), ("norm0_w", NE0), ("norm1_w", NE1), ("delta1", Q1)]


def half(hf):
    return slice(hf * HALF, (hf + 1) * HALF)


def turns(eng, n):
    yield 0, True, False
    with eng.Fori(1, n - 1) as i:
        yield i, False, False
    yield n - 1, False, True


def wait_after(eng, sem, n):
    if not (isinstance(n, int) and n <= 0):
        eng.wait_ge(sem, n)


def product3(nc, out, w_hi, w_lo, x_hi, x_lo, start, stop):
    nc.tensor.matmul(out, w_hi, x_hi, start=start, stop=False)
    nc.tensor.matmul(out, w_hi, x_lo, start=False, stop=False)
    return nc.tensor.matmul(out, w_lo, x_hi, start=False, stop=stop)
def norm_phase(nc, new, name, src, dst, ones, ident, eps, centred, hi, lo, weight=None, ahead=(), second=None):
    n = src.shape[1]
    assert n == 2
    width = n * P
    NT = TT // NHALF
    with ExitStack() as ctx:
        sb, sem = new(ctx)
        xc = sb("xc", [P, n, T]) if centred else src
        sq = sb("sq", [P, n, T])
        pair = sb("pair", [P, T]) if centred else None
        std, rstd = sb("std", [P, TT]), sb("rstd", [P, TT])
        diagonal = sb("diagonal", [P, TT, P])
        if second:
            weight2, hi2, lo2 = second
            ms2, std2, rstd2, factor2 = (sb(s, [P, TT]) for s in ("ms2", "std2", "rstd2", "factor2"))
            diagonal2, dst2 = sb("diagonal2", [P, TT, P]), sb("dst2", [P, n, T])
        ps_mean = ctx.enter_context(nc.psum_tensor(name + "_ps_mean", [P, NHALF, HALF], F32))
        ps_sq = ctx.enter_context(nc.psum_tensor(name + "_ps_sq", [P, NHALF, HALF], F32))
        ps_r = ctx.enter_context(nc.psum_tensor(name + "_ps_r", [P, NHALF, HALF], F32))
        paired, squares_paired, sums, centre, squared, sq_sums, stds, rstds, diagonals, spread, normed, his, los = (
            sem(s) for s in ("paired", "squares_paired", "sums", "centre", "squared", "sq_sums", "stds", "rstds", "diagonals", "spread", "normed", "his", "los"))
        partial2, ms2_made, stds2, rstds2, factors2, diagonals2, spread2, normed2, his2, los2 = (
            sem(s) for s in ("partial2", "ms2_made", "stds2", "rstds2", "factors2", "diagonals2", "spread2", "normed2", "his2", "los2"))
        ahead_loaded, ahead_his = [sem(f"ahead_loaded{i}") for i in range(len(ahead))], [sem(f"ahead_his{i}") for i in range(len(ahead))]
        nc.scalar.preload_act_table(ACT.Sqrt)
        block = ctx.enter_context(nc.Block())

        @block.sync
        def _(sp):
            for i, w in enumerate(ahead):
                load_and_split(nc, w, sp=sp, loaded=ahead_loaded[i])

        @block.tensor
        def _(pe):
            if centred:
                for hf in range(NHALF):
                    pe.wait_ge(paired, hf + 1)
                    nc.tensor.matmul(ps_mean[:, hf], ones, pair[:, half(hf)], start=True, stop=True).then_inc(sums, 1)
            for hf in range(NHALF):
                pe.wait_ge(squares_paired, hf + 1)
                for t in range(NT):
                    tok = slice((hf * NT + t) * P, (hf * NT + t + 1) * P)
                    mm = nc.tensor.matmul(ps_sq[:, hf, t:t + 1], sq[:, 0, tok], ones[:, 0:1], start=True, stop=True)
                mm.then_inc(sq_sums, 1)
            for hf in range(NHALF):
                pe.wait_ge(diagonals, hf + 1)
                nc.tensor.matmul(ps_r[:, hf], ones, diagonal[:, hf * NT:(hf + 1) * NT].rearrange("p t c -> p (t c)"),
                                 start=True, stop=True).then_inc(spread, 1)
            if second:
                for hf in range(NHALF):
                    pe.wait_ge(centre, NHALF)
                    pe.wait_ge(diagonals2, hf + 1)
                    nc.tensor.matmul(ps_mean[:, hf], ones, diagonal2[:, hf * NT:(hf + 1) * NT].rearrange("p t c -> p (t c)"),
                                     start=True, stop=True).then_inc(spread2, 1)

        @block.scalar
        def _(act):
            for hf in range(NHALF):
                if centred:
                    act.wait_ge(centre, hf + 1)
                nc.scalar.activation(sq[:, :, half(hf)], xc[:, :, half(hf)], ACT.Square).then_inc(squared, 1)
            for i, w in enumerate(ahead):
                load_and_split(nc, w, act=act, loaded=ahead_loaded[i], his=ahead_his[i])
            for hf in range(NHALF):
                act.wait_ge(sq_sums, hf + 1)
                nc.scalar.activation(std[:, hf * NT:(hf + 1) * NT], ps_sq[:, hf, 0:NT], ACT.Sqrt, bias=eps, scale=1.0 / width).then_inc(stds, 1)
            if second:
                for hf in range(NHALF):
                    part = slice(hf * NT, (hf + 1) * NT)
                    act.wait_ge(ms2_made, hf + 1)
                    nc.scalar.activation(std2[:, part], ms2[:, part], ACT.Sqrt, bias=eps).then_inc(stds2, 1)
            for hf in range(NHALF):
                act.wait_ge(normed, hf + 1)
                nc.scalar.activation(hi[:, :, half(hf)], dst[:, :, half(hf)], ACT.Copy).then_inc(his, 1)
            if second:
                for hf in range(NHALF):
                    act.wait_ge(normed2, hf + 1)
                    nc.scalar.activation(hi2[:, :, half(hf)], dst2[:, :, half(hf)], ACT.Copy).then_inc(his2, 1)

        def split_lo(engine, eng, hf):
            eng.wait_ge(his, hf + 1)
            engine.tensor_tensor(lo[:, :, half(hf)], dst[:, :, half(hf)], hi[:, :, half(hf)].bitcast(F32), ALU.subtract).then_inc(los, 1)

        def split_lo2(engine, eng, hf):
            eng.wait_ge(his2, hf + 1)
            engine.tensor_tensor(lo2[:, :, half(hf)], dst2[:, :, half(hf)], hi2[:, :, half(hf)].bitcast(F32), ALU.subtract).then_inc(los2, 1)

        @block.gpsimd
        def _(pool):
            for i, w in enumerate(ahead):
                load_and_split(nc, w, pool=pool, his=ahead_his[i])
            split_lo(nc.gpsimd, pool, 0)
            if second:
                split_lo2(nc.gpsimd, pool, 0)

        @block.vector
        def _(dve):
            def pair_squares(hf):
                dve.wait_ge(squared, hf + 1)
                nc.vector.tensor_tensor(sq[:, 0, half(hf)], sq[:, 0, half(hf)], sq[:, 1, half(hf)], ALU.add).then_inc(squares_paired, 1)

            if centred:
                for hf in range(NHALF):
                    nc.vector.tensor_tensor(pair[:, half(hf)], src[:, 0, half(hf)], src[:, 1, half(hf)], ALU.add).then_inc(paired, 1)
                for hf in range(NHALF):
                    dve.wait_ge(sums, hf + 1)
                    for k in range(n):
                        op = nc.vector.scalar_tensor_tensor(out=xc[:, k, half(hf)], in0=ps_mean[:, hf], scalar=-1.0 / width,
                                                            in1=src[:, k, half(hf)], op0=ALU.mult, op1=ALU.add)
                    op.then_inc(centre, 1)
            for hf in range(NHALF):
                pair_squares(hf)
            for hf in range(NHALF):
                part = slice(hf * NT, (hf + 1) * NT)
                dve.wait_ge(stds, hf + 1)
                nc.vector.reciprocal(rstd[:, part], std[:, part]).then_inc(rstds, 1)
                dve.wait_ge(rstds, hf + 1)
                nc.vector.tensor_tensor(diagonal[:, part], ident.unsqueeze(1).to_broadcast([P, NT, P]),
                                        rstd[:, part].unsqueeze(2).to_broadcast([P, NT, P]), ALU.mult).then_inc(diagonals, 1)
                if second:
                    nc.vector.scalar_tensor_tensor(out=ms2[:, part], in0=ps_sq[:, hf, 0:NT], scalar=1.0 / width, in1=rstd[:, part],
                                                   op0=ALU.mult, op1=ALU.mult).then_inc(partial2, 1)
                    dve.wait_ge(partial2, hf + 1)
                    nc.vector.tensor_tensor(ms2[:, part], ms2[:, part], rstd[:, part], ALU.mult).then_inc(ms2_made, 1)
            if second:
                for hf in range(NHALF):
                    part = slice(hf * NT, (hf + 1) * NT)
                    dve.wait_ge(stds2, hf + 1)
                    nc.vector.reciprocal(rstd2[:, part], std2[:, part]).then_inc(rstds2, 1)
                    dve.wait_ge(rstds2, hf + 1)
                    nc.vector.tensor_tensor(factor2[:, part], rstd[:, part], rstd2[:, part], ALU.mult).then_inc(factors2, 1)
                    dve.wait_ge(factors2, hf + 1)
                    nc.vector.tensor_tensor(diagonal2[:, part], ident.unsqueeze(1).to_broadcast([P, NT, P]),
                                            factor2[:, part].unsqueeze(2).to_broadcast([P, NT, P]), ALU.mult).then_inc(diagonals2, 1)
            if centred:
                dve.wait_ge(centre, NHALF)
            for hf in range(NHALF):
                dve.wait_ge(spread, hf + 1)
                for k in range(n):
                    if weight is None:
                        op = nc.vector.tensor_tensor(dst[:, k, half(hf)], xc[:, k, half(hf)], ps_r[:, hf], ALU.mult)
                    else:
                        op = nc.vector.scalar_tensor_tensor(out=dst[:, k, half(hf)], in0=xc[:, k, half(hf)],
                                                            scalar=weight[:, k:k + 1], in1=ps_r[:, hf],
                                                            op0=ALU.mult, op1=ALU.mult)
                op.then_inc(normed, 1)
            if second:
                for hf in range(NHALF):
                    dve.wait_ge(spread2, hf + 1)
                    for k in range(n):
                        op = nc.vector.scalar_tensor_tensor(out=dst2[:, k, half(hf)], in0=xc[:, k, half(hf)], scalar=weight2[:, k:k + 1],
                                                            in1=ps_mean[:, hf], op0=ALU.mult, op1=ALU.mult)
                    op.then_inc(normed2, 1)
            split_lo(nc.vector, dve, 1)
            if second:
                split_lo2(nc.vector, dve, 1)
def load_and_split(nc, w, sp=None, act=None, pool=None, loaded=None, his=None):
    w_dram, raw, hi, lo = w
    if sp:
        sp.dma_start(raw, w_dram.rearrange("(k p) n -> p k n", p=P)).then_inc(loaded, 16)
    if act:
        act.wait_ge(loaded, 16)
        nc.scalar.activation(hi[:], raw, ACT.Copy).then_inc(his, 1)
    if pool:
        pool.wait_ge(his, 1)
        nc.gpsimd.tensor_tensor(lo[:], raw, hi[:].bitcast(F32), ALU.subtract)


def mixer_project(nc, new, name, w_hi, w_lo, cw_dram, xn_hi, xn_lo, conv_outs, gate_s, dt, cp, dt_rows, tiles, mup, dcol, bias_col,
                  da_dram, Q, store, router_operands=None):
    dt_tile, DT, dt_alone = dt_rows
    nconv = len(conv_outs)
    with ExitStack() as ctx:
        sb, sem = new(ctx)
        padded = sb("padded", [P, nconv, B, KCONV - 1 + S])
        acc = sb("acc", [P, 2, B, S])
        cw, cw_last = sb("cw", [P, nconv, KCONV]), sb("cw_last", [P, nconv])
        dt_x, dt_a, dt_e, dt_u, dt_l = (sb(s, [P, T])[DT, :] for s in ("dt_x", "dt_a", "dt_e", "dt_u", "dt_l"))
        decay, starts = dt_a, dt_l
        acol = sb("acol", [P, 3])
        router = router_operands and Router(nc, ctx, new, *router_operands)
        BANKS = 6 if router else 8
        ps = ctx.enter_context(nc.psum_tensor(name + "_ps", [P, BANKS, HALF], F32))
        (loaded, cw_ready, projected, conv_took, gate_took, dt_took, pads, taps, silued, magnitude, exped, summed, logged, rest,
         corrected, dt_ready, a_capped, a_exp, a_ready, exponents, decays, cleared, copied, zeroed, cps, sent) = (sem(s) for s in (
            "loaded", "cw_ready", "projected", "conv_took", "gate_took", "dt_took", "pads", "taps", "silued", "magnitude", "exped",
            "summed", "logged", "rest", "corrected", "dt_ready", "a_capped", "a_exp", "a_ready", "exponents", "decays", "cleared",
            "copied", "zeroed", "cps", "sent"))
        block = ctx.enter_context(nc.Block())
        blocks = [(kind, c0, m, i, hf) for kind, c0, m, i in tiles for hf in range(NHALF)]
        convs = [i for kind, _, _, i in tiles if kind == "conv"]
        by_chunk = lambda ap: ap.rearrange("h (c l) -> h c l", l=Q)

        def block_of(kind, i, hf):
            return [(b[0], b[3], b[4]) for b in blocks].index((kind, i, hf)) + 1

        def readers(n):
            kind, _, _, i, hf = blocks[n]
            same = sum(1 for b in blocks[:n + 1] if b[0] == kind)
            out = [] if kind == "dt" else [(conv_took if kind == "conv" else gate_took, same)]
            return out + ([(dt_took, hf + 1)] if i == dt_tile and kind != "gate" else [])

        @block.sync
        def _(sp):
            sp.dma_start(cw[:], cw_dram).then_inc(loaded, 16)
            sp.wait_ge(zeroed, 1)
            sp.dma_start(da_dram.rearrange("c h l -> h c l"), by_chunk(decay)).then_inc(sent, 16)
            if router:
                router.sp(sp)
            sp.wait_ge(sent, 16)

        @block.gpsimd
        def _(pool):
            nc.gpsimd.memset(padded[:, :, :, 0:KCONV - 1], 0.0).then_inc(pads, 1)
            pool.wait_ge(rest, 1)
            pool.wait_ge(logged, 1)
            nc.gpsimd.tensor_tensor(dt_l, dt_l, dt_u, ALU.subtract).then_inc(corrected, 1)
            pool.wait_ge(dt_ready, 1)
            nc.gpsimd.memset(starts, 0.0).then_inc(cleared, 1)
            pool.wait_ge(cleared, 1)
            pool.wait_ge(decays, 1)
            nc.gpsimd.tensor_copy(by_chunk(starts)[:, :, 0:1], by_chunk(decay)[:, :, 0:1]).then_inc(copied, 1)
            pool.wait_ge(copied, 1)
            nc.gpsimd.memset(by_chunk(decay)[:, :, 0:1], 0.0).then_inc(zeroed, 1)
            if router:
                pool.wait_ge(zeroed, 1)
                router.pool(pool)

        @block.tensor
        def _(pe):
            for n, (kind, c0, m, i, hf) in enumerate(blocks):
                f = slice(c0, c0 + m)
                if router and n == 4:
                    router.pe_1(pe)
                if n >= BANKS:
                    for semaphore, count in readers(n - BANKS):
                        pe.wait_ge(semaphore, count)
                for k in range(KH):
                    mm = product3(nc, ps[0:m, n % BANKS], w_hi[:, k, f], w_lo[:, k, f],
                                  xn_hi[:, k, half(hf)], xn_lo[:, k, half(hf)], k == 0, k == KH - 1)
                mm.then_inc(projected, 1)
            if router:
                router.pe_2(pe)

        @block.scalar
        def _(act):
            def take_conv(j):
                i = convs[j]
                mc = conv_outs[i].shape[0]
                for hf in range(NHALF):
                    n = block_of("conv", i, hf)
                    act.wait_ge(projected, n)
                    src = ps[0:mc, (n - 1) % BANKS].rearrange("p (b s) -> p b s", b=2)
                    nc.scalar.activation(padded[0:mc, i, 2 * hf:2 * hf + 2, KCONV - 1:], src, ACT.Copy, scale=mup[1])
                    if j >= 2:
                        act.wait_ge(silued, j - 1)
                    nc.scalar.activation(acc[0:mc, j % 2, 2 * hf:2 * hf + 2], src, ACT.Identity, scale=cw_last[0:mc, i:i + 1],
                                         bias=bias_col[0:mc, i:i + 1]).then_inc(conv_took, 1)

            def silu(j):
                i = convs[j]
                mc = conv_outs[i].shape[0]
                act.wait_ge(taps, (KCONV - 1) * (j + 1))
                nc.scalar.activation(store(conv_outs[i]), acc[0:mc, j % 2], ACT.Silu).then_inc(silued, 1)

            def gates(i):
                for hf in range(NHALF):
                    n = block_of("gate", i, hf)
                    act.wait_ge(projected, n)
                    nc.scalar.activation(gate_s[:, i, half(hf)], ps[:, (n - 1) % BANKS], ACT.Silu, scale=mup[0]).then_inc(gate_took, 1)

            act.wait_ge(a_capped, 1)
            nc.scalar.activation(acol[DT, 1:2], acol[DT, 0:1], ACT.Exp).then_inc(a_exp, 1)
            act.wait_ge(cw_ready, 1)
            take_conv(0)
            act.wait_ge(magnitude, 1)
            nc.scalar.activation(dt_e, dt_a, ACT.Exp, scale=-1.0).then_inc(exped, 1)
            take_conv(1)
            act.wait_ge(summed, 1)
            nc.scalar.activation(dt_l, dt_u, ACT.Ln).then_inc(logged, 1)
            silu(0)
            take_conv(2)
            gates(0)
            silu(1)
            if router:
                router.act_1(act)
            take_conv(3)
            gates(1)
            act.wait_ge(exponents, 1)
            nc.scalar.activation(decay, decay, ACT.Exp).then_inc(decays, 1)
            silu(2)
            take_conv(4)
            gates(2)
            silu(3)
            take_conv(5)
            gates(3)
            silu(4)
            if router:
                router.act_2(act)
            silu(5)

        @block.vector
        def _(dve):
            done = [0]

            def convolve(j):
                i = convs[j]
                mc = conv_outs[i].shape[0]
                dve.wait_ge(conv_took, 2 * (j + 1))
                for k in range(KCONV - 1):
                    if k:
                        dve.wait_ge(taps, done[0])
                    nc.vector.scalar_tensor_tensor(out=acc[0:mc, j % 2], in0=padded[0:mc, i, :, k:k + S], scalar=cw[0:mc, i, k:k + 1],
                                                   in1=acc[0:mc, j % 2], op0=ALU.mult, op1=ALU.add).then_inc(taps, 1)
                    done[0] += 1

            nc.vector.tensor_scalar(acol[DT, 0:1], dcol[DT, 1:2], 88.0, None, ALU.min).then_inc(a_capped, 1)
            dve.wait_ge(loaded, 16)
            nc.vector.tensor_scalar(cw_last[:], cw[:, :, KCONV - 1], mup[1], None, ALU.mult).then_inc(cw_ready, 1)
            for hf in range(NHALF):
                n = block_of("conv" if dt_alone is None else "dt", dt_tile, hf)
                dve.wait_ge(projected, n)
                src = ps[DT, (n - 1) % BANKS]
                dst = dt_x[:, half(hf)] if dt_alone is None else dt_alone(dt_x, hf)
                src = src if dt_alone is None else src.rearrange("p (b c l) -> p b c l", b=2, l=Q)
                nc.vector.tensor_scalar(dst, src, dcol[DT, 0:1], None, ALU.add).then_inc(dt_took, 1)
            dve.wait_ge(dt_took, NHALF)
            nc.vector.scalar_tensor_tensor(out=dt_a, in0=dt_x, scalar=-1.0, in1=dt_x, op0=ALU.mult, op1=ALU.max).then_inc(magnitude, 1)
            dve.wait_ge(pads, 1)
            convolve(0)
            dve.wait_ge(exped, 1)
            nc.vector.tensor_scalar(dt_u, dt_e, 1.0, None, ALU.add).then_inc(summed, 1)
            convolve(1)
            dve.wait_ge(logged, 1)
            nc.vector.scalar_tensor_tensor(out=dt_u, in0=dt_u, scalar=-1.0, in1=dt_e, op0=ALU.add, op1=ALU.subtract).then_inc(rest, 1)
            dve.wait_ge(a_exp, 1)
            nc.vector.tensor_scalar(acol[DT, 2:3], acol[DT, 1:2], -1.0, None, ALU.mult).then_inc(a_ready, 1)
            if router:
                router.dve_1(dve)
            convolve(2)
            dve.wait_ge(corrected, 1)
            nc.vector.scalar_tensor_tensor(out=dt, in0=dt_x, scalar=0.0, in1=dt_l, op0=ALU.max, op1=ALU.add).then_inc(dt_ready, 1)
            dve.wait_ge(a_ready, 1)
            dve.wait_ge(dt_ready, 1)
            nc.vector.tensor_scalar(decay, dt, acol[DT, 2:3], -200.0, ALU.mult, ALU.max).then_inc(exponents, 1)
            if router:
                router.dve_2(dve)
            convolve(3)
            convolve(4)
            dve.wait_ge(zeroed, 1)
            nc.vector.tensor_tensor_scan(cp, decay, starts, 0.0, ALU.mult, ALU.add).then_inc(cps, 1)
            if router:
                router.dve_3(dve)
            convolve(5)
def turn_phase(nc, new, name, conv_x, bt, dt, cp, DT, x_tok, b_tok, dt_tok, cp_tok, ident, w_dram, raw, addends=None):
    n, nh = bt.shape[0], DT.stop - DT.start
    with ExitStack() as ctx:
        sb, sem = new(ctx)
        ps_x = ctx.enter_context(nc.psum_tensor(name + "_ps_x", [P, 2, HALF], F32))
        ps_b = ctx.enter_context(nc.psum_tensor(name + "_ps_b", [P, 2, HALF], F32))
        x_turned, b_turned, x_copied, b_copied, loaded = (sem(s) for s in ("x_turned", "b_turned", "x_copied", "b_copied", "loaded"))
        block = ctx.enter_context(nc.Block())

        @block.sync
        def _(sp):
            for j in range(2):
                sp.dma_start(raw[0][:, j], w_dram[j, :, 0:2]).then_inc(loaded, 16)
                sp.dma_start(raw[1][:, j], w_dram[j, :, 2]).then_inc(loaded, 16)
            sp.wait_ge(loaded, 64)

        @block.gpsimd
        def _(pool):
            if addends:
                a, b = addends
                nc.gpsimd.tensor_tensor(a[:], a[:], b[:], ALU.add)

        @block.tensor
        def _(pe):
            for t in range(TT):
                tok = slice(t * P, (t + 1) * P)
                if t >= 2:
                    wait_after(pe, x_copied, t - 1)
                for c in range(len(conv_x)):
                    mm = nc.tensor.transpose(ps_x[:, t % 2, c * P:(c + 1) * P], conv_x[c][:, tok], ident)
                mm.then_inc(x_turned, 1)
                if t >= 2:
                    wait_after(pe, b_copied, t - 1)
                o = ps_b[:, t % 2]
                nc.tensor.transpose(o[:, 0:n], bt[:, tok], ident[0:n, 0:n])
                nc.tensor.transpose(o[:, n:n + nh], dt[:, tok], ident[DT, DT])
                nc.tensor.transpose(o[:, n + nh:n + 2 * nh], cp[:, tok], ident[DT, DT]).then_inc(b_turned, 1)

        @block.scalar
        def _(act):
            for t in range(TT):
                act.wait_ge(x_turned, t + 1)
                nc.scalar.activation(x_tok[:, t, :], ps_x[:, t % 2], ACT.Copy).then_inc(x_copied, 1)

        @block.vector
        def _(dve):
            for t in range(TT):
                dve.wait_ge(b_turned, t + 1)
                o = ps_b[:, t % 2]
                nc.vector.tensor_copy(b_tok[:, t, :], o[:, 0:n])
                nc.vector.tensor_copy(dt_tok[:, t, :], o[:, n:n + nh])
                nc.vector.tensor_copy(cp_tok[:, t, :], o[:, n + nh:n + 2 * nh]).then_inc(b_copied, 1)


class Scan0:

    def __init__(self, nc, ctx, new, conv_x, bt, ct, x_tok, b_tok, dt_tok, cp_tok, da_dram, d_col, y_t, ident):
        sb, sem = new(ctx)
        self.nc, self.conv_x, self.bt, self.ct, self.x_tok, self.b_tok, self.dt_tok, self.cp_tok = nc, conv_x, bt, ct, x_tok, b_tok, dt_tok, cp_tok
        self.da_dram, self.d_col, self.y_t, self.ident = da_dram, d_col, y_t, ident
        self.delta, self.da = sb("delta", [P, NH0 * Q0]), sb("da", [P, NH0 * Q0])
        self.bts, self.cts, self.bs = sb("bts", [N0, Q0]), sb("cts", [N0, Q0]), sb("bs", [P, N0])
        self.m = sb("m", [P, NH0, Q0])
        self.xd, self.xdec = sb("xd", [P, NH0, P0]), sb("xdec", [P, NH0, P0])
        self.state = sb("state", [N0, E0])
        self.through, self.y_tok = sb("through", [P, E0]), sb("y_tok", [P, E0])
        self.ps = ctx.enter_context(nc.psum_tensor("s0_ps", [P, 2, HALF], F32))
        (self.delta_made, self.ld_da, self.staged, self.g_made, self.scanned, self.m_made, self.xd_made, self.xdec_made, self.y_made,
         self.s_made, self.s_kept, self.o_made, self.o_scaled, self.y_kept, self.turned, self.y_out) = (sem(s) for s in (
            "delta_made", "ld_da", "staged", "g_made", "scanned", "m_made", "xd_made", "xdec_made", "y_made", "s_made",
            "s_kept", "o_made", "o_scaled", "y_kept", "turned", "y_out"))

    def load_decays(self, act, q):
        act.dma_start(self.da[:], self.da_dram[bass.ds(q, 1)].rearrange("c h l -> c (h l)").partition_broadcast(P)).then_inc(self.ld_da, 16)

    def act_start(self, act):
        self.load_decays(act, 0)

    def act_step(self, act, b, c, t, s, last):
        q = 2 * b + c
        if (t, s) == (1, 0) and not (last and c == 1):
            act.wait_ge(self.scanned, q + 1)
            self.load_decays(act, q + 1)
        if (t, s) == (1, 2) and c == 0:
            act.wait_ge(self.y_made, q + 1)
            self.nc.scalar.activation(self.y_tok[:], self.ps[:, 0], ACT.Copy).then_inc(self.y_kept, 1)
        if (t, s) == (1, 3) and c == 0:
            act.wait_ge(self.s_made, b + 1)
            self.nc.scalar.activation(self.state[:], self.ps[0:N0, 1], ACT.Copy).then_inc(self.s_kept, 1)

    def pool_step(self, pool, b, c, t, s):
        if (t, s) == (0, 0):
            q = 2 * b + c
            wait_after(pool, self.turned, q)
            tok = bass.ds(q * Q0, Q0)
            self.nc.gpsimd.tensor_copy(self.bts[:], self.bt[:, tok])
            if c == 0:
                self.nc.gpsimd.tensor_copy(self.bs[:], self.b_tok[:, bass.ds(q, 1), :].rearrange("p a n -> p (a n)"))
            self.nc.gpsimd.tensor_copy(self.cts[:], self.ct[:, tok]).then_inc(self.staged, 1)

    def pe_step(self, pe, b, c, t, s):
        nc, q = self.nc, 2 * b + c
        if (t, s) == (0, 2):
            pe.wait_ge(self.staged, q + 1)
            wait_after(pe, self.y_kept, q)
            nc.tensor.matmul(self.ps[:, 0, 0:Q0], self.bts[:], self.cts[:], start=True, stop=True).then_inc(self.g_made, 1)
        if (t, s) == (0, 3) and c == 1:
            pe.wait_ge(self.s_kept, b + 1)
            pe.wait_ge(self.y_out, q)
            nc.tensor.matmul(self.ps[:, 1], self.cts[:], self.state[:], start=True, stop=True).then_inc(self.o_made, 1)
        if (t, s) == (1, 1):
            pe.wait_ge(self.m_made, q + 1)
            pe.wait_ge(self.xd_made, q + 1)
            for h in range(NH0):
                mm = nc.tensor.matmul(self.ps[:, 0, h * P0:(h + 1) * P0], self.m[:, h], self.xd[:, h], start=True, stop=True)
            mm.then_inc(self.y_made, 1)
        if (t, s) == (1, 2) and c == 0:
            pe.wait_ge(self.xdec_made, b + 1)
            wait_after(pe, self.y_out, q)
            nc.tensor.matmul(self.ps[0:N0, 1], self.bs[:], self.xdec[:].rearrange("p h q -> p (h q)"), start=True, stop=True).then_inc(self.s_made, 1)
        if (t, s) == (2, 0):
            pe.wait_ge(self.y_kept, q + 1)
            if c == 0:
                pe.wait_ge(self.s_kept, b + 1)
            else:
                pe.wait_ge(self.o_scaled, b + 1)
            for i in range(NE0):
                mm = nc.tensor.transpose(self.ps[:, 1, i * P:(i + 1) * P], self.y_tok[:, i * P:(i + 1) * P], self.ident)
            mm.then_inc(self.turned, 1)

    def dve_start(self, dve):
        self.nc.vector.tensor_copy(self.delta[:].rearrange("p (h l) -> p h l", l=Q0),
                                   self.ident.unsqueeze(1).to_broadcast([P, NH0, Q0])).then_inc(self.delta_made, 1)
        dve.wait_ge(self.delta_made, 1)

    def dve_step(self, dve, b, c, t, s):
        nc, q = self.nc, 2 * b + c
        if (t, s) == (0, 0):
            dve.wait_ge(self.ld_da, 16 * (q + 1))
            wait_after(dve, self.y_made, q)
            nc.vector.tensor_tensor_scan(self.m[:].rearrange("p h l -> p (h l)"), self.da[:], self.delta[:], 0.0,
                                         ALU.mult, ALU.add).then_inc(self.scanned, 1)
        if (t, s) == (0, 1):
            nc.vector.tensor_tensor(self.xd[:], self.x_tok[:, bass.ds(q, 1), :].rearrange("p a (h q) -> p (a h) q", q=P0),
                                    self.dt_tok[:, bass.ds(q, 1), :].rearrange("p a h -> p (a h)").unsqueeze(2).to_broadcast([P, NH0, P0]),
                                    ALU.mult).then_inc(self.xd_made, 1)
            if c == 0:
                dve.wait_ge(self.xd_made, q + 1)
                dve.wait_ge(self.scanned, q + 1)
                nc.vector.tensor_tensor(self.xdec[:], self.xd[:], self.m[:, :, Q0 - 1:Q0].to_broadcast([P, NH0, P0]),
                                        ALU.mult).then_inc(self.xdec_made, 1)
        if (t, s) == (0, 2):
            if c == 0:
                dve.wait_ge(self.xdec_made, b + 1)
            dve.wait_ge(self.scanned, q + 1)
            dve.wait_ge(self.g_made, q + 1)
            nc.vector.tensor_tensor(self.m[:], self.m[:], self.ps[:, 0, 0:Q0].unsqueeze(1).to_broadcast([P, NH0, Q0]),
                                    ALU.mult).then_inc(self.m_made, 1)
        if (t, s) == (0, 3) and c == 1:
            dve.wait_ge(self.o_made, b + 1)
            nc.vector.tensor_tensor(self.through[:].rearrange("p (h q) -> p h q", q=P0), self.ps[:, 1].rearrange("p (h q) -> p h q", q=P0),
                                    self.cp_tok[:, bass.ds(q, 1), :].rearrange("p a h -> p (a h)").unsqueeze(2).to_broadcast([P, NH0, P0]),
                                    ALU.mult).then_inc(self.o_scaled, 1)
        if (t, s) == (1, 2) and c == 1:
            dve.wait_ge(self.o_scaled, b + 1)
            dve.wait_ge(self.y_made, q + 1)
            nc.vector.tensor_tensor(self.y_tok[:], self.ps[:, 0], self.through[:], ALU.add).then_inc(self.y_kept, 1)
        if (t, s) == (2, 1):
            dve.wait_ge(self.turned, q + 1)
            tok = bass.ds(q * Q0, Q0)
            for i in range(NE0):
                op = nc.vector.scalar_tensor_tensor(out=self.y_t[:, i, tok], in0=self.conv_x[i][:, tok], scalar=self.d_col[:, i:i + 1],
                                                    in1=self.ps[:, 1, i * P:(i + 1) * P], op0=ALU.mult, op1=ALU.add)
            op.then_inc(self.y_out, 1)
class Router:

    def __init__(self, nc, ctx, new, name, h_t, gw, lower, w_dram, ident, X_, TOP, renorm, memory=None):
        sb, sem = new(ctx)
        self.nc, self.h_t, self.gw, self.lower, self.w_dram, self.ident, self.X_, self.TOP, self.renorm = nc, h_t, gw, lower, w_dram, ident, X_, TOP, renorm
        self.d, self.e, self.w = (sb(s, [P, TT, X_]) for s in ("d", "e", "w"))
        self.rank = self.d
        self.mx, self.den, self.rden = sb("mx", [P, TT]), sb("den", [P, TT]), sb("rden", [P, TT])
        memory = sb("pairs", [P, 2, TT * X_ * X_])[:] if memory is None else memory
        self.gt, self.eq = (memory[:, i].rearrange("p (t e f) -> p t e f", e=X_, f=X_) for i in range(2))
        self.w_t = sb("w_t", [X_, T])
        self.ps = ctx.enter_context(nc.psum_tensor(name + "_ps", [P, 2, HALF], F32))
        self.logits, self.shifted, self.exped, self.weighed, self.turned, self.copied, self.sent, self.chain, self.shared, self.equal, self.before, self.greater, self.counted = (
            sem(s) for s in ("logits", "shifted", "exped", "weighed", "turned", "copied", "sent", "chain", "shared", "equal",
                             "before", "greater", "counted"))
        self.links = 0

    def pe_1(self, pe):
        X_ = self.X_
        for t in range(TT):
            for k in range(KH):
                mm = self.nc.tensor.matmul(self.ps[:, 0, t * X_:(t + 1) * X_], self.h_t[:, k, t * P:(t + 1) * P], self.gw[:, k, :],
                                           start=k == 0, stop=k == KH - 1)
        mm.then_inc(self.logits, 1)

    def pe_2(self, pe):
        pe.wait_ge(self.weighed, 1)
        for t in range(TT):
            mm = self.nc.tensor.transpose(self.ps[0:self.X_, 1 - t // 4, (t % 4) * P:(t % 4 + 1) * P], self.w[:, t, :], self.ident)
        mm.then_inc(self.turned, 1)

    def act_1(self, act):
        act.wait_ge(self.shifted, 1)
        self.nc.scalar.activation(self.e[:], self.d[:], ACT.Exp).then_inc(self.exped, 1)

    def act_2(self, act):
        act.wait_ge(self.turned, 1)
        for hf in range(NHALF):
            op = self.nc.scalar.activation(self.w_t[:, half(hf)], self.ps[0:self.X_, 1 - hf], ACT.Copy)
        op.then_inc(self.copied, 1)

    def sp(self, sp):
        sp.wait_ge(self.copied, 1)
        sp.dma_start(self.w_dram, self.w_t[:]).then_inc(self.sent, 16)
        sp.wait_ge(self.sent, 16)

    def link(self, dve, op):
        self.links += 1
        op.then_inc(self.chain, 1)
        dve.wait_ge(self.chain, self.links)

    def dve_1(self, dve):
        nc = self.nc
        dve.wait_ge(self.logits, 1)
        l3 = self.ps[:, 0, 0:TT * self.X_].rearrange("p (t e) -> p t e", e=self.X_)
        self.link(dve, nc.vector.reduce_max(self.mx[:], l3, axis=X))
        nc.vector.tensor_tensor(self.d[:], l3, self.mx[:].unsqueeze(2).to_broadcast([P, TT, self.X_]), ALU.subtract).then_inc(self.shifted, 1)

    def dve_2(self, dve):
        nc, X_, e = self.nc, self.X_, self.e
        dve.wait_ge(self.exped, 1)
        self.link(dve, nc.vector.reduce_sum(self.den[:], e[:], axis=X))
        self.link(dve, nc.vector.reciprocal(self.rden[:], self.den[:]))
        nc.vector.tensor_tensor(e[:], e[:], self.rden[:].unsqueeze(2).to_broadcast([P, TT, X_]), ALU.mult).then_inc(self.shared, 1)
        dve.wait_ge(self.shared, 1)
        mine, other = self.squares()
        nc.vector.tensor_tensor(self.eq, other, mine, ALU.is_equal).then_inc(self.equal, 1)
        nc.vector.tensor_tensor(self.gt, other, mine, ALU.is_gt).then_inc(self.greater, 1)

    def squares(self):
        square = [P, TT, self.X_, self.X_]
        return self.e[:].unsqueeze(3).to_broadcast(square), self.e[:].unsqueeze(2).to_broadcast(square)

    def pool(self, pool):
        nc = self.nc
        pool.wait_ge(self.equal, 1)
        nc.gpsimd.tensor_tensor(self.eq, self.eq, self.lower.unsqueeze(1).to_broadcast([P, TT, self.X_, self.X_]), ALU.mult).then_inc(self.before, 1)
        pool.wait_ge(self.before, 1)
        pool.wait_ge(self.greater, 1)
        nc.gpsimd.tensor_tensor(self.gt, self.gt, self.eq, ALU.add).then_inc(self.counted, 1)

    def dve_3(self, dve):
        nc, X_, e, w = self.nc, self.X_, self.e, self.w
        wide = [P, TT, X_]
        dve.wait_ge(self.counted, 1)
        self.link(dve, nc.vector.reduce_sum(self.rank[:], self.gt, axis=X))
        op = nc.vector.scalar_tensor_tensor(out=w[:], in0=self.rank[:], scalar=self.TOP - 0.5, in1=e[:], op0=ALU.is_lt, op1=ALU.mult)
        if self.renorm:
            self.link(dve, op)
            self.link(dve, nc.vector.reduce_sum(self.den[:], w[:], axis=X))
            self.link(dve, nc.vector.reciprocal(self.rden[:], self.den[:]))
            op = nc.vector.tensor_tensor(w[:], w[:], self.rden[:].unsqueeze(2).to_broadcast(wide), ALU.mult)
        op.then_inc(self.weighed, 1)


def mixer_out_phase(nc, new, name, y_t, gate_s, norm_w, w_dram, w_raw, x_t, sq, ones, ident, eps, gate_first, out=None):
    n = y_t.shape[1]
    NT = TT // NHALF
    with ExitStack() as ctx:
        sb, sem = new(ctx)
        w_hi, w_lo = sb("w_hi", [P, n, H], F32R), sb("w_lo", [P, n, H], F32R)
        g = sb("g", [P, n, T])
        g_hi, g_lo = sb("g_hi", [P, n, T], F32R), sb("g_lo", [P, n, T], F32R)
        std, rstd, diagonal = sb("std", [P, TT]), sb("rstd", [P, TT]), sb("diagonal", [P, TT, P])
        factor = sb("factor", [P, T])
        ps = ctx.enter_context(nc.psum_tensor(name + "_ps", [P, KH, NHALF, HALF], F32))
        ps_sq = ctx.enter_context(nc.psum_tensor(name + "_ps_sq", [P, NHALF, HALF], F32))
        ps_r = ctx.enter_context(nc.psum_tensor(name + "_ps_r", [P, NHALF, HALF], F32))
        (loaded, w_his, w_los, gated, g_his, g_los, squared, paired, sq_sums, stds, rstds, diagonals, spread, factors,
         made, scaled, added, last_added, stored) = (sem(s) for s in (
            "loaded", "w_his", "w_los", "gated", "g_his", "g_los", "squared", "paired", "sq_sums", "stds", "rstds",
            "diagonals", "spread", "factors", "made", "scaled", "added", "last_added", "stored"))
        nc.scalar.preload_act_table(ACT.Sqrt)
        block = ctx.enter_context(nc.Block())

        @block.sync
        def _(sp):
            sp.dma_start(w_raw, w_dram.rearrange("(k p) n -> p k n", p=P)).then_inc(loaded, 16)
            if out is not None:
                for hf in range(NHALF):
                    sp.wait_ge(added, KH + hf)
                    if hf == NHALF - 1:
                        sp.wait_ge(last_added, 1)
                    sp.dma_start(out[:, :, half(hf)], x_t[:, :, half(hf)]).then_inc(stored, 16)
                sp.wait_ge(stored, 16 * NHALF)

        @block.scalar
        def _(act):
            def high(hf, k):
                act.wait_ge(gated, hf * n + k + 1)
                nc.scalar.activation(g_hi[:, k, half(hf)], g[:, k, half(hf)], ACT.Copy).then_inc(g_his, 1)

            for hf in range(NHALF):
                for k in range(n):
                    high(hf, k)
                    if hf == 0 and k == 1:
                        act.wait_ge(loaded, 16)
                        for i in range(n):
                            op = nc.scalar.activation(w_hi[:, i], w_raw[:, i], ACT.Copy, scale=norm_w[:, i:i + 1])
                        op.then_inc(w_his, 1)
                nc.scalar.activation(sq[:, :, half(hf)], (g if gate_first else y_t)[:, :, half(hf)], ACT.Square).then_inc(squared, 1)
            for hf in range(NHALF):
                act.wait_ge(sq_sums, hf + 1)
                nc.scalar.activation(std[:, hf * NT:(hf + 1) * NT], ps_sq[:, hf, 0:NT], ACT.Sqrt, bias=eps, scale=1.0 / (n * P)).then_inc(stds, 1)
                act.wait_ge(spread, hf + 1)
                nc.scalar.activation(factor[:, half(hf)], ps_r[:, hf], ACT.Copy).then_inc(factors, 1)

        @block.gpsimd
        def _(pool):
            for hf in range(NHALF):
                pool.wait_ge(squared, hf + 1)
                nc.gpsimd.tensor_tensor(sq[:, 0:n // 2, half(hf)], sq[:, 0:n // 2, half(hf)], sq[:, n // 2:, half(hf)],
                                        ALU.add).then_inc(paired, 1)
            for hf in range(NHALF):
                for d in range(KH - hf):
                    pool.wait_ge(scaled, hf * KH + d + 1)
                    nc.gpsimd.tensor_tensor(x_t[:, d, half(hf)], g[:, d, half(hf)], x_t[:, d, half(hf)], ALU.add).then_inc(added, 1)

        @block.tensor
        def _(pe):
            def statistics(hf):
                pe.wait_ge(paired, hf + 1)
                for t in range(NT):
                    tok = slice((hf * NT + t) * P, (hf * NT + t + 1) * P)
                    for k in range(n // 2):
                        mm = nc.tensor.matmul(ps_sq[:, hf, t:t + 1], sq[:, k, tok], ones[:, 0:1], start=k == 0, stop=k == n // 2 - 1)
                mm.then_inc(sq_sums, 1)

            def spread_factor(hf):
                pe.wait_ge(diagonals, hf + 1)
                nc.tensor.matmul(ps_r[:, hf], ones, diagonal[:, hf * NT:(hf + 1) * NT].rearrange("p t c -> p (t c)"),
                                 start=True, stop=True).then_inc(spread, 1)

            def product(hf, k):
                pe.wait_ge(g_los, hf * n + k + 1)
                for d in range(KH):
                    f = slice(d * P, (d + 1) * P)
                    mm = product3(nc, ps[:, d, hf], w_hi[:, k, f], w_lo[:, k, f], g_hi[:, k, half(hf)], g_lo[:, k, half(hf)],
                                  k == 0, k == n - 1)
                    if k == n - 1:
                        mm.then_inc(made, 1)

            pe.wait_ge(w_los, 1)
            for k in range(n):
                product(0, k)
            statistics(0)
            for k in range(n):
                product(1, k)
                if k == 1:
                    spread_factor(0)
                if k == 2:
                    statistics(1)
            spread_factor(1)

        @block.vector
        def _(dve):
            def gate(hf, k):
                nc.vector.tensor_tensor(g[:, k, half(hf)], y_t[:, k, half(hf)], gate_s[:, k, half(hf)], ALU.mult).then_inc(gated, 1)

            def low(hf, k):
                dve.wait_ge(g_his, hf * n + k + 1)
                nc.vector.tensor_tensor(g_lo[:, k, half(hf)], g[:, k, half(hf)], g_hi[:, k, half(hf)].bitcast(F32), ALU.subtract).then_inc(g_los, 1)

            def invert(hf):
                part = slice(hf * NT, (hf + 1) * NT)
                dve.wait_ge(stds, hf + 1)
                nc.vector.reciprocal(rstd[:, part], std[:, part]).then_inc(rstds, 1)
                dve.wait_ge(rstds, hf + 1)
                nc.vector.tensor_tensor(diagonal[:, part], ident.unsqueeze(1).to_broadcast([P, NT, P]),
                                        rstd[:, part].unsqueeze(2).to_broadcast([P, NT, P]), ALU.mult).then_inc(diagonals, 1)

            for k in range(n):
                gate(0, k)
            low(0, 0)
            low(0, 1)
            dve.wait_ge(w_his, 1)
            for k in range(n):
                op = nc.vector.scalar_tensor_tensor(out=w_lo[:, k], in0=w_raw[:, k], scalar=norm_w[:, k:k + 1], in1=w_hi[:, k].bitcast(F32),
                                                    op0=ALU.mult, op1=ALU.subtract)
            op.then_inc(w_los, 1)
            low(0, 2)
            low(0, 3)
            for k in range(n):
                gate(1, k)
                if k > 0:
                    low(1, k - 1)
            low(1, n - 1)
            for hf in range(NHALF):
                invert(hf)
                dve.wait_ge(factors, hf + 1)
                for d in range(KH):
                    dve.wait_ge(made, hf * KH + d + 1)
                    nc.vector.tensor_tensor(g[:, d, half(hf)], ps[:, d, hf], factor[:, half(hf)], ALU.mult).then_inc(scaled, 1)
            dve.wait_ge(scaled, NHALF * KH)
            nc.vector.tensor_tensor(x_t[:, KH - 1, half(1)], g[:, KH - 1, half(1)], x_t[:, KH - 1, half(1)], ALU.add).then_inc(last_added, 1)
def keys_values_phase(nc, new, io, wk, wv, hn_hi, hn_lo, kz, v_tok, wq_raw, wo_raw):
    with ExitStack() as ctx:
        sb, sem = new(ctx)
        (_, _, wk_hi, wk_lo), (_, _, wv_hi, wv_lo) = wk, wv
        ps = ctx.enter_context(nc.psum_tensor("kv_ps", [P, 8, HALF], F32))
        loaded, made, low_took, high_took, v_took, zeroed = (
            sem(s) for s in ("loaded", "made", "low_took", "high_took", "v_took", "zeroed"))
        block = ctx.enter_context(nc.Block())
        nk = KT * NHALF

        @block.sync
        def _(sp):
            for i in range(2):
                sp.dma_start(wq_raw[:, i], io["wq_tiles"][i]).then_inc(loaded, 16)
                sp.dma_start(wo_raw[:, i], io["wo_tiles"][i]).then_inc(loaded, 16)
            sp.wait_ge(loaded, 64)

        @block.gpsimd
        def _(pool):
            nc.gpsimd.memset(kz[D:P, 0], 0.0)
            nc.gpsimd.memset(kz[0:D, 1], 0.0).then_inc(zeroed, 1)

        @block.tensor
        def _(pe):
            for n in range(nk + TT):
                if n >= 8:
                    wait_after(pe, low_took, n - 7)
                    wait_after(pe, high_took, n - 7)
                for k in range(KH):
                    if n < nk:
                        f = slice(n // 2 * P, (n // 2 + 1) * P)
                        mm = product3(nc, ps[:, n % 8], wk_hi[:, k, f], wk_lo[:, k, f],
                                      hn_hi[:, k, half(n % 2)], hn_lo[:, k, half(n % 2)], k == 0, k == KH - 1)
                    else:
                        tok = slice((n - nk) * P, (n - nk + 1) * P)
                        mm = product3(nc, ps[:, n % 8], hn_hi[:, k, tok], hn_lo[:, k, tok],
                                      wv_hi[:, k], wv_lo[:, k], k == 0, k == KH - 1)
                mm.then_inc(made, 1)

        @block.scalar
        def _(act):
            for n in range(nk):
                act.wait_ge(made, n + 1)
                nc.scalar.activation(kz[0:D, 0, n // 2, half(n % 2)], ps[0:D, n % 8], ACT.Copy).then_inc(low_took, 1)
            for t in range(0, TT, 2):
                act.wait_ge(made, nk + t + 1)
                nc.scalar.activation(v_tok[:, t, :], ps[:, (nk + t) % 8], ACT.Copy).then_inc(v_took, 1)

        @block.vector
        def _(dve):
            for n in range(nk):
                dve.wait_ge(made, n + 1)
                nc.vector.tensor_copy(kz[D:P, 1, n // 2, half(n % 2)], ps[D:P, n % 8]).then_inc(high_took, 1)
            for t in range(1, TT, 2):
                dve.wait_ge(made, nk + t + 1)
                nc.vector.tensor_copy(v_tok[:, t, :], ps[:, (nk + t) % 8])


def attention_phase(nc, new, io, wq_raw, wo_raw, hn_hi, hn_lo, kz, v_tok, xn, h_t, ident, ident_bf, mask_bf):
    SCALE = float(D) ** -0.5
    NI = NHQ // NKV
    NU = NI * B
    AHEAD = 2
    with ExitStack() as ctx:
        sb, sem = new(ctx)
        wq_hi, wo_hi = sb("wq_hi", [P, 2, KH, P], F32R), sb("wo_hi", [P, 2, H], F32R)
        wq_lo, wo_lo = sb("wq_lo", [P, 2, KH, P], F32R), sb("wo_lo", [P, 2, H], F32R)
        q = sb("q", [P, 2, T])
        vs = sb("vs", [P, TT, P])
        probs = sb("probs", [P, 2, 6 * P])
        pt_a = sb("pt_a", [P, 2, 2, 2 * P])
        pt_b = sb("pt_b", [P, 2, 2, P])
        mx, nb = sb("mx", [P, 2, 4]), sb("nb", [P, 2, 4])
        rs, ri = sb("rs", [P, 2, 4]), sb("ri", [P, 2, 4])
        o_hi, o_lo = sb("o_hi", [P, 2, T], F32R), sb("o_lo", [P, 2, T], F32R)
        ps_a = ctx.enter_context(nc.psum_tensor("at_a", [P, HALF], F32))
        ps_s1 = ctx.enter_context(nc.psum_tensor("at_s1", [P, 2, HALF], F32))
        ps_s0 = ctx.enter_context(nc.psum_tensor("at_s0", [P, 2, HALF], F32))
        ps_t = ctx.enter_context(nc.psum_tensor("at_t", [P, 2, HALF], F32))
        ps_o = ctx.enter_context(nc.psum_tensor("at_o", [P, HALF], F32))
        ld_q, ld_o = [sem("ld_q0"), sem("ld_q1")], [sem("ld_o0"), sem("ld_o1")]
        (wq_his, wq_los, wo_his, wo_los, q_made, q_taken, v_staged, s_made, maxed, nb_made, exp_made, inverted, p_made,
         ta_made, tb_made, pta_copied, ptb_copied, o_made, o_his, o_los, wo_made, wo_taken, copied) = (
            sem(s) for s in ("wq_his", "wq_los", "wo_his", "wo_los", "q_made", "q_taken", "v_staged", "s_made", "maxed",
                             "nb_made", "exp_made", "inverted", "p_made", "ta_made", "tb_made", "pta_copied",
                             "ptb_copied", "o_made", "o_his", "o_los", "wo_made", "wo_taken", "copied"))
        nc.scalar.preload_act_table(ACT.Exp)
        block = ctx.enter_context(nc.Block())

        def later(m, i, b, n):
            k = 4 * i + b + n
            if k >= NU:
                m, k = m + 1, k - NU
            return None if isinstance(m, int) and m >= KT else (m, k // B, k % B)

        def before(m, i, b):
            return (m, i, b - 1) if b else (m, i - 1, B - 1) if i else (m - 1, NI - 1, B - 1)

        def next_tile(m, i, n):
            u = later(m, i, 0, n * B)
            return u and u[:2]

        @block.sync
        def _(sp):
            def load(m, i):
                j, slot = NI * m + i, i % 2
                wait_after(sp, wq_los, j - 1)
                sp.dma_start(wq_raw[:, slot], io["wq_tiles"][bass.ds(j, 1)].rearrange("a p k n -> p (a k) n")).then_inc(ld_q[slot], 16)
                wait_after(sp, wo_los, j - 1)
                sp.dma_start(wo_raw[:, slot], io["wo_tiles"][bass.ds(j, 1)].rearrange("a p n -> p (a n)")).then_inc(ld_o[slot], 16)

            for i in range(2, NI):
                load(0, i)
            with sp.Fori(1, KT) as m:
                for i in range(NI):
                    load(m, i)

        @block.gpsimd
        def _(pool):
            def split_q(m, i):
                pool.wait_ge(wq_his, NI * m + i + 1)
                nc.gpsimd.tensor_tensor(wq_lo[:, i % 2], wq_raw[:, i % 2], wq_hi[:, i % 2].bitcast(F32), ALU.subtract).then_inc(wq_los, 1)

            def split_o(m, i):
                pool.wait_ge(wo_his, NI * m + i + 1)
                nc.gpsimd.tensor_tensor(wo_lo[:, i % 2], wo_raw[:, i % 2], wo_hi[:, i % 2].bitcast(F32), ALU.subtract).then_inc(wo_los, 1)

            def stage_v(m, b):
                wait_after(pool, o_made, NU * m - B + b + 1)
                nc.gpsimd.tensor_copy(vs[:, 2 * b:2 * b + 2], v_tok[:, 2 * b:2 * b + 2, bass.ds(m * P, P)]).then_inc(v_staged, 1)

            split_q(0, 0)
            split_q(0, 1)
            for b in range(B):
                stage_v(0, b)
            for m, first, last in turns(pool, KT):
                for i in range(NI):
                    split_o(m, i)
                    ahead = next_tile(m, i, 2)
                    if ahead:
                        split_q(*ahead)
                    if i == NI - 1 and not last:
                        for b in range(B):
                            stage_v(m + 1, b)

        @block.tensor
        def _(pe):
            def project_q(m, i, hf):
                j = NI * m + i
                if hf == 0:
                    pe.wait_ge(wq_los, j + 1)
                wait_after(pe, q_taken, 2 * j + hf)
                wait_after(pe, wo_taken, 4 * (j - 2) + 2 * (hf + 1))
                for k in range(KH):
                    mm = product3(nc, ps_a[:], wq_hi[:, i % 2, k], wq_lo[:, i % 2, k],
                                  hn_hi[:, k, half(hf)], hn_lo[:, k, half(hf)], k == 0, k == KH - 1)
                mm.then_inc(q_made, 1)

            def project_o(m, i, hf, d, queries):
                j = NI * m + i
                if hf == 0 and d == 0:
                    pe.wait_ge(wo_los, j + 1)
                if d == 0:
                    pe.wait_ge(o_los, 4 * j + 2 * hf + 2)
                wait_after(pe, wo_taken, 4 * j + 2 * hf + d)
                if d == 0 and queries:
                    pe.wait_ge(q_taken, 2 * (j + 2) + (1 if hf else 0))
                f = slice(d * P, (d + 1) * P)
                product3(nc, ps_a[:], wo_hi[:, i % 2, f], wo_lo[:, i % 2, f],
                         o_hi[:, i % 2, half(hf)], o_lo[:, i % 2, half(hf)], True, True).then_inc(wo_made, 1)

            def scores(m, i, b):
                u = NU * m + 4 * i + b
                if b % 2 == 0:
                    pe.wait_ge(q_taken, 2 * (NI * m + i) + b // 2 + 1)
                wait_after(pe, exp_made, u - 1)
                both = [P, 2, P]
                tok = b * S
                s1 = ps_s1[:, b % 2].rearrange("p (h k) -> p h k", h=2)
                s0 = ps_s0[:, b % 2, 0:2 * P].rearrange("p (h k) -> p h k", h=2)
                kzm = kz[:, :, bass.ds(m, 1), :].rearrange("p h a t -> p h (a t)")
                nc.tensor.matmul(s1, q[:, i % 2, tok + P:tok + S], kzm[:, :, tok:tok + S], start=True, stop=False)
                nc.tensor.matmul(s1[:, :, P:], ident_bf, mask_bf.unsqueeze(1).to_broadcast(both), start=False, stop=True)
                nc.tensor.matmul(s0, q[:, i % 2, tok:tok + P], kzm[:, :, tok:tok + P], start=True, stop=False)
                nc.tensor.matmul(s0, ident_bf, mask_bf.unsqueeze(1).to_broadcast(both), start=False, stop=True).then_inc(s_made, 1)

            def turn(m, i, b):
                u = NU * m + 4 * i + b
                p = probs[:, b % 2]
                pe.wait_ge(p_made, u + 1)
                wait_after(pe, pta_copied, u)
                for h in range(2):
                    nc.tensor.transpose(ps_t[:, 0, 2 * h * P:(2 * h + 1) * P], p[:, (4 + h) * P:(5 + h) * P], ident)
                    mm = nc.tensor.transpose(ps_t[:, 0, (2 * h + 1) * P:(2 * h + 2) * P], p[:, 2 * h * P:(2 * h + 1) * P], ident)
                mm.then_inc(ta_made, 1)
                wait_after(pe, ptb_copied, u)
                for h in range(2):
                    mm = nc.tensor.transpose(ps_t[:, 1, h * P:(h + 1) * P], p[:, (2 * h + 1) * P:(2 * h + 2) * P], ident)
                mm.then_inc(tb_made, 1)

            def heads_out(m, i, b):
                u = NU * m + 4 * i + b
                if i == 0:
                    pe.wait_ge(v_staged, B * m + b + 1)
                pe.wait_ge(pta_copied, u + 1)
                pe.wait_ge(ptb_copied, u + 1)
                wait_after(pe, o_los, u)
                for h in range(2):
                    rows = slice(h * D, (h + 1) * D)
                    nc.tensor.matmul(ps_o[rows, 0:2 * P], vs[:, 2 * b, rows], pt_a[:, b % 2, h], start=True, stop=False)
                    mm = nc.tensor.matmul(ps_o[rows, P:2 * P], vs[:, 2 * b + 1, rows], pt_b[:, b % 2, h], start=False, stop=True)
                mm.then_inc(o_made, 1)

            for hf in range(NHALF):
                project_q(0, 0, hf)
            for b in range(AHEAD):
                scores(0, 0, b)
            for m, first, last in turns(pe, KT):
                for i in range(NI):
                    for b in range(B):
                        turn(m, i, b)
                        following = next_tile(m, i, 1)
                        if b % 2 == 0 and following:
                            project_q(*following, b // 2)
                        done = None
                        if b == 1 and not (first and i == 0):
                            done = ((m, i - 1) if i else (m - 1, NI - 1)) + (1,)
                        if b == 3:
                            done = (m, i, 0)
                        if done:
                            project_o(*done, 0, following)
                        unit = later(m, i, b, AHEAD)
                        if unit:
                            scores(*unit)
                        if done:
                            project_o(*done, 1, following)
                        heads_out(m, i, b)
            for d in range(KH):
                project_o(KT - 1, NI - 1, 1, d, None)

        @block.scalar
        def _(act):
            def split_q(m, i):
                j = NI * m + i
                wait_after(act, ld_q[i % 2], 16 * (NI // 2 * m + i // 2))
                wait_after(act, q_made, 2 * (j - 1))
                nc.scalar.activation(wq_hi[:, i % 2], wq_raw[:, i % 2], ACT.Copy).then_inc(wq_his, 1)

            def split_o(m, i):
                j = NI * m + i
                wait_after(act, ld_o[i % 2], 16 * (NI // 2 * m + i // 2))
                wait_after(act, wo_made, 4 * (j - 1))
                nc.scalar.activation(wo_hi[:, i % 2], wo_raw[:, i % 2], ACT.Copy).then_inc(wo_his, 1)

            def take_q(m, i, hf):
                j = NI * m + i
                act.wait_ge(q_made, 2 * j + hf + 1)
                nc.scalar.activation(q[:, i % 2, half(hf)], ps_a[:], ACT.Copy).then_inc(q_taken, 1)

            def exps(m, i, b):
                u = NU * m + 4 * i + b
                wait_after(act, nb_made, u + 1)
                parts = ((ps_s1[:, b % 2, 0:2 * P], 0, 2 * P), (ps_s1[:, b % 2, 2 * P:4 * P], 2 * P, 2 * P),
                         (ps_s0[:, b % 2, 0:P], 4 * P, P), (ps_s0[:, b % 2, P:2 * P], 5 * P, P))
                for n, (src, c, w) in enumerate(parts):
                    op = nc.scalar.activation(probs[:, b % 2, c:c + w], src, ACT.Exp, bias=nb[:, b % 2, n:n + 1], scale=SCALE,
                                              accum_out=rs[:, b % 2, n:n + 1])
                op.then_inc(exp_made, 1)

            def take_pt(m, i, b):
                u = NU * m + 4 * i + b
                act.wait_ge(ta_made, u + 1)
                nc.scalar.activation(pt_a[:, b % 2].rearrange("p h q -> p (h q)"), ps_t[:, 0], ACT.Copy).then_inc(pta_copied, 1)

            def take_o(m, i, b):
                u = NU * m + 4 * i + b
                act.wait_ge(o_made, u + 1)
                nc.scalar.activation(o_hi[:, i % 2, b * S:(b + 1) * S], ps_o[:, 0:2 * P], ACT.Copy).then_inc(o_his, 1)

            split_q(0, 0)
            split_q(0, 1)
            for hf in range(NHALF):
                take_q(0, 0, hf)
            exps(0, 0, 0)
            for m, first, last in turns(act, KT):
                for i in range(NI):
                    for b in range(B):
                        if not (first and i == 0 and b == 0):
                            take_o(*before(m, i, b))
                        take_pt(m, i, b)
                        following, ahead = next_tile(m, i, 1), next_tile(m, i, 2)
                        unit = later(m, i, b, 1)
                        if unit:
                            exps(*unit)
                        if b % 2 == 0 and following:
                            take_q(*following, b // 2)
                        if b == 1 and ahead:
                            split_q(*ahead)
                        if b == 1:
                            split_o(m, i)
            take_o(KT - 1, NI - 1, B - 1)

        @block.vector
        def _(dve):
            def maxima(m, i, b):
                u = NU * m + 4 * i + b
                dve.wait_ge(s_made, u + 1)
                nc.vector.reduce_max(mx[:, b % 2, 0:2], ps_s1[:, b % 2].rearrange("p (h k) -> p h k", h=2), axis=X)
                nc.vector.reduce_max(mx[:, b % 2, 2:4], ps_s0[:, b % 2, 0:2 * P].rearrange("p (h k) -> p h k", h=2), axis=X).then_inc(maxed, 1)
                dve.wait_ge(maxed, u + 1)
                nc.vector.tensor_scalar(nb[:, b % 2], mx[:, b % 2], -SCALE, None, ALU.mult).then_inc(nb_made, 1)

            def normalize(m, i, b):
                u = NU * m + 4 * i + b
                dve.wait_ge(exp_made, u + 1)
                nc.vector.reciprocal(ri[:, b % 2], rs[:, b % 2]).then_inc(inverted, 1)
                dve.wait_ge(inverted, u + 1)
                for n, (c, w) in enumerate(((0, 2 * P), (2 * P, 2 * P), (4 * P, P), (5 * P, P))):
                    p = probs[:, b % 2, c:c + w]
                    op = nc.vector.tensor_scalar(p, p, ri[:, b % 2, n:n + 1], None, ALU.mult)
                op.then_inc(p_made, 1)

            def take_pt(m, i, b):
                u = NU * m + 4 * i + b
                dve.wait_ge(tb_made, u + 1)
                nc.vector.tensor_copy(pt_b[:, b % 2].rearrange("p h q -> p (h q)"), ps_t[:, 1, 0:2 * P]).then_inc(ptb_copied, 1)

            def split_o(m, i, b):
                u = NU * m + 4 * i + b
                dve.wait_ge(o_his, u + 1)
                o = (slice(None), i % 2, slice(b * S, (b + 1) * S))
                nc.vector.tensor_tensor(o_lo[o], ps_o[:, 0:2 * P], o_hi[o].bitcast(F32), ALU.subtract).then_inc(o_los, 1)

            def take_projection(m, i, hf, d):
                dve.wait_ge(wo_made, 4 * (NI * m + i) + 2 * hf + d + 1)
                nc.vector.tensor_tensor(h_t[:, d, half(hf)], ps_a[:], h_t[:, d, half(hf)], ALU.add).then_inc(wo_taken, 1)

            nc.vector.tensor_copy(h_t[:], xn[:]).then_inc(copied, 1)
            dve.wait_ge(copied, 1)
            for b in range(AHEAD):
                maxima(0, 0, b)
            normalize(0, 0, 0)
            for m, first, last in turns(dve, KT):
                for i in range(NI):
                    for b in range(B):
                        if not (first and i == 0 and b == 0):
                            split_o(*before(m, i, b))
                        take_pt(m, i, b)
                        done = None
                        if b == 1 and not (first and i == 0):
                            done = ((m, i - 1) if i else (m - 1, NI - 1)) + (1,)
                        if b == 3:
                            done = (m, i, 0)
                        if done:
                            take_projection(*done, 0)
                        unit = later(m, i, b, 1)
                        if unit:
                            normalize(*unit)
                        if done:
                            take_projection(*done, 1)
                        unit = later(m, i, b, AHEAD)
                        if unit:
                            maxima(*unit)
            split_o(KT - 1, NI - 1, B - 1)
            for d in range(KH):
                take_projection(KT - 1, NI - 1, 1, d)
class Experts:

    def __init__(self, nc, ctx, new, name, w_dram, raw, func, t_hi, t_lo, acc):
        sb, sem = new(ctx)
        self.nc, self.w_dram, self.func, self.t_hi, self.t_lo, self.acc = nc, w_dram, func, t_hi, t_lo, acc
        self.raw_ab, self.raw_c = raw
        self.ab_hi, self.ab_lo = sb("ab_hi", [P, 2, 2, H], F32R), sb("ab_lo", [P, 2, 2, H], F32R)
        self.c_hi, self.c_lo = sb("c_hi", [P, 2, H], F32R), sb("c_lo", [P, 2, H], F32R)
        self.r, self.rc, self.g = sb("r", [P, 2, HALF]), sb("rc", [P, 2, HALF]), sb("g", [P, 2, HALF])
        self.g_hi, self.g_lo = sb("g_hi", [P, 2, HALF], F32R), sb("g_lo", [P, 2, HALF], F32R)
        self.ps_u = ctx.enter_context(nc.psum_tensor(name + "_u", [P, 2, HALF], F32))
        self.ps_v = ctx.enter_context(nc.psum_tensor(name + "_v", [P, 2, HALF], F32))
        self.ps_y = ctx.enter_context(nc.psum_tensor(name + "_y", [P, KH, HALF], F32))
        self.ld_ab, self.ld_c = [sem("ld_ab0"), sem("ld_ab1")], [sem("ld_c0"), sem("ld_c1")]
        (self.ab_his, self.ab_los, self.c_his, self.c_los, self.u_made, self.r_made, self.rc_made, self.g_made, self.g_his,
         self.g_los, self.y_made, self.y_added) = (
            sem(s) for s in ("ab_his", "ab_los", "c_his", "c_los", "u_made", "r_made", "rc_made", "g_made", "g_his", "g_los",
                             "y_made", "y_added"))

    def load(self, sp, t, j):
        src = self.w_dram[bass.ds(2 * t + j, 1)].rearrange("a p j n -> p (a j) n")
        wait_after(sp, self.ab_los, 2 * t + j - 1)
        sp.dma_start(self.raw_ab[:, j], src[:, 0:2]).then_inc(self.ld_ab[j], 16)
        wait_after(sp, self.c_los, 2 * t + j - 1)
        sp.dma_start(self.raw_c[:, j], src[:, 2]).then_inc(self.ld_c[j], 16)

    def up(self, pe, t, s):
        nc, (hf, j), n = self.nc, divmod(s, 2), 4 * t + s
        if hf == 0:
            pe.wait_ge(self.ab_los, 2 * t + j + 1)
        wait_after(pe, self.g_made, n - 1)
        for ps, i in ((self.ps_u, 0), (self.ps_v, 1)):
            for k in range(KH):
                f = slice(k * P, (k + 1) * P)
                mm = product3(nc, ps[:, j], self.ab_hi[:, j, i, f], self.ab_lo[:, j, i, f],
                              self.t_hi[:, k, half(hf)], self.t_lo[:, k, half(hf)], k == 0, k == KH - 1)
        mm.then_inc(self.u_made, 1)

    def down(self, pe, t, s):
        nc, (hf, j), n = self.nc, divmod(s, 2), 4 * t + s
        if hf == 0:
            pe.wait_ge(self.c_los, 2 * t + j + 1)
        pe.wait_ge(self.g_los, n + 1)
        if j == 0:
            wait_after(pe, self.y_added, 2 * t + hf)
        for d in range(KH):
            f = slice(d * P, (d + 1) * P)
            mm = product3(nc, self.ps_y[:, d], self.c_hi[:, j, f], self.c_lo[:, j, f], self.g_hi[:, j], self.g_lo[:, j],
                          j == 0, j == 1)
        mm.then_inc(self.y_made, 1)

    def down_behind(self, pe, t, s, first):
        if s >= 2:
            self.down(pe, t, s - 2)
        elif not first:
            self.down(pe, t - 1, s + 2)

    def pe_end(self, pe, t):
        self.down(pe, t, 2)
        self.down(pe, t, 3)

    def split_ab_hi(self, act, t, j):
        wait_after(act, self.ld_ab[j], 16 * t)
        wait_after(act, self.u_made, 4 * t - 1 + j)
        self.nc.scalar.activation(self.ab_hi[:, j], self.raw_ab[:, j], ACT.Copy).then_inc(self.ab_his, 1)

    def split_c_hi(self, act, t, j):
        wait_after(act, self.ld_c[j], 16 * t)
        wait_after(act, self.y_made, 4 * t - 1 + j)
        self.nc.scalar.activation(self.c_hi[:, j], self.raw_c[:, j], ACT.Copy).then_inc(self.c_his, 1)

    def act_start(self, act):
        for j in range(2):
            self.split_ab_hi(act, 0, j)

    def activate(self, act, t, s, last):
        j, n = s % 2, 4 * t + s
        if s >= 2 and not last:
            self.split_ab_hi(act, t + 1, s - 2)
        act.wait_ge(self.u_made, n + 1)
        wait_after(act, self.rc_made, n - 1)
        self.nc.scalar.activation(self.r[:, j], self.ps_u[:, j], self.func).then_inc(self.r_made, 1)
        if s < 2:
            self.split_c_hi(act, t, s)

    def split_g_hi(self, act, t, s):
        j, n = s % 2, 4 * t + s
        act.wait_ge(self.g_made, n + 1)
        wait_after(act, self.y_made, n - 1)
        self.nc.scalar.activation(self.g_hi[:, j], self.g[:, j], ACT.Copy).then_inc(self.g_his, 1)

    def split_c_lo(self, pool, t, j):
        pool.wait_ge(self.c_his, 2 * t + j + 1)
        self.nc.gpsimd.tensor_tensor(self.c_lo[:, j], self.raw_c[:, j], self.c_hi[:, j].bitcast(F32),
                                     ALU.subtract).then_inc(self.c_los, 1)

    def pool_step(self, pool, t, s, router):
        (hf, j), n = divmod(s, 2), 4 * t + s
        pool.wait_ge(self.r_made, n + 1)
        self.nc.gpsimd.tensor_tensor(self.rc[:, j], self.r[:, j], router, ALU.mult).then_inc(self.rc_made, 1)
        if s < 2:
            self.split_c_lo(pool, t, s)

    def split_ab_lo(self, dve, t, j):
        dve.wait_ge(self.ab_his, 2 * t + j + 1)
        self.nc.vector.tensor_tensor(self.ab_lo[:, j], self.raw_ab[:, j], self.ab_hi[:, j].bitcast(F32),
                                     ALU.subtract).then_inc(self.ab_los, 1)

    def add_y(self, dve, t, hf):
        dve.wait_ge(self.y_made, 4 * t + 2 * hf + 2)
        op = self.nc.vector.tensor_tensor(self.acc[:, :, half(hf)], self.ps_y[:], self.acc[:, :, half(hf)], ALU.add)
        op.then_inc(self.y_added, 1)

    def dve_prepare(self, dve, t, s, first, last):
        if s == 0 and first:
            self.split_ab_lo(dve, t, 0)
            self.split_ab_lo(dve, t, 1)
        if s >= 2 and not last:
            self.split_ab_lo(dve, t + 1, s - 2)
        if s == 3:
            self.add_y(dve, t, 0)
        if s == 1 and not first:
            self.add_y(dve, t - 1, 1)

    def gate(self, dve, t, s):
        j, n = s % 2, 4 * t + s
        dve.wait_ge(self.rc_made, n + 1)
        self.nc.vector.tensor_tensor(self.g[:, j], self.rc[:, j], self.ps_v[:, j], ALU.mult).then_inc(self.g_made, 1)

    def split_g(self, dve, t, s):
        j, n = s % 2, 4 * t + s
        dve.wait_ge(self.g_his, n + 1)
        self.nc.vector.tensor_tensor(self.g_lo[:, j], self.g[:, j], self.g_hi[:, j].bitcast(F32), ALU.subtract).then_inc(self.g_los, 1)

    def dve_end(self, dve, t):
        self.add_y(dve, t, 1)


def experts0_and_scan0_phase(nc, new, io, raw, t_hi, t_lo, cw_dram, x_t, scan_operands):
    NT = FT0 // 2
    NX = X0 // B
    with ExitStack() as ctx:
        sb, sem = new(ctx)
        x = Experts(nc, ctx, new, "x0", io["x0_w"], raw, ACT.Relu, t_hi, t_lo, x_t)
        scan = Scan0(nc, ctx, new, *scan_operands)
        router = sb("router", [P, NX, T])
        ld_router = [sem("ld_router0"), sem("ld_router1")]
        block = ctx.enter_context(nc.Block())

        def steps():
            for c in range(NX):
                for t in range(NT):
                    for s in range(4):
                        yield c, t, s

        @block.sync
        def _(sp):
            for t in range(1, NX * NT):
                for j in range(2):
                    x.load(sp, t, j)
            with sp.Fori(1, B) as b:
                for t in range(NX * NT):
                    for j in range(2):
                        x.load(sp, NX * NT * b + t, j)

        @block.tensor
        def _(pe):
            for b, first, last in turns(pe, B):
                for c, t, s in steps():
                    turn = NT * (NX * b + c) + t
                    x.up(pe, turn, s)
                    scan.pe_step(pe, b, c, t, s)
                    x.down_behind(pe, turn, s, first and c == 0 and t == 0)
            x.pe_end(pe, NT * X0 - 1)

        @block.scalar
        def _(act):
            def load_router(e, slot):
                act.dma_start(router[:, slot], cw_dram[bass.ds(e, 1)].partition_broadcast(P)).then_inc(ld_router[slot], 16)

            load_router(0, 0)
            scan.act_start(act)
            x.act_start(act)
            load_router(1, 1)
            for b, first, last in turns(act, B):
                for c, t, s in steps():
                    e = NX * b + c
                    x.activate(act, NT * e + t, s, last and c == NX - 1 and t == NT - 1)
                    x.split_g_hi(act, NT * e + t, s)
                    scan.act_step(act, b, c, t, s, last)
                    if t == NT - 1 and s == 3 and not last:
                        act.wait_ge(x.rc_made, 4 * NT * (e + 1))
                        load_router(e + NX, c)

        @block.gpsimd
        def _(pool):
            for b, first, last in turns(pool, B):
                for c, t, s in steps():
                    if t == 0 and s == 0:
                        pool.wait_ge(ld_router[c], 16 * (b + 1))
                    x.pool_step(pool, NT * (NX * b + c) + t, s, router[:, c, half(s // 2)])
                    scan.pool_step(pool, b, c, t, s)

        @block.vector
        def _(dve):
            scan.dve_start(dve)
            for b, first, last in turns(dve, B):
                for c, t, s in steps():
                    turn = NT * (NX * b + c) + t
                    x.dve_prepare(dve, turn, s, first and c == 0 and t == 0, last and c == NX - 1 and t == NT - 1)
                    x.gate(dve, turn, s)
                    x.split_g(dve, turn, s)
                    scan.dve_step(dve, b, c, t, s)
            x.dve_end(dve, NT * X0 - 1)


def router_segments(q):
    out, p = [], 0
    while p < P:
        e = (q * P + p) // F1
        stop = min(P, (e + 1) * F1 - q * P)
        out.append((e, p, stop))
        p = stop
    return out if len(out) > 1 else [(out[0][0], 0, P // 2), (out[0][0], P // 2, P)]


def turns_beside_chunks(eng, n, chunks):
    yield 0, True, False, True, True
    with eng.Fori(1, chunks - 1) as t:
        yield t, False, False, True, True
    yield chunks - 1, False, False, True, False
    with eng.Fori(chunks, n - 1) as t:
        yield t, False, False, False, False
    yield n - 1, False, True, False, False


def experts1_and_scan1_phase(nc, new, io, raw, t_hi, t_lo, cw_dram, x_t, router, scan_operands):
    NT = FT1 // 2
    with ExitStack() as ctx:
        sb, sem = new(ctx)
        x = Experts(nc, ctx, new, "x1", io["x1_w"], raw, ACT.Silu, t_hi, t_lo, x_t)
        scan = Scan1(nc, ctx, new, *scan_operands)
        ld_router = [sem("ld_router0"), sem("ld_router1")]
        nc.scalar.preload_act_table(ACT.Silu)
        block = ctx.enter_context(nc.Block())

        @block.sync
        def _(sp):
            for t in range(NT):
                for j in range(2):
                    if t > 0:
                        x.load(sp, t, j)
                        sp.wait_ge(x.rc_made, 4 * (t - 1) + 3 + j)
                    for e, a, z in router_segments(2 * t + j):
                        sp.dma_start(router[a:z, j], cw_dram[e:e + 1].partition_broadcast(z - a)).then_inc(ld_router[j], 16)
                if t == 0:
                    scan.load_first_tot(sp)

        @block.tensor
        def _(pe):
            for t, first, last, chunk, more in turns_beside_chunks(pe, NT, NC1):
                for s in range(4):
                    x.up(pe, t, s)
                    if chunk:
                        scan.pe_place(pe, t, s, 0)
                    x.down_behind(pe, t, s, first)
                    if chunk:
                        scan.pe_place(pe, t, s, 1)
            x.pe_end(pe, NT - 1)

        @block.scalar
        def _(act):
            scan.act_start(act)
            x.act_start(act)
            for t, first, last, chunk, more in turns_beside_chunks(act, NT, NC1):
                for s in range(4):
                    x.activate(act, t, s, last)
                    if chunk:
                        scan.take_y(act, t, s)
                    x.split_g_hi(act, t, s)
                    if first and s == 0:
                        act.wait_ge(scan.cleared, 1)
                        scan.spread_x(act, 0)
                    if chunk:
                        scan.act_step(act, t, s, more)

        @block.gpsimd
        def _(pool):
            scan.pool_start(pool)
            for t, first, last, chunk, more in turns_beside_chunks(pool, NT, NC1):
                for s in range(4):
                    if s < 2:
                        pool.wait_ge(ld_router[s], 32 * (t + 1))
                    x.pool_step(pool, t, s, router[:, s % 2, half(s // 2)])
                    if chunk:
                        scan.pool_step(pool, t, s, more)

        @block.vector
        def _(dve):
            scan.dve_start(dve)
            for t, first, last, chunk, more in turns_beside_chunks(dve, NT, NC1):
                for s in range(4):
                    x.dve_prepare(dve, t, s, first, last)
                    if first and s == 0:
                        scan.scan_decays(dve, 0)
                    if chunk and s == 0:
                        scan.weigh_decays(dve, t)
                    x.gate(dve, t, s)
                    if chunk:
                        scan.keep_early(dve, t, s)
                    x.split_g(dve, t, s)
                    if chunk:
                        scan.dve_step(dve, t, s, more)
            x.dve_end(dve, NT - 1)
class Scan1:

    HL = NH1 * Q1
    HG = NH1 // 4

    def __init__(self, nc, ctx, new, conv_x, bt, ct, x_tok, b_tok, dt_tok, cp_tok, da_dram, tot_dram, delta_col, d_col, y_t, ident):
        sb, sem = new(ctx)
        self.nc, self.conv_x, self.bt, self.ct, self.x_tok, self.b_tok, self.dt_tok, self.cp_tok = nc, conv_x, bt, ct, x_tok, b_tok, dt_tok, cp_tok
        self.da_dram, self.tot_dram, self.delta_col, self.d_col, self.y_t, self.ident = da_dram, tot_dram, delta_col, d_col, y_t, ident
        self.delta, self.da, self.tot = sb("delta", [P, self.HL]), sb("da", [P, self.HL]), sb("tot", [P, B * NH1])
        self.bts, self.cts, self.bs = sb("bts", [N1, P]), sb("cts", [N1, P]), sb("bs", [P, N1])
        self.m = sb("m", [P, NH1, Q1])
        self.xd, self.xdec = sb("xd", [P, NH1, P1]), sb("xdec", [P, NH1, P1])
        self.xbd = sb("xbd", [P, NH1, B, P1])
        self.state = sb("state", [N1, B, E1])
        self.last = sb("last", [P, NH1])
        self.through, self.y_in = sb("through", [P, E1]), sb("y_in", [P, B, P])
        self.ps = ctx.enter_context(nc.psum_tensor("s1_ps", [P, 2, HALF], F32))
        (self.tot_sent, self.delta_made, self.ld_tot, self.ld_da, self.bc_staged, self.b_staged, self.g_made, self.scanned,
         self.m_made, self.xd_made, self.xbd_made, self.xdec_made, self.y_made, self.s_made, self.decayed, self.s_kept, self.o_made,
         self.o_scaled, self.y_kept, self.last_kept, self.turned, self.y_out, self.cleared, self.state_clear) = (sem(s) for s in (
            "tot_sent", "delta_made", "ld_tot", "ld_da", "bc_staged", "b_staged", "g_made", "scanned", "m_made", "xd_made",
            "xbd_made", "xdec_made", "y_made", "s_made", "decayed", "s_kept", "o_made", "o_scaled", "y_kept", "last_kept", "turned",
            "y_out", "cleared", "state_clear"))

    @staticmethod
    def rows(b):
        return slice(b * Q1, (b + 1) * Q1)

    def load_decays(self, act, c):
        for b in range(B):
            act.dma_start(self.da[self.rows(b), :],
                          self.da_dram[bass.ds(c * B + b, 1)].rearrange("c h l -> c (h l)").partition_broadcast(Q1)).then_inc(self.ld_da, 16)

    def load_tot(self, act, c):
        act.dma_start(self.tot[:], self.tot_dram[bass.ds(c * B, B)].rearrange("(o b) h -> o (b h)", o=1).partition_broadcast(P)).then_inc(self.ld_tot, 16)

    def spread_x(self, act, c):
        act.wait_ge(self.xd_made, c + 1)
        wait_after(act, self.y_made, c)
        for b in range(B):
            op = self.nc.scalar.activation(self.xbd[self.rows(b), :, b], self.xd[self.rows(b)], ACT.Copy)
        op.then_inc(self.xbd_made, 1)

    def act_start(self, act):
        self.load_decays(act, 0)

    def load_first_tot(self, sp):
        sp.dma_start(self.tot_dram.rearrange("(c b) h -> b c h", b=B), self.cp_tok[Q1 - 1:P:Q1]).then_inc(self.tot_sent, 16)
        sp.wait_ge(self.tot_sent, 16)
        self.load_tot(sp, 0)

    def act_step(self, act, c, s, more):
        if s == 0 and more:
            act.wait_ge(self.scanned, c + 1)
            self.load_decays(act, c + 1)
        if s == 2 and more:
            act.wait_ge(self.decayed, 2 * c + 2)
            self.load_tot(act, c + 1)
        if s == 3 and more:
            self.spread_x(act, c + 1)

    def take_y(self, act, c, s):
        if s == 1:
            act.wait_ge(self.y_made, c + 1)
            self.nc.scalar.activation(self.y_in[:].rearrange("l b (g q) -> l g b q", q=P1),
                                      self.ps[:, 0].rearrange("l (g b q) -> l g b q", b=B, q=P1), ACT.Copy).then_inc(self.y_kept, 1)

    def stage_bc(self, pool, c):
        wait_after(pool, self.o_made, c)
        self.nc.gpsimd.tensor_copy(self.bts[:], self.bt[:, bass.ds(c * P, P)])
        self.nc.gpsimd.tensor_copy(self.cts[:], self.ct[:, bass.ds(c * P, P)]).then_inc(self.bc_staged, 1)

    def pool_start(self, pool):
        self.nc.gpsimd.memset(self.xbd[:], 0.0).then_inc(self.cleared, 1)
        self.stage_bc(pool, 0)
        self.nc.gpsimd.memset(self.state[:], 0.0).then_inc(self.state_clear, 1)
        pool.wait_ge(self.state_clear, 1)

    def pool_step(self, pool, c, s, more):
        if s == 0:
            wait_after(pool, self.s_made, B * c)
            pool.wait_ge(self.xd_made, c + 1)
            pool.wait_ge(self.last_kept, c + 1)
            self.nc.gpsimd.tensor_tensor(self.xdec[:], self.xd[:], self.last[:].unsqueeze(2).to_broadcast([P, NH1, P1]), ALU.mult).then_inc(self.xdec_made, 1)
            self.nc.gpsimd.tensor_copy(self.bs[:], self.b_tok[:, bass.ds(c, 1), :].rearrange("p a n -> p (a n)")).then_inc(self.b_staged, 1)
        if s < 2:
            pool.wait_ge(self.o_made, c + 1)
            pool.wait_ge(self.ld_tot, 16 * (c + 1))
            st = self.state[:, 2 * s:2 * s + 2].rearrange("n b (h q) -> n (b h) q", q=P1)
            tot = self.tot[:, 2 * s * NH1:(2 * s + 2) * NH1].unsqueeze(2).to_broadcast([P, 2 * NH1, P1])
            self.nc.gpsimd.tensor_tensor(st, st, tot, ALU.mult).then_inc(self.decayed, 1)
        if s == 1 and more:
            self.stage_bc(pool, c + 1)

    def add_to_state(self, pe, c, b):
        if b == 0:
            pe.wait_ge(self.b_staged, c + 1)
            pe.wait_ge(self.xdec_made, c + 1)
        self.nc.tensor.matmul(self.ps[:, 0 if b in (1, 2) else 1], self.bs[self.rows(b), :], self.xdec[self.rows(b)].rearrange("p h q -> p (h q)"),
                              start=True, stop=True, tile_position=(b * Q1, 0)).then_inc(self.s_made, 1)

    def pe_place(self, pe, c, s, place):
        nc, ps = self.nc, self.ps[:, place]
        if (s, place) == (0, 0):
            pe.wait_ge(self.bc_staged, c + 1)
            wait_after(pe, self.s_kept, B * c - 1)
            for b in range(B):
                mm = nc.tensor.matmul(ps[self.rows(b), 0:Q1], self.bts[:, self.rows(b)], self.cts[:, self.rows(b)], start=True, stop=True,
                                      tile_position=(0, b * Q1))
            mm.then_inc(self.g_made, 1)
        if (s, place) == (0, 1):
            wait_after(pe, self.s_kept, B * c)
            pe.wait_ge(self.state_clear, 1)
            for b in range(B):
                mm = nc.tensor.matmul(ps[self.rows(b), :], self.cts[:, self.rows(b)], self.state[:, b], start=True, stop=True,
                                      tile_position=(0, b * Q1))
            mm.then_inc(self.o_made, 1)
        if (s, place) == (1, 0):
            pe.wait_ge(self.m_made, c + 1)
            pe.wait_ge(self.xbd_made, c + 1)
            for h in range(NH1):
                hq, hg = h // self.HG, h % self.HG
                mm = nc.tensor.matmul(ps[hq * Q1:(hq + 1) * Q1, hg * Q1:(hg + 1) * Q1], self.m[:, h],
                                      self.xbd[:, h].rearrange("p b q -> p (b q)"), start=True, stop=True, tile_position=(0, hq * Q1))
            mm.then_inc(self.y_made, 1)
        if (s, place) == (1, 1):
            pe.wait_ge(self.o_scaled, c + 1)
            self.add_to_state(pe, c, 0)
        if (s, place) == (2, 0):
            pe.wait_ge(self.y_kept, c + 1)
            self.add_to_state(pe, c, 1)
        if (s, place) == (2, 1):
            pe.wait_ge(self.s_kept, B * c + 1)
            pe.wait_ge(self.y_kept, c + 1)
            for t in range(NE1):
                nc.tensor.matmul(ps[:, t * P:(t + 1) * P], self.through[:, t * P:(t + 1) * P], self.ident, start=t == 0, stop=False)
            for b in range(B):
                mm = nc.tensor.matmul(ps.rearrange("p (h b l) -> p h b l", b=B, l=Q1)[:, :, b], self.y_in[:, b], self.ident,
                                      start=False, stop=b == B - 1)
            mm.then_inc(self.turned, 1)
        if (s, place) == (3, 0):
            pe.wait_ge(self.s_kept, B * c + 2)
            self.add_to_state(pe, c, 2)
        if (s, place) == (3, 1):
            pe.wait_ge(self.y_out, c + 1)
            self.add_to_state(pe, c, 3)

    def scan_decays(self, dve, c):
        dve.wait_ge(self.ld_da, 64 * (c + 1))
        wait_after(dve, self.y_made, c)
        self.nc.vector.tensor_tensor_scan(self.m[:].rearrange("p h l -> p (h l)"), self.da[:], self.delta[:], 0.0,
                                          ALU.mult, ALU.add).then_inc(self.scanned, 1)
        dve.wait_ge(self.scanned, c + 1)
        wait_after(dve, self.xdec_made, c)
        self.nc.vector.tensor_copy(self.last[:], self.m[:, :, Q1 - 1]).then_inc(self.last_kept, 1)

    def scale_x(self, dve, c):
        wait_after(dve, self.xbd_made, c)
        wait_after(dve, self.xdec_made, c)
        self.nc.vector.tensor_tensor(self.xd[:], self.x_tok[:, bass.ds(c, 1), :].rearrange("p a (h q) -> p (a h) q", q=P1),
                                     self.dt_tok[:, bass.ds(c, 1), :].rearrange("p a h -> p (a h)").unsqueeze(2).to_broadcast([P, NH1, P1]),
                                     ALU.mult).then_inc(self.xd_made, 1)

    def dve_start(self, dve):
        self.nc.vector.tensor_copy(self.delta[:].rearrange("p (h l) -> p h l", l=Q1),
                                   self.delta_col.unsqueeze(1).to_broadcast([P, NH1, Q1])).then_inc(self.delta_made, 1)
        dve.wait_ge(self.delta_made, 1)
        self.scale_x(dve, 0)

    def keep_state(self, dve, c, b):
        dve.wait_ge(self.s_made, B * c + b + 1)
        dve.wait_ge(self.decayed, 2 * c + b // 2 + 1)
        self.nc.vector.tensor_tensor(self.state[:, b], self.ps[:, 0 if b in (1, 2) else 1], self.state[:, b], ALU.add).then_inc(self.s_kept, 1)

    def weigh_decays(self, dve, c):
        dve.wait_ge(self.last_kept, c + 1)
        dve.wait_ge(self.g_made, c + 1)
        self.nc.vector.tensor_tensor(self.m[:], self.m[:], self.ps[:, 0, 0:Q1].unsqueeze(1).to_broadcast([P, NH1, Q1]), ALU.mult).then_inc(self.m_made, 1)

    def keep_early(self, dve, c, s):
        if s >= 2:
            self.keep_state(dve, c, s - 1)

    def dve_step(self, dve, c, s, more):
        nc = self.nc
        if s == 0:
            dve.wait_ge(self.o_made, c + 1)
            nc.vector.tensor_tensor(self.through[:].rearrange("p (h q) -> p h q", q=P1), self.ps[:, 1].rearrange("p (h q) -> p h q", q=P1),
                                    self.cp_tok[:, bass.ds(c, 1), :].rearrange("p a h -> p (a h)").unsqueeze(2).to_broadcast([P, NH1, P1]),
                                    ALU.mult).then_inc(self.o_scaled, 1)
        if s == 1:
            self.keep_state(dve, c, 0)
        if s == 2:
            if more:
                self.scan_decays(dve, c + 1)
            dve.wait_ge(self.turned, c + 1)
            tok = bass.ds(c * P, P)
            for t in range(NE1):
                nat = self.y_t[:, t, :].rearrange("p (b c l) -> p b c l", b=B, l=Q1)[:, :, bass.ds(c, 1), :].rearrange("p b a l -> p b (a l)")
                op = nc.vector.scalar_tensor_tensor(out=nat, in0=self.conv_x[t][:, tok].rearrange("p (b l) -> p b l", b=B),
                                                    scalar=self.d_col[:, t:t + 1],
                                                    in1=self.ps[:, 1, t * P:(t + 1) * P].rearrange("p (b l) -> p b l", b=B),
                                                    op0=ALU.mult, op1=ALU.add)
            op.then_inc(self.y_out, 1)
        if s == 3:
            if more:
                self.scale_x(dve, c + 1)
            self.keep_state(dve, c, 3)
def program(nc, io, out):
    count = [0]

    def new(ctx):
        count[0] += 1
        n = count[0]

        def sb(name, shape, dt=F32):
            return ctx.enter_context(nc.sbuf_tensor(f"t{n}_{name}", shape, dt))

        mine = []

        def sem(name):
            mine.append(nc.alloc_semaphore(f"s{n}_{name}"))
            return mine[-1]

        def clear():
            if mine:
                nc.clear_and_free_semaphores(mine)
                nc.all_engine_barrier()

        ctx.callback(clear)

        return sb, sem

    def weights(sb, name, memory=None):
        n = io[name].shape[1]
        raw = sb(name, [P, KH, n])[:] if memory is None else memory[:, 0:KH * n].rearrange("p (k n) -> p k n", k=KH)
        return io[name], raw, sb(name + "_hi", [P, KH, n], F32R), sb(name + "_lo", [P, KH, n], F32R)

    with ExitStack() as whole:
        sb, sem = new(whole)
        da0_dram = nc.dram_tensor("da0_scratch", [B * S // Q0, NH0, Q0], F32).ap()
        da1_dram = nc.dram_tensor("da1_scratch", [NC1 * B, NH1, Q1], F32).ap()
        tot1_dram = nc.dram_tensor("tot1_scratch", [NC1 * B, NH1], F32).ap()
        cw0_dram = nc.dram_tensor("cw0_scratch", [X0, T], F32).ap()
        cw1_dram = nc.dram_tensor("cw1_scratch", [X1, T], F32).ap()
        x_t = sb("x", [P, KH, T])
        xn = sb("xn", [P, KH, T])
        xn_hi, xn_lo = sb("xn_hi", [P, KH, T], F32R), sb("xn_lo", [P, KH, T], F32R)
        ones, small = sb("ones", [P, P]), sb("small", [P, sum(width for _, width in SMALL)])
        ident_bf, mask_bf = sb("ident_bf", [P, P], BF16), sb("mask_bf", [P, P], BF16)
        at, start = {}, 0
        for key, width in SMALL:
            at[key] = small[:, start:start + width]
            start += width
        ident, mask_f, eps, delta1 = (at[key] for key in ("ident", "mask", "eps", "delta1"))
        ln1_w, ln2_w, norm0_w, norm1_w = (at[key] for key in ("ln1_w", "ln2_w", "norm0_w", "norm1_w"))
        gw0, gw1 = at["gw0"].rearrange("p (k e) -> p k e", k=KH), at["gw1"].rearrange("p (k e) -> p k e", k=KH)
        lower0, lower1 = at["lower0"].rearrange("p (e f) -> p e f", e=X0), at["lower1"].rearrange("p (e f) -> p e f", e=X1)
        conv0_b, dt0, d0 = (at[key] for key in ("conv0_b", "dt0", "d0"))
        conv1_b, dt1, d1 = (at[key] for key in ("conv1_b", "dt1", "d1"))
        ld, ready = sem("ld"), sem("ready")

        with nc.Block() as block:
            @block.sync
            def _(sp):
                sp.dma_start(x_t[:], io["x"]).then_inc(ld, 16)

            @block.scalar
            def _(act):
                act.dma_start(small[:], io["small"]).then_inc(ready, 16)

            @block.vector
            def _(dve):
                nc.vector.memset(ones[:], 1.0)
                dve.wait_ge(ready, 16)
                nc.vector.tensor_copy(ident_bf[:], ident)
                nc.vector.tensor_copy(mask_bf[:], mask_f)

            @block.gpsimd
            def _(pool):
                pool.wait_ge(ld, 16)

        ones_, ident_ = ones[:], ident
        with ExitStack() as layer:
            sbl, _ = new(layer)
            h_t = sbl("h_t", [P, KH, T])
            with ExitStack() as att:
                sba, _ = new(att)
                hn_hi, hn_lo = sba("hn_hi", [P, KH, T], F32R), sba("hn_lo", [P, KH, T], F32R)
                kz, v_tok = sba("kz", [P, 2, KT, T]), sba("v_tok", [P, TT, NKV * D])
                wq_raw, wo_raw = sba("wq_raw", [P, 2, KH, P]), sba("wo_raw", [P, 2, H])
                with ExitStack() as kv:
                    sbk, _ = new(kv)
                    wk, wv = weights(sbk, "wk"), weights(sbk, "wv")
                    norm_phase(nc, new, "n0", x_t, xn, ones_, ident_, eps[:, 0:1], True, hi=xn_hi, lo=xn_lo, second=(ln1_w, hn_hi, hn_lo),
                               ahead=(wk, wv))
                    keys_values_phase(nc, new, io, wk, wv, hn_hi, hn_lo, kz, v_tok, wq_raw, wo_raw)
                attention_phase(nc, new, io, wq_raw, wo_raw, hn_hi, hn_lo, kz, v_tok, xn, h_t, ident_, ident_bf[:], mask_bf[:])
            with ExitStack() as mix:
                sbm, _ = new(mix)
                gate_s, cx = sbm("gate_s", [P, NE0, T]), sbm("conv_x", [P, NE0, T])
                t_hi, t_lo = sbm("t_hi", [P, KH, T], F32R), sbm("t_lo", [P, KH, T], F32R)
                conv_x = [cx[:, i] for i in range(NE0)]
                bt, ct = sbm("bt", [N0, T])[:], sbm("ct", [N0, T])[:]
                DT = slice(N0, N0 + NH0)
                x_tok, b_tok = sbm("x_tok", [P, TT, E0]), sbm("b_tok", [P, TT, N0])
                dt_tok, cp_tok = sbm("dt_tok", [P, TT, NH0]), sbm("cp_tok", [P, TT, NH0])
                raw = sbm("raw_ab", [P, 2, 2, H]), sbm("raw_c", [P, 2, H])
                raw_out = raw[0][:].rearrange("p i j n -> p (i j) n")
                with ExitStack() as steps:
                    sbs, _ = new(steps)
                    dt, cp = sbs("dt", [P, T])[DT, :], sbs("cp", [P, T])[DT, :]
                    unused = x_tok[:].rearrange("p t n -> p (t n)")
                    w_in = weights(sbs, "in0_w", unused)
                    norm_phase(nc, new, "n2", h_t, xn, ones_, ident_, eps[:, 0:1], False, weight=ln2_w, hi=t_hi, lo=t_lo, ahead=(w_in,))
                    conv = lambda i: ("conv", (4 + i) * P, P, i)
                    gate = lambda i: ("gate", i * P, P, i)
                    tiles = [("conv", 8 * P + N0, N0 + NH0, 5), ("conv", 8 * P, N0, 4), conv(0), gate(0), conv(1), gate(1), conv(2), gate(2),
                             conv(3), gate(3)]
                    mixer_project(nc, new, "m0", w_in[2], w_in[3], io["conv0_w"], xn_hi, xn_lo, conv_x + [bt, ct], gate_s, dt, cp,
                                  (5, DT, None), tiles, (1.0, 1.0), dt0, conv0_b, da0_dram, Q0, lambda ap: ap.rearrange("p (b s) -> p b s", b=B),
                                  ("r0", xn, gw0, lower0, cw0_dram, ident_, X0, TOP0, True,
                                   unused[:, 0:2 * TT * X0 * X0].rearrange("p (a n) -> p a n", a=2)))
                    turn_phase(nc, new, "t0", conv_x, bt, dt, cp, DT, x_tok, b_tok, dt_tok, cp_tok, ident_, io["x0_w"], raw, addends=(x_t, h_t))
                y_t = sbm("y_t", [P, NE0, T])
                experts0_and_scan0_phase(nc, new, io, raw, t_hi, t_lo, cw0_dram, x_t,
                                         (conv_x, bt, ct, x_tok, b_tok, dt_tok, cp_tok, da0_dram, d0, y_t, ident_))
                mixer_out_phase(nc, new, "o0", y_t, gate_s, norm0_w, io["out0_w"], raw_out, x_t, cx, ones_, ident_, eps[:, 1:2], True)
        with ExitStack() as layer:
            sbl, _ = new(layer)
            gate_s = sbl("gate_s", [P, NE1, T])
            with ExitStack() as mix:
                sbm, _ = new(mix)
                cx = sbm("conv_x", [P, NE1, T])
                conv_x = [cx[:, i] for i in range(NE1)]
                bt, ct = sbm("bt", [N1, T])[:], sbm("ct", [N1, T])[:]
                DT = slice(0, NH1)
                x_tok, b_tok = sbm("x_tok", [P, TT, E1]), sbm("b_tok", [P, TT, N1])
                dt_tok, cp_tok = sbm("dt_tok", [P, TT, NH1]), sbm("cp_tok", [P, TT, NH1])
                raw = sbm("raw_ab", [P, 2, 2, H]), sbm("raw_c", [P, 2, H])
                raw_out = raw[0][:].rearrange("p i j n -> p (i j) n")
                with ExitStack() as steps:
                    sbs, _ = new(steps)
                    dt, cp = sbs("dt", [P, T])[DT, :], sbs("cp", [P, T])[DT, :]
                    unused = x_tok[:].rearrange("p t n -> p (t n)")
                    w_in = weights(sbs, "in1_w", unused)
                    norm_phase(nc, new, "n3", x_t, xn, ones_, ident_, eps[:, 0:1], True, hi=xn_hi, lo=xn_lo, ahead=(w_in,))
                    tiles = [("dt", 10 * P, NH1, -1), conv(4), conv(5), conv(0), gate(0), conv(1), gate(1), conv(2), gate(2), conv(3), gate(3)]
                    by_chunk = lambda ap: ap.rearrange("p (c b l) -> p b c l", b=B, l=Q1)
                    mixer_project(nc, new, "m1", w_in[2], w_in[3], io["conv1_w"], xn_hi, xn_lo, conv_x + [bt, ct], gate_s, dt, cp,
                                  (-1, DT, lambda ap, hf: by_chunk(ap)[:, 2 * hf:2 * hf + 2]), tiles, (0.25, 0.5), dt1, conv1_b,
                                  da1_dram, Q1, by_chunk, ("r1", xn, gw1, lower1, cw1_dram, ident_, X1, TOP1, False,
                                   unused[:, 0:2 * TT * X1 * X1].rearrange("p (a n) -> p a n", a=2)))
                    turn_phase(nc, new, "t1", conv_x, bt, dt, cp, DT, x_tok, b_tok, dt_tok, cp_tok, ident_, io["x1_w"], raw)
                y_t = sbm("y_t", [P, NE1, T])
                experts1_and_scan1_phase(nc, new, io, raw, xn_hi, xn_lo, cw1_dram, x_t, xn,
                                         (conv_x, bt, ct, x_tok, b_tok, dt_tok, cp_tok, da1_dram, tot1_dram, delta1, d1, y_t, ident_))
                mixer_out_phase(nc, new, "o1", y_t, gate_s, norm1_w, io["out1_w"], raw_out, x_t, cx, ones_, ident_, eps[:, 0:1], False, out)


def layout(inputs):
    f32 = np.float32
    g = {k: np.asarray(v) for k, v in inputs.items()}

    def col(v, n):
        return np.ascontiguousarray(v.reshape(n, P).T)

    def kpn(w):
        return np.ascontiguousarray(w.reshape(KH, P, -1).transpose(1, 0, 2))

    a = {}
    a["x"] = np.ascontiguousarray(g["L0_attn_x"].reshape(T, KH, P).transpose(2, 1, 0))
    a["in0_w"] = np.ascontiguousarray(g["L0_attn_in_proj_w"].T)
    a["in1_w"] = np.ascontiguousarray(g["L1_attn_in_proj_w"])
    a["out0_w"] = np.ascontiguousarray(g["L0_attn_out_proj_w"].T)
    a["out1_w"] = np.ascontiguousarray(g["L1_attn_out_proj_w"])
    a["wk"], a["wv"] = np.ascontiguousarray(g["L0_ffn_wk"]), np.ascontiguousarray(g["L0_ffn_wv"])
    for n, (w, b, N) in enumerate(((g["L0_attn_conv_w"], g["L0_attn_conv_b"], N0), (g["L1_attn_conv_w"], g["L1_attn_conv_b"], N1))):
        cw, cb = np.zeros((P, 6, KCONV), f32), np.zeros((P, 6), f32)
        for i in range(4):
            cw[:, i], cb[:, i] = w[i * P:(i + 1) * P], b[i * P:(i + 1) * P]
        for i in range(2):
            cw[0:N, 4 + i], cb[0:N, 4 + i] = w[512 + i * N:512 + (i + 1) * N], b[512 + i * N:512 + (i + 1) * N]
        a[f"conv{n}_w"], a[f"conv{n}_b"] = cw, cb
    dt0, dt1 = np.zeros((P, 2), f32), np.zeros((P, 2), f32)
    dt0[N0:N0 + NH0, 0], dt0[N0:N0 + NH0, 1] = g["L0_attn_dt_bias"], g["L0_attn_A_log"]
    dt1[0:NH1, 0], dt1[0:NH1, 1] = g["L1_attn_dt_bias"], g["L1_attn_A_log"]
    a["dt0"], a["dt1"] = dt0, dt1
    a["d0"] = col(np.repeat(g["L0_attn_D"], P0), NE0)
    a["d1"] = col(np.repeat(g["L1_attn_D"], P1), NE1)
    a["norm0_w"], a["norm1_w"] = col(g["L0_attn_norm_w"], NE0), col(g["L1_attn_norm_w"], NE1)
    a["ln1_w"], a["ln2_w"] = col(g["L0_ffn_ln1_w"], KH), col(g["L0_ffn_ln2_w"], KH)
    a["gw0"], a["gw1"] = kpn(g["L0_ffn_gate_w"]), kpn(np.ascontiguousarray(g["L1_ffn_gate_w"].T))
    order = [(2 * m + r) * (NHQ // NKV) + i for m in range(KT) for i in range(4) for r in range(2)]
    wq = g["L0_ffn_wq"].reshape(KH, P, NHQ, D)[:, :, order].reshape(KH, P, QT, P)
    a["wq_tiles"] = np.ascontiguousarray(wq.transpose(2, 1, 0, 3))
    a["wo_tiles"] = np.ascontiguousarray(g["L0_ffn_wo"].reshape(NHQ, D, H)[order].reshape(QT, P, H))
    w1 = g["L0_ffn_w1"].reshape(X0, KH, P, FT0, P).transpose(0, 3, 2, 1, 4).reshape(X0 * FT0, P, H)
    w3 = g["L0_ffn_w3"].reshape(X0, KH, P, FT0, P).transpose(0, 3, 2, 1, 4).reshape(X0 * FT0, P, H)
    w2 = g["L0_ffn_w2"].reshape(X0 * FT0, P, H)
    a["x0_w"] = np.ascontiguousarray(np.stack([w1, w3, w2], axis=2))
    wg = g["L1_ffn_w_gate"].reshape(FT1, P, KH, P).transpose(0, 3, 2, 1).reshape(FT1, P, H)
    wu = g["L1_ffn_w_up"].reshape(FT1, P, KH, P).transpose(0, 3, 2, 1).reshape(FT1, P, H)
    wd = g["L1_ffn_w_down"].transpose(0, 2, 1).reshape(FT1, P, H)
    a["x1_w"] = np.ascontiguousarray(np.stack([wg, wu, wd], axis=2))
    a["ident"] = np.eye(P, dtype=f32)
    a["mask"] = np.where(np.arange(P)[None, :] > np.arange(P)[:, None], f32(NEG_MASK), f32(0)).astype(f32)
    a["eps"] = np.tile(np.array([[1e-5, 1e-6]], f32), (P, 1))
    a["lower0"] = np.tile(np.tril(np.ones((X0, X0), f32), -1)[None], (P, 1, 1))
    a["lower1"] = np.tile(np.tril(np.ones((X1, X1), f32), -1)[None], (P, 1, 1))
    a["delta1"] = np.tile(np.eye(Q1, dtype=f32), (B, 1))
    a["small"] = np.concatenate([a.pop(key).reshape(P, width) for key, width in SMALL], axis=1)
    return a


def build(nc, arrays):
    io = {k: nc.dram_tensor(f"in_{k}", v.shape, mybir.dt.from_np(v.dtype), kind="ExternalInput").ap() for k, v in arrays.items()}
    out = nc.dram_tensor("out_x", (P, KH, T), F32, kind="ExternalOutput").ap()
    program(nc, io, out)


def kernel(**inputs):
    import concourse.bacc as bacc
    from concourse.bass_utils import run_bass_kernel_spmd

    arrays = layout(inputs)
    nc = bacc.Bacc("TRN2", target_bir_lowering=False, num_devices=1)
    build(nc, arrays)
    r = run_bass_kernel_spmd(nc, [{f"in_{k}": v for k, v in arrays.items()}], core_ids=[0])
    y = r.results[0]["out_x"]
    return np.ascontiguousarray(y.transpose(2, 1, 0)).reshape(B, S, H)
```
